# Optimizing a Trainium2 kernel written in Bass

```python
import numpy as np
import jax
import jax.numpy as jnp

def _softmax(x, axis=-1):
    return jax.nn.softmax(x, axis=axis)

def _gelu(x):
    return jax.nn.gelu(x, approximate=True)

def _silu(x):
    return jax.nn.silu(x)

def _sigmoid(x):
    return jax.nn.sigmoid(x)

def _layernorm(x, axis=-1, eps=1e-05):
    m = jnp.mean(x, axis=axis, keepdims=True)
    v = jnp.var(x, axis=axis, keepdims=True)
    return (x - m) / jnp.sqrt(v + eps)

def _scatter_add(tgt, idx, src, axis=0):
    return tgt.at[idx].add(src)

def _segment_sum(src, seg, n):
    return jax.ops.segment_sum(src, seg, n)
kernel_name = 'mk_adaln_d2_jaxref_r8_0b6299'

def setup_inputs(seed: int=0):
    np.random.seed(seed)
    _w = jnp.asarray

    def _L0_attn_setup():
        import jax, jax.numpy as jnp
        import numpy as np
        HEAD_NUM = 16
        ROPE_BASE = 10000.0

        def _rotate_half(x):
            x_even = x[..., ::2]
            x_odd = x[..., 1::2]
            return jnp.stack((-x_odd, x_even), axis=-1).reshape(x.shape)

        def _rope_cos_sin(seq_len, head_dim):
            half = head_dim // 2
            inv_freq = 1.0 / ROPE_BASE ** (jnp.arange(half, dtype=jnp.float32) / half)
            t = jnp.arange(seq_len, dtype=jnp.float32)
            freqs = t[:, None] * inv_freq[None, :]
            cos = jnp.repeat(jnp.cos(freqs), 2, axis=-1)
            sin = jnp.repeat(jnp.sin(freqs), 2, axis=-1)
            return (cos, sin)
        key = jax.random.key(seed)
        ks = jax.random.split(key, 9)
        B, S, H = (2, 256, 256)
        std = 1.0 / np.sqrt(H)
        return {'x': jax.random.normal(ks[0], (B, S, H), jnp.float32), 'Wq': jax.random.normal(ks[1], (H, H), jnp.float32) * std, 'bq': jax.random.normal(ks[2], (H,), jnp.float32) * std, 'Wk': jax.random.normal(ks[3], (H, H), jnp.float32) * std, 'bk': jax.random.normal(ks[4], (H,), jnp.float32) * std, 'Wv': jax.random.normal(ks[5], (H, H), jnp.float32) * std, 'bv': jax.random.normal(ks[6], (H,), jnp.float32) * std, 'Wo': jax.random.normal(ks[7], (H, H), jnp.float32) * std, 'bo': jax.random.normal(ks[8], (H,), jnp.float32) * std}
    _L0_attn_in = _L0_attn_setup()

    def _L0_ffn_setup():
        import jax, jax.numpy as jnp
        import numpy as np
        NUM_EXPERTS = 8
        TOP_K = 2
        DIM = 256
        HIDDEN = 896
        B, S = (2, 128)
        key = jax.random.key(seed)
        ks = jax.random.split(key, 5)
        scale = 0.02
        x = jax.random.normal(ks[0], (B, S, DIM), dtype=jnp.float32)
        Wg = jax.random.normal(ks[1], (DIM, NUM_EXPERTS), dtype=jnp.float32) * scale
        w1 = jax.random.normal(ks[2], (NUM_EXPERTS, DIM, HIDDEN), dtype=jnp.float32) * scale
        w3 = jax.random.normal(ks[3], (NUM_EXPERTS, DIM, HIDDEN), dtype=jnp.float32) * scale
        w2 = jax.random.normal(ks[4], (NUM_EXPERTS, HIDDEN, DIM), dtype=jnp.float32) * scale
        return {'x': x, 'Wg': Wg, 'w1': w1, 'w3': w3, 'w2': w2}
    _L0_ffn_in = _L0_ffn_setup()
    _L0_c = _w((lambda *s: np.random.randn(*s).astype(np.float32) * 0.05)(2, 256))
    _L0_wmod = _w((lambda *s: np.random.randn(*s).astype(np.float32) * 0.05)(256, 6 * 256) * 256 ** (-0.5))

    def _L1_attn_setup():
        import jax, jax.numpy as jnp
        import numpy as np
        B, T, HID = (1, 256, 256)
        H = 16
        D = HID // H
        EPS = 1e-05

        def _layer_norm(x, eps=1e-05):
            mu = jnp.mean(x, axis=-1, keepdims=True)
            var = jnp.mean((x - mu) ** 2, axis=-1, keepdims=True)
            return (x - mu) * jax.lax.rsqrt(var + eps)

        def _feature_map(x, gamma, beta):
            return _layer_norm(x * gamma + beta)
        key = jax.random.key(seed)
        ks = jax.random.split(key, 8)
        s = HID ** (-0.5)
        return {'hidden_states': jax.random.normal(ks[0], (B, T, HID), jnp.float32), 'Wq': jax.random.normal(ks[1], (HID, HID), jnp.float32) * s, 'Wk': jax.random.normal(ks[2], (HID, HID), jnp.float32) * s, 'Wv': jax.random.normal(ks[3], (HID, HID), jnp.float32) * s, 'Wo': jax.random.normal(ks[4], (HID, HID), jnp.float32) * s, 'gamma': 1.0 + 0.1 * jax.random.normal(ks[5], (D,), jnp.float32), 'beta': 0.1 * jax.random.normal(ks[6], (D,), jnp.float32)}
    _L1_attn_in = _L1_attn_setup()

    def _L1_ffn_setup():
        import jax, jax.numpy as jnp
        import numpy as np
        TOP_K = 8

        def _moe_block(hf, gw, ew):
            T, D = hf.shape
            E = gw.shape[0]
            logits = hf @ gw.T
            w = jax.nn.softmax(logits, axis=-1)
            vals, idx = jax.lax.top_k(w, TOP_K)
            w_dense = jnp.zeros_like(w).at[jnp.arange(T)[:, None], idx].add(vals)
            out = jnp.zeros_like(hf)
            for e in range(E):
                out = out + w_dense[:, e:e + 1] * (hf @ ew[e].T)
            return out
        key = jax.random.key(seed)
        k_x, k_g, k_e = jax.random.split(key, 3)
        L, E, D = (4, 16, 256)
        x = jax.random.normal(k_x, (4, 256, D), dtype=jnp.float32)
        gate_w = jax.random.normal(k_g, (L, E, D), dtype=jnp.float32) * 0.02
        expert_w = jax.random.normal(k_e, (L, E, D, D), dtype=jnp.float32) * 0.02
        return {'x': x, 'gate_w': gate_w, 'expert_w': expert_w}
    _L1_ffn_in = _L1_ffn_setup()
    _L1_c = _w((lambda *s: np.random.randn(*s).astype(np.float32) * 0.05)(2, 256))
    _L1_wmod = _w((lambda *s: np.random.randn(*s).astype(np.float32) * 0.05)(256, 6 * 256) * 256 ** (-0.5))
    _d = {'L0_attn_x': _L0_attn_in['x'], 'L0_attn_Wq': _L0_attn_in['Wq'], 'L0_attn_bq': _L0_attn_in['bq'], 'L0_attn_Wk': _L0_attn_in['Wk'], 'L0_attn_bk': _L0_attn_in['bk'], 'L0_attn_Wv': _L0_attn_in['Wv'], 'L0_attn_bv': _L0_attn_in['bv'], 'L0_attn_Wo': _L0_attn_in['Wo'], 'L0_attn_bo': _L0_attn_in['bo'], 'L0_ffn_Wg': _L0_ffn_in['Wg'], 'L0_ffn_w1': _L0_ffn_in['w1'], 'L0_ffn_w3': _L0_ffn_in['w3'], 'L0_ffn_w2': _L0_ffn_in['w2'], 'L0_c': _L0_c, 'L0_wmod': _L0_wmod, 'L1_attn_Wq': _L1_attn_in['Wq'], 'L1_attn_Wk': _L1_attn_in['Wk'], 'L1_attn_Wv': _L1_attn_in['Wv'], 'L1_attn_Wo': _L1_attn_in['Wo'], 'L1_attn_gamma': _L1_attn_in['gamma'], 'L1_attn_beta': _L1_attn_in['beta'], 'L1_ffn_gate_w': _L1_ffn_in['gate_w'], 'L1_ffn_expert_w': _L1_ffn_in['expert_w'], 'L1_c': _L1_c, 'L1_wmod': _L1_wmod}
    _x0 = _d['L0_attn_x']
    _d['L0_attn_x'] = jax.random.normal(jax.random.fold_in(jax.random.key(seed), 1), (2, 1024, 256), dtype=_x0.dtype)
    del _x0
    return _d

def reference(L0_attn_x, L0_attn_Wq, L0_attn_bq, L0_attn_Wk, L0_attn_bk, L0_attn_Wv, L0_attn_bv, L0_attn_Wo, L0_attn_bo, L0_ffn_Wg, L0_ffn_w1, L0_ffn_w3, L0_ffn_w2, L0_c, L0_wmod, L1_attn_Wq, L1_attn_Wk, L1_attn_Wv, L1_attn_Wo, L1_attn_gamma, L1_attn_beta, L1_ffn_gate_w, L1_ffn_expert_w, L1_c, L1_wmod):

    def _L0_attn_ref(x, Wq, bq, Wk, bk, Wv, bv, Wo, bo):
        import jax, jax.numpy as jnp
        import numpy as np
        HEAD_NUM = 16
        ROPE_BASE = 10000.0

        def _rotate_half(x):
            x_even = x[..., ::2]
            x_odd = x[..., 1::2]
            return jnp.stack((-x_odd, x_even), axis=-1).reshape(x.shape)

        def _rope_cos_sin(seq_len, head_dim):
            half = head_dim // 2
            inv_freq = 1.0 / ROPE_BASE ** (jnp.arange(half, dtype=jnp.float32) / half)
            t = jnp.arange(seq_len, dtype=jnp.float32)
            freqs = t[:, None] * inv_freq[None, :]
            cos = jnp.repeat(jnp.cos(freqs), 2, axis=-1)
            sin = jnp.repeat(jnp.sin(freqs), 2, axis=-1)
            return (cos, sin)
        B, S, H = x.shape
        nh = HEAD_NUM
        d = H // nh
        scale = jnp.float32(np.sqrt(d))

        def proj(W, b):
            y = x @ W.T + b
            return y.reshape(B, S, nh, d).transpose(0, 2, 1, 3)
        Q = proj(Wq, bq)
        K = proj(Wk, bk)
        V = proj(Wv, bv)
        cos, sin = _rope_cos_sin(S, d)
        Q = Q * cos + _rotate_half(Q) * sin
        K = K * cos + _rotate_half(K) * sin
        scores = jnp.einsum('bhqd,bhkd->bhqk', Q, K) / scale
        causal = jnp.tril(jnp.ones((S, S), dtype=bool))
        scores = jnp.where(causal, scores, jnp.float32(-jnp.inf))
        attn = jax.nn.softmax(scores, axis=-1)
        out = jnp.einsum('bhqk,bhkd->bhqd', attn, V)
        out = out.transpose(0, 2, 1, 3).reshape(B, S, H)
        return out @ Wo.T + bo

    def _L0_ffn_ref(x, Wg, w1, w3, w2):
        import jax, jax.numpy as jnp
        import numpy as np
        NUM_EXPERTS = 8
        TOP_K = 2
        DIM = 256
        HIDDEN = 896
        B, S = (2, 128)
        Bs, Ss, D = x.shape
        E = Wg.shape[1]
        xf = x.reshape(-1, D)
        T = xf.shape[0]
        scores = xf @ Wg
        ew, ei = jax.lax.top_k(scores, TOP_K)
        ew = jax.nn.softmax(ew, axis=-1)
        cw = jnp.zeros((T, E), dtype=x.dtype).at[jnp.arange(T)[:, None], ei].set(ew)
        y = jnp.zeros_like(xf)
        for e in range(E):
            h = jax.nn.silu(xf @ w1[e]) * (xf @ w3[e])
            y = y + cw[:, e:e + 1] * (h @ w2[e])
        return y.reshape(Bs, Ss, D)

    def _L1_attn_ref(hidden_states, Wq, Wk, Wv, Wo, gamma, beta):
        import jax, jax.numpy as jnp
        import numpy as np
        B, T, HID = (1, 256, 256)
        H = 16
        D = HID // H
        EPS = 1e-05

        def _layer_norm(x, eps=1e-05):
            mu = jnp.mean(x, axis=-1, keepdims=True)
            var = jnp.mean((x - mu) ** 2, axis=-1, keepdims=True)
            return (x - mu) * jax.lax.rsqrt(var + eps)

        def _feature_map(x, gamma, beta):
            return _layer_norm(x * gamma + beta)
        b, t, _ = hidden_states.shape
        q = (hidden_states @ Wq.T).reshape(b, t, H, D)
        k = (hidden_states @ Wk.T).reshape(b, t, H, D)
        v = (hidden_states @ Wv.T).reshape(b, t, H, D)
        q = _feature_map(q, gamma, beta)
        k = _feature_map(k, gamma, beta)
        q = q * D ** (-0.5)
        attn = jnp.einsum('bqhd,bkhd->bhqk', q, k) ** 2
        mask = jnp.tril(jnp.ones((t, t), dtype=bool))
        attn = jnp.where(mask, attn, 0.0)
        o = jnp.einsum('bhqk,bkhd->bqhd', attn, v)
        z = jnp.sum(attn, axis=-1)
        o = o / (jnp.swapaxes(z, 1, 2)[..., None] + EPS)
        o = o.reshape(b, t, H * D)
        return o @ Wo.T

    def _L1_ffn_ref(x, gate_w, expert_w):
        import jax, jax.numpy as jnp
        import numpy as np
        TOP_K = 8

        def _moe_block(hf, gw, ew):
            T, D = hf.shape
            E = gw.shape[0]
            logits = hf @ gw.T
            w = jax.nn.softmax(logits, axis=-1)
            vals, idx = jax.lax.top_k(w, TOP_K)
            w_dense = jnp.zeros_like(w).at[jnp.arange(T)[:, None], idx].add(vals)
            out = jnp.zeros_like(hf)
            for e in range(E):
                out = out + w_dense[:, e:e + 1] * (hf @ ew[e].T)
            return out
        b, t, d = x.shape
        L = gate_w.shape[0]
        h = x
        for l in range(L):
            hf = h.reshape(-1, d)
            h = _moe_block(hf, gate_w[l], expert_w[l]).reshape(b, t, d)
        return h
    x = L0_attn_x
    mod = (_silu(L0_c) @ L0_wmod).reshape(L0_c.shape[0], 6, 1, -1)
    sa, ca, ga, sb, cb, gb = (mod[:, 0], mod[:, 1], mod[:, 2], mod[:, 3], mod[:, 4], mod[:, 5])
    ga = (2 * (ga >= 0) - 1) * jnp.maximum(jnp.abs(ga), 0.25)
    gb = (2 * (gb >= 0) - 1) * jnp.maximum(jnp.abs(gb), 0.25)
    h = _layernorm(x, axis=-1) * (1 + ca) + sa
    x = x + ga * _L0_attn_ref(h, L0_attn_Wq, L0_attn_bq, L0_attn_Wk, L0_attn_bk, L0_attn_Wv, L0_attn_bv, L0_attn_Wo, L0_attn_bo)
    h = _layernorm(x, axis=-1) * (1 + cb) + sb
    x = x + gb * _L0_ffn_ref(h, L0_ffn_Wg, L0_ffn_w1, L0_ffn_w3, L0_ffn_w2)
    mod = (_silu(L1_c) @ L1_wmod).reshape(L1_c.shape[0], 6, 1, -1)
    sa, ca, ga, sb, cb, gb = (mod[:, 0], mod[:, 1], mod[:, 2], mod[:, 3], mod[:, 4], mod[:, 5])
    ga = (2 * (ga >= 0) - 1) * jnp.maximum(jnp.abs(ga), 0.25)
    gb = (2 * (gb >= 0) - 1) * jnp.maximum(jnp.abs(gb), 0.25)
    h = _layernorm(x, axis=-1) * (1 + ca) + sa
    x = x + ga * _L1_attn_ref(h, L1_attn_Wq, L1_attn_Wk, L1_attn_Wv, L1_attn_Wo, L1_attn_gamma, L1_attn_beta)
    h = _layernorm(x, axis=-1) * (1 + cb) + sb
    x = x + gb * _L1_ffn_ref(h, L1_ffn_gate_w, L1_ffn_expert_w)
    return x

_drawn_inputs = setup_inputs


def setup_inputs(seed=0):
    import zlib

    import numpy as np

    out = dict(_drawn_inputs(seed))
    spreads = {}
    factors = {'L0_attn_bq': 8.0,
     'L0_attn_bk': 8.0,
     'L0_attn_bv': 3.549,
     'L0_attn_bo': 3.658,
     'L0_ffn_Wg': 8.0,
     'L0_ffn_w1': 8.0,
     'L0_ffn_w3': 8.0,
     'L0_ffn_w2': 8.0,
     'L1_attn_gamma': 8.0,
     'L1_attn_beta': 8.0,
     'L1_ffn_gate_w': 8.0,
     'L1_ffn_expert_w': 8.0}
    for name, (base, spread) in spreads.items():
        noise = np.random.default_rng([zlib.crc32(name.encode()), seed]).standard_normal(out[name].shape)
        drawn = base * np.exp(spread * noise) if base else spread * noise
        out[name] = jnp.asarray(drawn.astype(out[name].dtype))
    for name, factor in factors.items():
        out[name] = (out[name] * factor).astype(out[name].dtype)
    return out
```

```python
from contextlib import ExitStack

import concourse.bass as bass
from concourse import mybir

F32 = mybir.dt.float32
F32R = mybir.dt.float32r
BF16 = mybir.dt.bfloat16
U32 = mybir.dt.uint32
I32 = mybir.dt.int32
ALU = mybir.AluOpType
ACT = mybir.ActivationFunctionType
AX_X = mybir.AxisListType.X

P = 128
D = 256
KC = D // P
B = 2
S = 1024
TB = S // P
T = B * TB
HN = 16
HD = D // HN
NQ = 4
E0 = 8
HID = 896
HC = HID // P
SLOT = 256
SLOTS = (T * P * 2 + E0 * (SLOT - 1)) // SLOT
E1 = 16
L1N = 4
PAIRS = E1 // 2
STK = 64
MH, ML = 48, 49
BIG = 3.0e38
LN_EPS = 1e-5
Z_EPS = 1e-5

C_ID, C_TRI, C_ONE, C_COS, C_SIN = 0, 128, 256, 384, 512
C_THR, C_SLOT, C_SC, C_BE, C_MQ, C_MK, C_W = 640, 648, 672, 673, 801, 929, 1057


class Tally:

    def __init__(self, sem):
        self.sem, self.n, self.at = sem, 0, {}

    def plan(self, label, k=1):
        self.n += k
        self.at[label] = self.n

    def wait(self, eng, label):
        eng.wait_ge(self.sem, self.at[label])


def adaln_kernel(nc, x, cT0, wmod0, wqkv0, bqkv0, wo0, bo0, wg, w1, w3, w2,
                 cT1, wmod1, wqkv1, wo1, gamma, beta, gw1, ew1, consts, out):
    ctx = ExitStack()
    with ctx:
        def sem(name):
            return ctx.enter_context(nc.semaphore(name))

        def tally(name):
            return Tally(sem(name))

        def sb(name, shape, dt, scope=ctx):
            return scope.enter_context(nc.sbuf_tensor(name, shape, dt))

        PS = ctx.enter_context(nc.psum_tensor("PS", [P, 8, 512], F32))

        slot_in = nc.dram_tensor("slot_in", [SLOTS * SLOT, D], F32, kind="Internal").ap()
        slot_out = nc.dram_tensor("slot_out", [SLOTS * SLOT, D], F32, kind="Internal").ap()
        max_rows = nc.dram_tensor("max_rows", [B * NQ, 64, P], F32, kind="Internal").ap()

        X = sb("X", [P, T, D], F32)
        CST = sb("CST", [P, C_W], F32)
        IDB = sb("IDB", [P, P], BF16)
        MQB = sb("MQB", [P, P], BF16)
        MKB = sb("MKB", [P, P], BF16)
        CS = sb("CS", [P, 2, KC, B], F32)
        CB = sb("CB", [P, KC, B, P], F32)
        MOD = sb("MOD", [P, B, 3 * D], F32)
        STAT = sb("STAT", [P, T, 6], F32)
        MV = sb("MV", [P, T, 2], F32)
        SM = sb("SM", [P, 6, T], F32)
        GT2 = sb("GT2", [P, 2, D], F32)
        ident = CST[:, C_ID:C_ID + P]

        sa = ExitStack()
        Q = sb("Q", [P, HN // 2, S], F32R, sa)
        K = [sb("KA", [P, HN // 2, S], F32R, sa), sb("KB", [P, HN // 2, S], F32R, sa)]
        V = sb("V", [P, TB, HN, HD + 1], F32, sa)
        PR = sb("PR", [P, 2, 4, S], F32, sa)
        HTH = sb("HTH", [P, 2, KC, P], F32R, sa)
        HTL = sb("HTL", [P, 2, KC, P], F32R, sa)
        WH = sb("WH", [P, KC, 3 * D], F32R, sa)
        WL = sb("WL", [P, KC, 3 * D], F32R, sa)
        WOH = sb("WOH", [P, KC, D], F32R, sa)
        WOL = sb("WOL", [P, KC, D], F32R, sa)
        BZ = sb("BZ", [P, 3 * D], F32R, sa)
        BOZ = sb("BOZ", [P, D], F32R, sa)
        BE = sb("BE", [P, P], F32R, sa)
        OT = sb("OT", [P, S], F32, sa)
        ON = sb("ON", [P, TB, D], F32, sa)
        GB = sb("GB", [P, 2, HD], F32, sa)
        MP = sb("MP", [P, 4, TB, 2], F32, sa)
        MX = sb("MX", [P, 2, 4, TB], F32, sa)
        MS = sb("MS", [P, 4, 2, TB], F32, sa)
        MT = sb("MT", [64, P], F32, sa)
        RC = sb("RC", [P, 2, 16], F32, sa)
        sa.close()
        flat = PR[:, :, :, :].rearrange("p a b c -> p (a b c)")
        QS = [flat[:, g * 2048:g * 2048 + 1024].rearrange("p (h c) -> p h c", h=HN) for g in range(2)]
        KS = [flat[:, g * 2048 + 1024:g * 2048 + 2048].rearrange("p (h c) -> p h c", h=HN) for g in range(2)]
        TA = flat[:, 4096:4608]
        TB_ = flat[:, 4608:5120]
        TQ = [flat[:, 5120 + 512 * g:5632 + 512 * g] for g in range(2)]
        HR = [flat[:, 6144 + 256 * g:6400 + 256 * g] for g in range(2)]
        FS = flat[:, 6656:6912].rearrange("p (a b) -> p a b", b=32)
        wraw = flat[:, 0:1536].rearrange("p (k n) -> p k n", k=KC)
        woraw = flat[:, 1536:2048].rearrange("p (k n) -> p k n", k=KC)
        wmraw = flat[:, 2048:3584].rearrange("p (k n) -> p k n", k=KC)
        braw = flat[:, 3584:4352]
        boraw = flat[:, 4352:4608]

        sf = ExitStack()
        HF = sb("HF", [P, T, D], F32, sf)
        WM0 = sb("WM0", [P, KC, 3 * D], F32, sf)
        HG = sb("HG", [P, 2, KC, P], F32, sf)
        WG = sb("WG", [P, KC, E0], F32, sf)
        LG = sb("LG", [P, T, 2 * E0], F32, sf)
        T8 = sb("T8", [P, T, 8], F32, sf)
        R2 = sb("R2", [P, T, 8], F32, sf)
        R1 = sb("R1", [P, T, 8], F32, sf)
        RP = sb("RP", [P, T, 2 * E0], F32, sf)
        RP1 = sb("RP1", [P, T, 2 * E0], F32, sf)
        MM = sb("MM", [P, T, E0], F32, sf)
        A0 = sb("A0", [P, T, E0], F32, sf)
        A1 = sb("A1", [P, T, E0], F32, sf)
        W01 = sb("W01", [P, 2, T], F32, sf)
        WT = sb("WT", [P, 2, T], F32, sf)
        WIN = sb("WIN", [P, T, E0], F32, sf)
        TOT = sb("TOT", [P, T, E0], F32, sf)
        PRE = sb("PRE", [P, T + 1, E0], F32, sf)
        CMP = sb("CMP", [P, E0, 8], F32, sf)
        NT = sb("NT", [P, E0], F32, sf)
        OF = sb("OF", [P, E0 + 1], F32, sf)
        POS = sb("POS", [P, T, E0], F32, sf)
        PA = sb("PA", [P, 2, T, E0], F32, sf)
        PF = sb("PF", [P, 2, T], F32, sf)
        IX = sb("IX", [P, 2, T], U32, sf)
        SE = sb("SE", [P, 24, E0], F32, sf)
        EF = sb("EF", [P, 24], F32, sf)
        EI = sb("EI", [P, 24], I32, sf)
        ZT = sb("ZT", [P, 2 * D], F32, sf)
        XT = sb("XT", [P, 2, 2, D], F32, sf)
        XTH = sb("XTH", [P, 2, KC, SLOT], F32R, sf)
        XTL = sb("XTL", [P, 2, KC, SLOT], F32R, sf)
        R13 = sb("R13", [P, 2, KC, HID], F32, sf)
        RW2 = sb("RW2", [P, HC, D], F32, sf)
        H13 = sb("H13", [P, 2, 2, KC, HID], F32R, sf)
        L13 = sb("L13", [P, 2, 2, KC, HID], F32R, sf)
        H2 = sb("H2", [P, 2, HC, D], F32R, sf)
        L2 = sb("L2", [P, 2, HC, D], F32R, sf)
        SI = sb("SI", [P, 2, SLOT], F32, sf)
        GG = sb("GG", [P, 2, SLOT], F32, sf)
        HH = sb("HH", [P, HC, SLOT], F32R, sf)
        HL = sb("HL", [P, HC, SLOT], F32R, sf)
        YO = sb("YO", [P, 2, 2, D], F32, sf)
        sf.close()
        G0 = R13[:, 0, :, :].rearrange("p k n -> p (k n)")[:, 0:4 * D].rearrange("p (a c d) -> p a c d", a=2, c=2)
        GT = R13[:, 1, :, :].rearrange("p k n -> p (k n)")[:, 0:2 * D].rearrange("p (a d) -> p a d", a=2)

        sg = ExitStack()
        WM1 = sb("WM1", [P, KC, 3 * D], F32, sg)
        HR1 = sb("HR1", [P, 2, D], F32, sg)
        XH = sb("XH", [P, KC, T * P], F32R, sg)
        XL = sb("XL", [P, KC, T * P], F32R, sg)
        AC = sb("AC", [P, 2, T, D], F32, sg)
        GR = sb("GR", [P, L1N, KC, P], F32, sg)
        GWH = sb("GWH", [P, L1N, KC, P], F32R, sg)
        GWL = sb("GWL", [P, L1N, KC, P], F32R, sg)
        LT = sb("LT", [E1, T * P], F32, sg)
        LGT = sb("LGT", [P, T, E1], F32, sg)
        M8 = sb("M8", [P, T, 8], F32, sg)
        RPL = sb("RPL", [P, T, E1], F32, sg)
        EX = sb("EX", [P, T, E1], F32, sg)
        SU = sb("SU", [P, 2, T], F32, sg)
        MK = sb("MK", [P, T, E1], F32, sg)
        WD = sb("WD", [P, T, E1], F32, sg)
        WP = sb("WP", [P, 2, T, 2], F32, sg)
        ER = sb("ER", [P, 2, KC, 2, D], F32, sg)
        EH = sb("EH", [P, 2, KC, 2, D], F32R, sg)
        EL = sb("EL", [P, 2, KC, 2, D], F32R, sg)
        OUT_T = sb("OUT_T", [P, 2, D], F32, sg)
        sg.close()

        def ln_index(use, t):
            return {("A", 0, 0): 0, ("A", 0, 1): 8, ("F", 0): 16, ("A", 1, 0): 32,
                    ("A", 1, 1): 40, ("F", 1): 48}[use] + t

        USES = [("A", 0, 0), ("A", 0, 1), ("F", 0), ("A", 1, 0), ("A", 1, 1), ("F", 1)]
        UNITS = [(L, b) for L in range(2) for b in range(B)]

        loaded = sem("loaded")
        cvt = sem("cvt")
        psum_zero = sem("psum_zero")
        chain = sem("chain")
        silu_c = sem("silu_c")
        cb_ready = sem("cb_ready")
        mod_w = tally("mod_w")
        mod_mm = tally("mod_mm")
        mod_ready = tally("mod_ready")
        w_load = tally("w_load")
        w_hi = tally("w_hi")
        w_ready = tally("w_ready")
        sq_in = tally("sq_in")
        sq_out = tally("sq_out")
        fm_in = tally("fm_in")
        fm_out = tally("fm_out")
        h_ready = tally("h_ready")
        tr_done = tally("tr_done")
        ht_hi = tally("ht_hi")
        ht_lo = tally("ht_lo")
        qkv_done = tally("qkv_done")
        q_ready = tally("q_ready")
        v_ready = tally("v_ready")
        stage_init = tally("stage_init")
        stage_hi = tally("stage_hi")
        stage_lo = tally("stage_lo")
        stk_tr = tally("stk_tr")
        stk_q = tally("stk_q")
        stk_k = tally("stk_k")
        max_mm = tally("max_mm")
        max_red = tally("max_red")
        ms_ready = tally("ms_ready")
        ms_tr = tally("ms_tr")
        mt_ready = tally("mt_ready")
        m_out = tally("m_out")
        m_rows = tally("m_rows")
        st_done = tally("st_done")
        p_act = tally("p_act")
        p_dve = tally("p_dve")
        p_mask = tally("p_mask")
        pv_done = tally("pv_done")
        o_evac = tally("o_evac")
        o_tr = tally("o_tr")
        on_ready = tally("on_ready")
        on_tr = tally("on_tr")
        ont = tally("ont")
        pr_done = tally("pr_done")
        x_new = tally("x_new")
        wg_load = sem("wg_load")
        lg_mm = sem("lg_mm")
        gate_in = sem("gate_in")
        gate_exp = sem("gate_exp")
        route_in = sem("route_in")
        route_mm = sem("route_mm")
        zero_t = sem("zero_t")
        zeroed = sem("zeroed")
        idx_ready = sem("idx_ready")
        scattered = sem("scattered")
        xs_load = [sem(f"xs_load{n}") for n in range(2)]
        wr_load = [sem(f"wr_load{n}") for n in range(3)]
        xs_tr = sem("xs_tr")
        xs_hi = sem("xs_hi")
        xs_lo = sem("xs_lo")
        ws_hi = [sem(f"ws_hi{n}") for n in range(3)]
        ws_lo = [sem(f"ws_lo{n}") for n in range(3)]
        up_mm = sem("up_mm")
        up_silu = sem("up_silu")
        up_gate = sem("up_gate")
        up_hi = sem("up_hi")
        up_lo = sem("up_lo")
        dn_mm = sem("dn_mm")
        y_evac = sem("y_evac")
        y_out = [sem(f"y_out{n}") for n in range(2)]
        gathered = [sem(f"gathered{n}") for n in range(2)]
        g_used = sem("g_used")
        gw_load = sem("gw_load")
        gw_hi = sem("gw_hi")
        gw_lo = sem("gw_lo")
        gt_mm = tally("gt_mm")
        gt_evac = tally("gt_evac")
        gt_tr = tally("gt_tr")
        gt_max = tally("gt_max")
        gt_exp = tally("gt_exp")
        acc_zero = sem("acc_zero")
        er_load = [sem("er_load0"), sem("er_load1")]
        er_hi = sem("er_hi")
        er_lo = sem("er_lo")
        ex_mm = sem("ex_mm")
        wp_ready = sem("wp_ready")
        ev_a = sem("ev_a")
        ev_b = sem("ev_b")
        ln_tr = tally("ln_tr")
        ln_hi = tally("ln_hi")
        ln_lo = tally("ln_lo")
        o_ready = sem("o_ready")
        stored = [sem(f"stored{n}") for n in range(2)]

        for n in range(4):
            mod_w.plan(n, 16)
            mod_mm.plan(n, B)
            for b in range(B):
                mod_ready.plan((n, b), 3)
        for L in range(2):
            w_load.plan(L, 16 * 4)
            w_hi.plan(L, 4 if L == 0 else 2)
            w_ready.plan(L, 4 if L == 0 else 2)
        for u in USES:
            sq_in.plan(u)
            sq_out.plan(u)
            for t in range(T if u[0] == "F" else TB):
                h_ready.plan((u, t))
                tr_done.plan((u, t))
                ht_hi.plan((u, t))
                if u != ("F", 0):
                    ht_lo.plan((u, t))
        for L, b in UNITS:
            for what in () if b else ("ones", "KA", "KB"):
                stage_init.plan((L, what))
            stage_init.plan((L, b), 6)
            for t in range(TB):
                qkv_done.plan((L, b, t))
                q_ready.plan((L, b, t))
                v_ready.plan((L, b, t))
                if L == 1:
                    fm_in.plan((b, t))
                    fm_out.plan((b, t))
                stage_hi.plan((L, b, t), 2)
                stage_lo.plan((L, b, t), 2)
                for what in ("q", "k"):
                    for h in range(2):
                        stk_tr.plan((L, b, t, what, h))
                for h in range(2):
                    stk_q.plan((L, b, t, h))
                    stk_k.plan((L, b, t, h), 2)

        def max_chunks(i):
            w = (i + 1) * P
            if w <= 512:
                return [(0, w)]
            return [(0, 384), (384, 256)] if w == 640 else [(0, 512), (512, w - 512)]

        LEAD = 12

        def steps(L):
            maxes = []
            for g in range(NQ if L == 0 else 0):
                mine = [("max", g, i, j) for i in range(TB) for j in range(4)] + [("msc", g)]
                maxes += mine[:4] + ([("ms", g - 1)] if g else []) + mine[4:]
            if L == 0:
                maxes.append(("ms", NQ - 1))
            seq = maxes[:34 + LEAD]
            rest = maxes[34 + LEAD:]
            for n in range(NQ * TB * 4):
                g, k, j = n // 32, n // 4 % 8, n % 4
                seq.append(("st", g, k, j))
                if j == 1 and n > 4:
                    seq.append(("pv", g, k - 1) if k else ("pv", g - 1, 7))
                seq += rest[:1]
                rest = rest[1:]
                while rest and rest[0][0] in ("ms", "msc"):
                    seq.append(rest.pop(0))
                if g and k == 2 and j == 1:
                    seq += [("otr", g - 1, 0), ("otr", g - 1, 1)]
            return seq + rest + [("pv", NQ - 1, 7), ("otr", NQ - 1, 0), ("otr", NQ - 1, 1)]

        STEPS = {L: steps(L) for L in range(2)}
        ring, ring_read = {}, []

        def ring_use(key, what, label):
            ring[key] = len(ring_read)
            ring_read.append((what, label))

        for L, b in UNITS:
            for st in STEPS[L]:
                key = (L, b) + st
                if st[0] == "max":
                    for c in range(len(max_chunks(st[2]))):
                        max_mm.plan(key + (c,))
                        max_red.plan(key + (c,))
                        ring_use(key + (c,), max_red, key + (c,))
                elif st[0] == "msc":
                    ms_ready.plan((L, b, "ms", st[1]))
                elif st[0] == "ms":
                    for what in (ms_tr, mt_ready):
                        what.plan(key)
                    m_out.plan(key, 16)
                    m_rows.plan(key, 64)
                    ring_use(key, mt_ready, key)
                elif st[0] == "st":
                    st_done.plan(key)
                    (p_dve if L == 1 and st[3] == 3 else p_act).plan(key)
                    if L == 1:
                        p_mask.plan(key)
                elif st[0] == "pv":
                    pv_done.plan(key)
                    if st[2] == TB - 1:
                        o_evac.plan(key)
                elif st[0] == "otr":
                    o_tr.plan(key)
                    on_ready.plan(key)
                    ring_use(key, on_ready, key)
            for t in range(TB):
                on_tr.plan((L, b, t))
                ont.plan((L, b, t))
                ring_use((L, b, "ont", t), ont, (L, b, t))
                pr_done.plan((L, b, t))
                x_new.plan(("A", L, b, t))
            if (L, b) == (0, 1):
                for t in range(T):
                    x_new.plan(("F", 0, t))
        for l in range(L1N):
            for c in range(4):
                gt_mm.plan((l, c))
                gt_evac.plan((l, c))
            for what in (gt_tr, gt_max, gt_exp):
                what.plan(l)
            for t in range(T if l < L1N - 1 else 0):
                ln_tr.plan((l, t))
                ln_hi.plan((l, t))
                ln_lo.plan((l, t))

        def st_index(L, b, st):
            _, g, k, j = st
            return (L * B + b) * NQ * TB * 4 + g * 32 + k * 4 + j

        block = ctx.enter_context(nc.Block())

        @block.sync
        def _(sp):
            for par in range(2):
                sp.sem_inc(y_out[par], 16)
            sp.dma_start(CST[:, :], consts).then_inc(loaded, 16)
            sp.dma_start(CS[:, 0, :, :], cT0.rearrange("(k p) b -> p k b", p=P)).then_inc(loaded, 16)
            sp.dma_start(CS[:, 1, :, :], cT1.rearrange("(k p) b -> p k b", p=P)).then_inc(loaded, 16)
            sp.dma_start(X[:, :, :], x.rearrange("(t p) d -> p t d", p=P)).then_inc(loaded, 16)

            def attention_loads(L):
                wm, w, wo = (wmod0, wqkv0, wo0) if L == 0 else (wmod1, wqkv1, wo1)
                sp.dma_start(wmraw, wm[:, 0:3 * D].rearrange("(k p) n -> p k n", p=P)).then_inc(mod_w.sem, 16)
                sp.dma_start(wraw, w.rearrange("(k p) n -> p k n", p=P)).then_inc(w_load.sem, 16)
                sp.dma_start(woraw, wo.rearrange("(k p) n -> p k n", p=P)).then_inc(w_load.sem, 16)
                if L == 0:
                    sp.dma_start(braw[0:2, :], bqkv0).then_inc(w_load.sem, 16)
                    sp.dma_start(boraw[0:2, :], bo0).then_inc(w_load.sem, 16)
                else:
                    sp.dma_start(GB[:, 0, :], gamma).then_inc(w_load.sem, 16)
                    sp.dma_start(GB[:, 1, :], beta).then_inc(w_load.sem, 16)

            attention_loads(0)
            for b in range(B):
                for st in STEPS[0]:
                    if st[0] != "ms":
                        continue
                    g, key = st[1], (0, b) + st
                    scratch = max_rows[b * NQ + g, :, :]
                    mt_ready.wait(sp, key)
                    sp.dma_start(scratch, MT[:, :]).then_inc(m_out.sem, 16)
                    m_out.wait(sp, key)
                    for j in range(4):
                        row = STK * (j % 2) + MH
                        sp.dma_start(Q[row:row + 2, 2 * g + j // 2, :].bitcast(F32),
                                     scratch[16 * j:16 * j + 16, :].rearrange("(h i) q -> h (i q)", h=2)
                                     ).then_inc(m_rows.sem, 16)

            x_new.wait(sp, ("A", 0, 1, TB - 1))
            sp.dma_start(WM0[:, :, :], wmod0[:, 3 * D:].rearrange("(k p) n -> p k n", p=P)).then_inc(mod_w.sem, 16)
            sp.dma_start(WG[:, :, :], wg.rearrange("(k p) e -> p k e", p=P)).then_inc(wg_load, 16)
            sp.wait_ge(zero_t, 1)
            zrows = slot_in.rearrange("(c p r) d -> c p (r d)", p=P, r=2)
            for c in range(SLOTS):
                sp.dma_start(zrows[c], ZT[:, :]).then_inc(zeroed, 16)

            def slot_rows(s, par):
                sp.dma_start(XT[:, par, :, :], slot_in[bass.ds(s * SLOT, SLOT), :]
                             .rearrange("(a p) d -> p a d", p=P)).then_inc(xs_load[par], 16)

            def slot_weights(s, wait):
                e = sp.value_load(EI[0:1, bass.ds(s, 1)], min_val=0, max_val=E0 - 1)
                for n, w in enumerate((w1, w3, w2)):
                    if wait:
                        sp.wait_ge(ws_hi[n], s)
                        sp.wait_ge(ws_lo[n], s)
                    dst = R13[:, n, :, :] if n < 2 else RW2[:, :, :]
                    sp.dma_start(dst, w[bass.ds(e, 1), :, :].rearrange("a (k p) n -> p (a k) n", p=P)
                                 ).then_inc(wr_load[n], 16)

            sp.wait_ge(idx_ready, 3)
            sp.wait_ge(scattered, 16 * 2 * T)
            slot_rows(0, 0)
            slot_weights(0, False)
            with sp.Fori(0, (SLOTS - 1) // 2, 1) as i:
                for par in range(2):
                    s = i * 2 + par
                    if par:
                        sp.wait_ge(xs_tr, s)
                    slot_rows(s + 1, (par + 1) % 2)
                    if not par:
                        sp.wait_ge(xs_lo, s + 1)
                    slot_weights(s + 1, True)
                    sp.wait_ge(y_evac, s + 2)
                    sp.dma_start(slot_out[bass.ds(s * SLOT, SLOT), :].rearrange("(a p) d -> p a d", p=P),
                                 YO[:, par, :, :]).then_inc(y_out[par], 16)
            sp.wait_ge(y_evac, SLOTS + 1)
            sp.dma_start(slot_out[(SLOTS - 1) * SLOT:SLOTS * SLOT, :].rearrange("(a p) d -> p a d", p=P),
                         YO[:, 0, :, :]).then_inc(y_out[0], 16)

            x_new.wait(sp, ("F", 0, T - 1))
            attention_loads(1)

            x_new.wait(sp, ("A", 1, 1, TB - 1))
            sp.dma_start(WM1[:, :, :], wmod1[:, 3 * D:].rearrange("(k p) n -> p k n", p=P)).then_inc(mod_w.sem, 16)
            for l in range(L1N):
                sp.dma_start(GR[:, l, :, :], gw1[l].rearrange("(k p) e -> p k e", p=P)).then_inc(gw_load, 16)
            ew_pairs = ew1.rearrange("(n e k p) m -> n k p e m", e=2, k=KC, p=P)
            for par in range(2):
                for k in range(KC):
                    sp.dma_start(ER[:, par, k, :, :], ew_pairs[par, k]).then_inc(er_load[par], 16)
            with sp.Fori(0, L1N * PAIRS // 2 - 1, 1) as i:
                for par in range(2):
                    sp.wait_ge(er_lo, i * 2 + (par + 1))
                    for k in range(KC):
                        sp.dma_start(ER[:, par, k, :, :],
                                     ew_pairs[bass.ds(i * 2 + (2 + par), 1), k, :, :, :]
                                     .rearrange("a p e m -> p (a e) m")).then_inc(er_load[par], 16)
            for t in range(T):
                sp.wait_ge(o_ready, t + 1)
                sp.dma_start(out[t * P:(t + 1) * P, :], OUT_T[:, t % 2, :]).then_inc(stored[t % 2], 16)
            for par in range(2):
                sp.wait_ge(stored[par], 16 * T // 2)

        @block.gpsimd
        def _(pool):
            def stage(L, b):
                if b == 0:
                    if L == 1:
                        x_new.wait(pool, ("F", 0, T - 1))
                    pool.memset(V[:, :, :, HD:HD + 1], 1.0).then_inc(stage_init.sem, 1)
                    stage_init.wait(pool, (L, "ones"))
                    pool.memset(K[0][STK:P, :, :].bitcast(F32), 0.0).then_inc(stage_init.sem, 1)
                    stage_init.wait(pool, (L, "KA"))
                    pool.memset(K[1][0:STK, :, :].bitcast(F32), 0.0).then_inc(stage_init.sem, 1)
                    stage_init.wait(pool, (L, "KB"))
                    w_ready.wait(pool, L)
                    mod_mm.wait(pool, 2 * L)
                else:
                    pv_done.wait(pool, (L, 0, "pv", NQ - 1, TB - 1))
                for g in range(2):
                    pool.memset(QS[g][:, :, MH:STK], 0.0).then_inc(stage_init.sem, 1)
                    pool.memset(KS[g][:, :, MH:MH + 2], 1.0).then_inc(stage_init.sem, 1)
                    pool.memset(KS[g][:, :, MH + 2:STK], 0.0).then_inc(stage_init.sem, 1)

            stage(0, 0)
            stage(0, 1)
            pool.wait_ge(idx_ready, 3)
            pool.wait_ge(zeroed, 16 * SLOTS)
            for t in range(T):
                for c in range(2):
                    pool.indirect_dma_start(slot_in[:, :], bass.IndirectOffsetOnAxis(ap=IX[:, c, t:t + 1], axis=0),
                                            HF[:, t, :], None).then_inc(scattered, 16)

            def low_w2(s, par):
                pool.wait_ge(ws_hi[2], s + 1)
                pool.wait_ge(dn_mm, s + 1)
                pool.tensor_tensor(L2[:, par, :, :], RW2[:, :, :], H2[:, par, :, :].bitcast(F32),
                                   ALU.subtract).then_inc(ws_lo[2], 1)

            with pool.Fori(0, (SLOTS - 1) // 2, 1) as i:
                for par in range(2):
                    low_w2(i * 2 + par, par)
            low_w2(SLOTS - 1, 0)
            for par in range(2):
                pool.wait_ge(y_out[par], 16 + 16 * ((SLOTS + 1 - par) // 2))
            for t in range(T):
                if t >= 2:
                    pool.wait_ge(g_used, t - 1)
                for c in range(2):
                    pool.indirect_dma_start(G0[:, t % 2, c, :], None, slot_out[:, :],
                                            bass.IndirectOffsetOnAxis(ap=IX[:, c, t:t + 1], axis=0)
                                            ).then_inc(gathered[t % 2], 16)
            for b in range(B):
                stage(1, b)
                for st in STEPS[1]:
                    if st[0] != "st":
                        continue
                    _, g, k, j = st
                    key = (1, b) + st
                    (p_dve if j == 3 else p_act).wait(pool, key)
                    diag = PR[:, k % 2, j, k * P:(k + 1) * P]
                    pool.affine_select(out=diag, in_=diag, compare_op=ALU.is_ge, fill=0.0, base=0,
                                       pattern=[[1, P]], channel_multiplier=-1).then_inc(p_mask.sem, 1)
            x_new.wait(pool, ("A", 1, 1, TB - 1))
            for l in range(L1N):
                if l >= 2:
                    ln_tr.wait(pool, (l - 2, T - 1))
                pool.memset(AC[:, l % 2, :, :], 0.0).then_inc(acc_zero, 1)
                with pool.Fori(0, PAIRS // 2, 1) as i:
                    for par in range(2):
                        n = i * 2 + (l * PAIRS + par)
                        pool.wait_ge(er_hi, n + 1)
                        pool.wait_ge(ex_mm, n * T + T)
                        pool.tensor_tensor(EL[:, par, :, :, :], ER[:, par, :, :, :],
                                           EH[:, par, :, :, :].bitcast(F32), ALU.subtract).then_inc(er_lo, 1)

        @block.scalar
        def _(act):
            act.wait_ge(loaded, 64)
            act.activation(CS[:, :, :, :], CS[:, :, :, :], ACT.Silu).then_inc(silu_c, 1)

            def high_weights(L):
                w_load.wait(act, L)
                act.activation(WH[:, :, :], wraw, ACT.Copy).then_inc(w_hi.sem, 1)
                act.activation(WOH[:, :, :], woraw, ACT.Copy).then_inc(w_hi.sem, 1)

            def root(use):
                n = T if use[0] == "F" else TB
                sq_in.wait(act, use)
                act.activation(SM[:, 1, 0:n], SM[:, 0, 0:n], ACT.Sqrt).then_inc(sq_out.sem, 1)

            def transposed_hi(use, t):
                tr_done.wait(act, (use, t))
                if use == ("F", 0):
                    if t >= 2:
                        act.wait_ge(lg_mm, t - 1)
                    dst = HG[:, t % 2, :, :]
                elif use == ("F", 1):
                    dst = XH[:, :, t * P:(t + 1) * P]
                else:
                    if t >= 2:
                        qkv_done.wait(act, use[1:] + (t - 2,))
                    dst = HTH[:, t % 2, :, :]
                act.activation(dst, PS[:, t % 2, 0:D].rearrange("p (k c) -> p k c", k=KC),
                               ACT.Copy).then_inc(ht_hi.sem, 1)

            def project(L, b):
                root(("A", L, b))
                stage_init.wait(act, (L, b))
                for s in range(TB + 3):
                    if s < TB:
                        transposed_hi(("A", L, b), s)
                    if 0 <= s - 1 < TB:
                        t = s - 1
                        qkv_done.wait(act, (L, b, t))
                        act.activation(V[:, t, :, 0:HD], PS[:, 4 + t % 2, 0:D].rearrange("p (h c) -> p h c", h=HN),
                                       ACT.Copy).then_inc(v_ready.sem, 1)
                    if 0 <= s - 2 < TB:
                        t = s - 2
                        if L == 1:
                            fm_in.wait(act, (b, t))
                            act.activation(FS[:, 1, :], FS[:, 0, :], ACT.Sqrt).then_inc(fm_out.sem, 1)
                        q_ready.wait(act, (L, b, t))
                        if t >= 2:
                            stk_tr.wait(act, (L, b, t - 2, "k", 1))
                        src = TQ[t % 2].rearrange("p (a h c) -> p a h c", a=2, h=HN)
                        for a, dst in ((0, QS[t % 2][:, :, 0:2 * HD].rearrange("p h (r c) -> p h r c", r=2)),
                                       (1, KS[t % 2][:, :, 0:4 * HD].rearrange("p h (r c) -> p h r c", r=4)[:, :, 0:3:2, :])):
                            act.activation(dst.bitcast(F32R), src[:, a, :, None, :].to_broadcast([P, HN, 2, HD]),
                                           ACT.Copy).then_inc(stage_hi.sem, 1)
                    if 0 <= s - 3 < TB:
                        t = s - 3
                        for h in range(2):
                            stk_tr.wait(act, (L, b, t, "q", h))
                            act.activation(Q[:, 4 * h:4 * h + 4, t * P:(t + 1) * P],
                                           PS[:, 6 + h, :].rearrange("p (a c) -> p a c", a=4),
                                           ACT.Copy).then_inc(stk_q.sem, 1)

            def attend(L, b):
                for st in STEPS[L]:
                    key = (L, b) + st
                    if st[0] == "st" and not (L == 1 and st[3] == 3):
                        _, g, k, j = st
                        st_done.wait(act, key)
                        if g or k >= 2:
                            pv_done.wait(act, (L, b, "pv") + ((g, k - 2) if k >= 2 else (g - 1, k + 6)))
                        else:
                            stk_k.wait(act, (L, b, TB - 1, 1))
                        bank = 2 * (st_index(L, b, st) % 2)
                        src = PS[:, bank:bank + 2, :].rearrange("p a c -> p (a c)")[:, k * P:S]
                        act.activation(PR[:, k % 2, j, k * P:S], src, ACT.Exp if L == 0 else ACT.Square,
                                       scale=0.25).then_inc(p_act.sem, 1)
                    if st[0] == "pv" and st[2] == TB - 1:
                        pv_done.wait(act, key)
                        if st[1] > 0:
                            o_tr.wait(act, (L, b, "otr", st[1] - 1, 1))
                        act.activation(OT[:, :], PS[:, 4:6, :].rearrange("p a c -> p (a c)"),
                                       ACT.Copy).then_inc(o_evac.sem, 1)

            high_weights(0)
            act.wait_ge(cvt, 6)
            act.activation(BZ[0:2, :], braw[0:2, :], ACT.Copy).then_inc(w_hi.sem, 1)
            act.activation(BOZ[0:2, :], boraw[0:2, :], ACT.Copy).then_inc(w_hi.sem, 1)
            for L, b in UNITS[:2]:
                project(L, b)
                attend(L, b)

            root(("F", 0))
            for t in range(T):
                transposed_hi(("F", 0), t)
            act.wait_ge(gate_in, 1)
            act.activation(WT[:, 0, :], WT[:, 1, :], ACT.Exp).then_inc(gate_exp, 1)

            def high_slot_weights(s, par, n):
                act.wait_ge(wr_load[n], s * 16 + 16)
                act.wait_ge(dn_mm, s + 1)
                src, dst = (R13[:, n, :, :], H13[:, par, n, :, :]) if n < 2 else (RW2[:, :, :], H2[:, par, :, :])
                act.activation(dst, src, ACT.Copy).then_inc(ws_hi[n], 1)

            def high_slot_rows(s, par):
                act.wait_ge(xs_tr, s + 1)
                act.activation(XTH[:, par, :, :], PS[:, 6, :].rearrange("p (k c) -> p k c", k=KC), ACT.Copy).then_inc(xs_hi, 1)

            def slot_hidden(s, c):
                act.wait_ge(up_mm, s * HC + (c + 1))
                act.activation(SI[:, c % 2, :], PS[:, c % 4, 0:SLOT], ACT.Silu).then_inc(up_silu, 1)
                act.wait_ge(up_gate, s * HC + (c + 1))
                act.activation(HH[:, c, :], GG[:, c % 2, :], ACT.Copy).then_inc(up_hi, 1)

            high_slot_rows(0, 0)
            for n in range(3):
                high_slot_weights(0, 0, n)
            with act.Fori(0, (SLOTS - 1) // 2, 1) as i:
                for par in range(2):
                    s = i * 2 + par
                    for c in range(HC):
                        slot_hidden(s, c)
                        if c in (1, 3, 5):
                            high_slot_weights(s + 1, (par + 1) % 2, (c - 1) // 2)
                        if c == 4:
                            high_slot_rows(s + 1, (par + 1) % 2)
            for c in range(HC):
                slot_hidden(SLOTS - 1, c)

            high_weights(1)
            for L, b in UNITS[2:]:
                project(L, b)
                attend(L, b)
            act.wait_ge(gw_load, 16 * L1N)
            act.activation(GWH[:, :, :, :], GR[:, :, :, :], ACT.Copy).then_inc(gw_hi, 1)
            root(("F", 1))
            for t in range(T):
                transposed_hi(("F", 1), t)
            for l in range(L1N):
                for c in range(4):
                    gt_mm.wait(act, (l, c))
                    if l:
                        gt_tr.wait(act, l - 1)
                    act.activation(LT[:, c * 512:(c + 1) * 512], PS[0:E1, 2 + c, :], ACT.Copy).then_inc(gt_evac.sem, 1)

                def high_pair(n, par, count):
                    act.wait_ge(er_load[par], count)
                    act.wait_ge(ex_mm, n * T + T)
                    act.activation(EH[:, par, :, :, :], ER[:, par, :, :, :], ACT.Copy).then_inc(er_hi, 1)

                gt_max.wait(act, l)
                act.activation(EX[:, :, :], EX[:, :, :], ACT.Exp).then_inc(gt_exp.sem, 1)
                with act.Fori(0, PAIRS // 2, 1) as i:
                    for par in range(2):
                        high_pair(i * 2 + (l * PAIRS + par), par, i * 32 + 32 * (l * PAIRS // 2 + 1))
                for t in range(T if l < L1N - 1 else 0):
                    ln_tr.wait(act, (l, t))
                    act.activation(XH[:, :, t * P:(t + 1) * P], PS[:, t % 2, 0:D].rearrange("p (k c) -> p k c", k=KC),
                                   ACT.Copy).then_inc(ln_hi.sem, 1)

        @block.vector
        def _(dve):
            links = [0]

            def link(ins):
                links[0] += 1
                ins.then_inc(chain, 1)
                dve.wait_ge(chain, links[0])

            dve.sem_inc(ev_b, T)
            dve.sem_inc(y_evac, 1)
            dve.memset(PS[:, 4:6, :], 0.0).then_inc(psum_zero, 1)
            dve.memset(BZ[:, :].bitcast(F32), 0.0).then_inc(cvt, 1)
            dve.memset(BOZ[:, :].bitcast(F32), 0.0).then_inc(cvt, 1)
            dve.memset(MP[:, :, :, :], -BIG).then_inc(cvt, 1)
            dve.wait_ge(loaded, 64)
            dve.tensor_copy(IDB[:, :], ident).then_inc(cvt, 1)
            dve.tensor_copy(MQB[:, :], CST[:, C_MQ:C_MQ + P]).then_inc(cvt, 1)
            dve.tensor_copy(MKB[:, :], CST[:, C_MK:C_MK + P]).then_inc(cvt, 1)
            dve.tensor_copy(BE[:, :], CST[:, C_BE:C_BE + P]).then_inc(cvt, 1)
            dve.wait_ge(silu_c, 1)

            def spread(L):
                dve.tensor_copy(CB[:, :, :, :].rearrange("p k b c -> p (k b) c"),
                                CS[:, L, :, :].rearrange("p k b -> p (k b)")[:, :, None].to_broadcast([P, KC * B, P])
                                ).then_inc(cb_ready, 1)

            def modulation(n):
                mod_mm.wait(dve, n)
                for b in range(B):
                    src = PS[:, 4 + 2 * b:6 + 2 * b, :].rearrange("p a c -> p (a c)")
                    gate = src[:, 2 * D:3 * D]
                    dve.tensor_copy(MOD[:, b, 0:D], src[:, 0:D]).then_inc(mod_ready.sem, 1)
                    dve.tensor_scalar(MOD[:, b, D:2 * D], src[:, D:2 * D], 1.0, None, ALU.add).then_inc(mod_ready.sem, 1)
                    dve.tensor_scalar(GT2[:, 1, :], gate, 0.0, 2.0, ALU.is_ge, ALU.mult)
                    link(dve.tensor_scalar(GT2[:, 0, :], gate, -1.0, None, ALU.mult))
                    link(dve.tensor_tensor(GT2[:, 0, :], gate, GT2[:, 0, :], ALU.max))
                    link(dve.tensor_scalar(GT2[:, 0, :], GT2[:, 0, :], 0.25, None, ALU.max))
                    dve.scalar_tensor_tensor(out=MOD[:, b, 2 * D:3 * D], in0=GT2[:, 1, :], scalar=-1.0,
                                             in1=GT2[:, 0, :], op0=ALU.add, op1=ALU.mult).then_inc(mod_ready.sem, 1)
                    mod_ready.wait(dve, (n, b))

            def low_weights(L):
                w_hi.wait(dve, L)
                dve.tensor_tensor(WL[:, :, :], wraw, WH[:, :, :].bitcast(F32), ALU.subtract).then_inc(w_ready.sem, 1)
                dve.tensor_tensor(WOL[:, :, :], woraw, WOH[:, :, :].bitcast(F32), ALU.subtract).then_inc(w_ready.sem, 1)
                if L == 0:
                    for dst, raw in ((BZ, braw), (BOZ, boraw)):
                        dve.scalar_tensor_tensor(out=dst[0:2, :], in0=dst[0:2, :].bitcast(F32), scalar=CST[0:2, C_SC:C_SC + 1],
                                                 in1=raw[0:2, :], op0=ALU.mult, op1=ALU.add).then_inc(w_ready.sem, 1)

            def refine(y, v, tmp):
                link(dve.tensor_tensor(tmp, y, y, ALU.mult))
                link(dve.tensor_tensor(tmp, tmp, v, ALU.mult))
                link(dve.tensor_scalar(tmp, tmp, -0.5, 1.5, ALU.mult, ALU.add))
                link(dve.tensor_tensor(y, y, tmp, ALU.mult))

            def statistics(use):
                t0, n = (0, T) if use[0] == "F" else (use[2] * TB, TB)
                if use != ("A", 0, 0):
                    before = {("A", 0, 1): ("A", 0, 0, TB - 1), ("F", 0): ("A", 0, 1, TB - 1), ("A", 1, 0): ("F", 0, T - 1),
                              ("A", 1, 1): ("A", 1, 0, TB - 1), ("F", 1): ("A", 1, 1, TB - 1)}[use]
                    x_new.wait(dve, before)
                for t in range(n):
                    last = dve.bn_stats(STAT[:, t, :], X[:, t0 + t, :])
                link(last)
                for t in range(n):
                    last = dve.bn_aggr(MV[:, t, :], STAT[:, t, :])
                link(last)
                dve.tensor_scalar(SM[:, 0, 0:n], MV[:, 0:n, 1], LN_EPS, None, ALU.add).then_inc(sq_in.sem, 1)
                sq_out.wait(dve, use)
                link(dve.reciprocal(SM[:, 2, 0:n], SM[:, 1, 0:n]))
                refine(SM[:, 2, 0:n], SM[:, 0, 0:n], SM[:, 3, 0:n])
                link(dve.scalar_tensor_tensor(out=SM[:, 4, 0:n], in0=MV[:, 0:n, 0], scalar=-1.0, in1=SM[:, 2, 0:n],
                                              op0=ALU.mult, op1=ALU.mult))

            def normalised(use, t, h):
                t0 = 0 if use[0] == "F" else use[2] * TB
                b = (t0 + t) // TB
                if t >= 2 and use != ("F", 0):
                    tr_done.wait(dve, (use, t - 2))
                link(dve.tensor_scalar(h, X[:, t0 + t, :], SM[:, 2, t:t + 1], SM[:, 4, t:t + 1], ALU.mult, ALU.add))
                link(dve.tensor_tensor(h, h, MOD[:, b, D:2 * D], ALU.mult))
                dve.tensor_tensor(h, h, MOD[:, b, 0:D], ALU.add).then_inc(h_ready.sem, 1)

            def transposed_lo(use, t):
                ht_hi.wait(dve, (use, t))
                hi, lo = ((XH[:, :, t * P:(t + 1) * P], XL[:, :, t * P:(t + 1) * P]) if use == ("F", 1)
                          else (HTH[:, t % 2, :, :], HTL[:, t % 2, :, :]))
                dve.tensor_tensor(lo, PS[:, t % 2, 0:D].rearrange("p (k c) -> p k c", k=KC), hi.bitcast(F32),
                                  ALU.subtract).then_inc(ht_lo.sem, 1)

            def rotate(b, t):
                qkv_done.wait(dve, (0, b, t))
                src = PS[:, 2 + t % 2, :].rearrange("p (h c) -> p h c", c=HD)
                cos = CST[:, C_COS + t * HD:C_COS + (t + 1) * HD]
                sin = CST[:, C_SIN + t * HD:C_SIN + (t + 1) * HD]
                dve.tensor_tensor(TA.rearrange("p (h c) -> p h c", c=HD), src,
                                  cos[:, None, :].to_broadcast([P, 2 * HN, HD]), ALU.mult)
                tb = TB_.rearrange("p (h c) -> p h c", c=HD)
                for o in range(2):
                    last = dve.tensor_tensor(tb[:, :, o:HD:2], src[:, :, 1 - o:HD:2],
                                             sin[:, None, o:HD:2].to_broadcast([P, 2 * HN, HD // 2]), ALU.mult)
                link(last)
                dve.tensor_tensor(TQ[t % 2], TA, TB_, ALU.add).then_inc(q_ready.sem, 1)

            def feature_map(b, t):
                qkv_done.wait(dve, (1, b, t))
                src = PS[:, 2 + t % 2, :].rearrange("p (h c) -> p h c", c=HD)
                ta, tb = (v.rearrange("p (h c) -> p h c", c=HD) for v in (TA, TB_))
                link(dve.tensor_tensor(ta, src, GB[:, 0, None, :].to_broadcast([P, 2 * HN, HD]), ALU.mult))
                link(dve.tensor_tensor(ta, ta, GB[:, 1, None, :].to_broadcast([P, 2 * HN, HD]), ALU.add))
                link(dve.tensor_reduce(FS[:, 2, :], ta, AX_X, ALU.add))
                link(dve.scalar_tensor_tensor(out=tb, in0=FS[:, 2, :, None].to_broadcast([P, 2 * HN, HD]), scalar=-1.0 / HD,
                                              in1=ta, op0=ALU.mult, op1=ALU.add))
                link(dve.tensor_tensor(ta, tb, tb, ALU.mult))
                link(dve.tensor_reduce(FS[:, 3, :], ta, AX_X, ALU.add))
                dve.tensor_scalar(FS[:, 0, :], FS[:, 3, :], 1.0 / HD, LN_EPS, ALU.mult, ALU.add).then_inc(fm_in.sem, 1)
                fm_out.wait(dve, (b, t))
                link(dve.reciprocal(FS[:, 4, :], FS[:, 1, :]))
                refine(FS[:, 4, :], FS[:, 0, :], FS[:, 5, :])
                dve.tensor_tensor(TQ[t % 2].rearrange("p (h c) -> p h c", c=HD), tb,
                                  FS[:, 4, :, None].to_broadcast([P, 2 * HN, HD]), ALU.mult).then_inc(q_ready.sem, 1)

            def project(L, b):
                use = ("A", L, b)
                statistics(use)
                stage_init.wait(dve, (L, b))
                for s in range(TB + 3):
                    if s < TB:
                        normalised(use, s, HR[s % 2])
                    if 0 <= s - 1 < TB:
                        if s - 1 >= 2:
                            qkv_done.wait(dve, (L, b, s - 3))
                        transposed_lo(use, s - 1)
                    if 0 <= s - 2 < TB:
                        (feature_map if L else rotate)(b, s - 2)
                    if 0 <= s - 3 < TB:
                        t = s - 3
                        for h in range(2):
                            stk_tr.wait(dve, (L, b, t, "k", h))
                            for e, rows in ((0, slice(0, STK)), (1, slice(STK, P))):
                                dve.tensor_copy(K[e][rows, 4 * h:4 * h + 4, t * P:(t + 1) * P],
                                                PS[rows, 6 + h, :].rearrange("p (a c) -> p a c", a=4)).then_inc(stk_k.sem, 1)
                    if 0 <= s - 2 < TB:
                        t = s - 2
                        stage_hi.wait(dve, (L, b, t))
                        src = TQ[t % 2].rearrange("p (a h c) -> p a h c", a=2, h=HN)
                        dve.tensor_tensor(QS[t % 2][:, :, 2 * HD:3 * HD].bitcast(F32R), src[:, 0, :, :], QS[t % 2][:, :, 0:HD],
                                          ALU.subtract).then_inc(stage_lo.sem, 1)
                        dve.tensor_tensor(KS[t % 2][:, :, HD:2 * HD].bitcast(F32R), src[:, 1, :, :], KS[t % 2][:, :, 0:HD],
                                          ALU.subtract).then_inc(stage_lo.sem, 1)

            def attend(L, b):
                for st in STEPS[L]:
                    key = (L, b) + st
                    if st[0] == "max":
                        _, g, i, j = st
                        for c, (c0, w) in enumerate(max_chunks(i)):
                            max_mm.wait(dve, key + (c,))
                            dve.tensor_reduce(MP[:, j, i, c:c + 1], PS[:, 6 + ring[key + (c,)] % 2, 0:w], AX_X,
                                              ALU.max).then_inc(max_red.sem, 1)
                    elif st[0] == "msc":
                        g = st[1]
                        max_red.wait(dve, (L, b, "max", g, TB - 1, 3, 1))
                        link(dve.tensor_reduce(MX[:, 0, :, :], MP[:, :, :, :], AX_X, ALU.max))
                        link(dve.tensor_scalar(MX[:, 1, :, :], MX[:, 0, :, :], -1.0, None, ALU.mult))
                        link(dve.tensor_copy(MS[:, :, 0, :].bitcast(F32R), MX[:, 1, :, :]))
                        dve.tensor_tensor(MS[:, :, 1, :].bitcast(F32R), MX[:, 1, :, :], MS[:, :, 0, :],
                                          ALU.subtract).then_inc(ms_ready.sem, 1)
                    elif st[0] == "ms":
                        ms_tr.wait(dve, key)
                        if b or st[1]:
                            m_out.wait(dve, (L, b, "ms", st[1] - 1) if st[1] else (L, 0, "ms", NQ - 1))
                        dve.tensor_copy(MT[:, :], PS[0:64, 6 + ring[key] % 2, 0:P]).then_inc(mt_ready.sem, 1)
                    elif st[0] == "st" and L == 1 and st[3] == 3:
                        _, g, k, j = st
                        st_done.wait(dve, key)
                        if g or k >= 2:
                            pv_done.wait(dve, (L, b, "pv") + ((g, k - 2) if k >= 2 else (g - 1, k + 6)))
                        else:
                            stk_k.wait(dve, (L, b, TB - 1, 1))
                        bank = 2 * (st_index(L, b, st) % 2)
                        src = PS[:, bank:bank + 2, :].rearrange("p a c -> p (a c)")[:, k * P:S]
                        dst = PR[:, k % 2, j, k * P:S]
                        link(dve.tensor_scalar(dst, src, 0.0625, None, ALU.mult))
                        dve.tensor_tensor(dst, src, dst, ALU.mult).then_inc(p_dve.sem, 1)
                    elif st[0] == "otr":
                        _, g, half = st
                        o_tr.wait(dve, key)
                        if g or half:
                            on_ready.wait(dve, (L, b, "otr") + ((g, 0) if half else (g - 1, 1)))
                        src = PS[:, 6 + ring[key] % 2, :].rearrange("p (t j c) -> p t j c", t=4, j=4)
                        sums = src[:, :, :, HD:HD + 1].rearrange("p t j a -> p t (j a)")
                        rc = RC[:, 0, :].rearrange("p (t j) -> p t j", t=4)
                        if L == 1:
                            link(dve.tensor_scalar(RC[:, 1, :].rearrange("p (t j) -> p t j", t=4), sums, Z_EPS, None, ALU.add))
                            sums = RC[:, 1, :].rearrange("p (t j) -> p t j", t=4)
                        link(dve.reciprocal(rc, sums))
                        dve.tensor_tensor(ON[:, 4 * half:4 * half + 4, 64 * g:64 * g + 64].rearrange("p t (j c) -> p t j c", j=4),
                                          src[:, :, :, 0:HD], rc[:, :, :, None].to_broadcast([P, 4, 4, HD]),
                                          ALU.mult).then_inc(on_ready.sem, 1)
                for t in range(TB + 1):
                    if t < TB:
                        on_tr.wait(dve, (L, b, t))
                        if t >= 2:
                            pr_done.wait(dve, (L, b, t - 2))
                        src = PS[:, 6 + ring[(L, b, "ont", t)] % 2, 0:D].rearrange("p (k c) -> p k c", k=KC)
                        link(dve.tensor_copy(HTH[:, t % 2, :, :], src))
                        dve.tensor_tensor(HTL[:, t % 2, :, :], src, HTH[:, t % 2, :, :].bitcast(F32),
                                          ALU.subtract).then_inc(ont.sem, 1)
                    if t >= 1:
                        pr_done.wait(dve, (L, b, t - 1))
                        if t >= 3:
                            x_new.wait(dve, ("A", L, b, t - 3))
                        gated = GT2[:, (t - 1) % 2, :]
                        link(dve.tensor_tensor(gated, PS[:, (t - 1) % 2, 0:D], MOD[:, b, 2 * D:3 * D], ALU.mult))
                        dve.tensor_tensor(X[:, b * TB + t - 1, :], X[:, b * TB + t - 1, :], gated,
                                          ALU.add).then_inc(x_new.sem, 1)

            spread(0)
            modulation(0)
            low_weights(0)
            for L, b in UNITS[:2]:
                project(L, b)
                attend(L, b)

            dve.memset(ZT[:, :], 0.0).then_inc(zero_t, 1)
            dve.memset(LG[:, :, :], BIG)
            dve.memset(R1[:, :, :], BIG)
            dve.memset(R2[:, :, :], BIG)
            link(dve.memset(PRE[:, :, :], 0.0))
            link(dve.memset(OF[:, :], 0.0))
            modulation(1)
            statistics(("F", 0))
            for t in range(T):
                normalised(("F", 0), t, HF[:, t, :])
            dve.wait_ge(lg_mm, T)
            link(dve.tensor_copy(LG[:, :, 0:E0], PS[:, 2, 0:T * E0].rearrange("p (t e) -> p t e", t=T)))
            for t in range(T):
                last = dve.max(T8[:, t, :], LG[:, t, 0:E0])
            link(last)
            dve.tensor_copy(R2[:, :, 0:2], T8[:, :, 0:2])
            dve.tensor_copy(R1[:, :, 0:1], T8[:, :, 0:1])
            link(dve.tensor_tensor(WT[:, 1, :], T8[:, :, 1], T8[:, :, 0], ALU.subtract))
            dve.tensor_copy(WT[:, 1, :], WT[:, 1, :]).then_inc(gate_in, 1)
            for t in range(T):
                dve.match_replace(RP[:, t, :], R2[:, t, :], LG[:, t, :], -BIG)
                last = dve.match_replace(RP1[:, t, :], R1[:, t, :], LG[:, t, :], -BIG)
            link(last)
            dve.tensor_tensor(MM[:, :, :], RP[:, :, 0:E0], LG[:, :, 0:E0], ALU.not_equal).then_inc(route_in, 1)
            link(dve.tensor_tensor(A0[:, :, :], RP1[:, :, 0:E0], LG[:, :, 0:E0], ALU.not_equal))
            dve.wait_ge(route_in, 1)
            link(dve.tensor_tensor(A1[:, :, :], MM[:, :, :], A0[:, :, :], ALU.subtract))
            dve.wait_ge(gate_exp, 1)
            link(dve.tensor_scalar(WT[:, 1, :], WT[:, 0, :], 1.0, None, ALU.add))
            link(dve.reciprocal(W01[:, 0, :], WT[:, 1, :]))
            link(dve.tensor_tensor(W01[:, 1, :], W01[:, 0, :], WT[:, 0, :], ALU.mult))
            dve.wait_ge(route_mm, 1)
            dve.tensor_copy(WIN[:, :, :], PS[:, 3, 0:T * E0].rearrange("p (t e) -> p t e", t=T))
            link(dve.tensor_copy(TOT[:, :, :], PS[:, 3, P:P + T * E0].rearrange("p (t e) -> p t e", t=T)))
            for t in range(T):
                link(dve.tensor_tensor(PRE[:, t + 1, :], PRE[:, t, :], TOT[:, t, :], ALU.add))
            link(dve.tensor_tensor(CMP[:, :, :], PRE[:, T, :, None].to_broadcast([P, E0, 8]),
                                   CST[:, None, C_THR:C_THR + 8].to_broadcast([P, E0, 8]), ALU.is_gt))
            link(dve.tensor_reduce(NT[:, :], CMP[:, :, :], AX_X, ALU.add))
            for e in range(E0):
                link(dve.tensor_tensor(OF[:, e + 1:e + 2], OF[:, e:e + 1], NT[:, e:e + 1], ALU.add))
            link(dve.tensor_tensor(POS[:, :, :], WIN[:, :, :], PRE[:, 0:T, :], ALU.add))
            link(dve.scalar_tensor_tensor(out=POS[:, :, :], in0=OF[:, None, 0:E0].to_broadcast([P, T, E0]), scalar=float(SLOT),
                                          in1=POS[:, :, :], op0=ALU.mult, op1=ALU.add))
            dve.tensor_tensor(PA[:, 0, :, :], POS[:, :, :], A0[:, :, :], ALU.mult)
            link(dve.tensor_tensor(PA[:, 1, :, :], POS[:, :, :], A1[:, :, :], ALU.mult))
            link(dve.tensor_reduce(PF[:, :, :], PA[:, :, :, :], AX_X, ALU.add))
            dve.tensor_copy(IX[:, :, :], PF[:, :, :]).then_inc(idx_ready, 1)
            link(dve.tensor_tensor(SE[:, :, :], CST[:, C_SLOT:C_SLOT + 24, None].to_broadcast([P, 24, E0]),
                                   OF[:, None, 1:E0 + 1].to_broadcast([P, 24, E0]), ALU.is_ge))
            link(dve.tensor_reduce(EF[:, :], SE[:, :, :], AX_X, ALU.add))
            dve.tensor_scalar(EF[:, :], EF[:, :], float(E0 - 1), None, ALU.min).then_inc(idx_ready, 1)
            dve.wait_ge(idx_ready, 2)
            dve.tensor_copy(EI[:, :], EF[:, :]).then_inc(idx_ready, 1)

            def low_slot_weights(s, par, n):
                dve.wait_ge(ws_hi[n], s + 1)
                dve.tensor_tensor(L13[:, par, n, :, :], R13[:, n, :, :], H13[:, par, n, :, :].bitcast(F32),
                                  ALU.subtract).then_inc(ws_lo[n], 1)

            def low_slot_rows(s, par):
                dve.wait_ge(xs_hi, s + 1)
                dve.tensor_tensor(XTL[:, par, :, :], PS[:, 6, :].rearrange("p (k c) -> p k c", k=KC),
                                  XTH[:, par, :, :].bitcast(F32), ALU.subtract).then_inc(xs_lo, 1)

            def hidden_gate(s, c):
                dve.wait_ge(up_silu, s * HC + (c + 1))
                if c >= 2:
                    dve.wait_ge(up_lo, s * HC + (c - 1))
                dve.tensor_tensor(GG[:, c % 2, :], PS[:, c % 4, SLOT:2 * SLOT], SI[:, c % 2, :], ALU.mult).then_inc(up_gate, 1)

            def hidden_low(s, c):
                dve.wait_ge(up_hi, s * HC + (c + 1))
                dve.tensor_tensor(HL[:, c, :], GG[:, c % 2, :], HH[:, c, :].bitcast(F32), ALU.subtract).then_inc(up_lo, 1)

            def slot_output(s, par, pair):
                dve.wait_ge(dn_mm, s + 3)
                dve.wait_ge(y_out[par], pair * 16 + 16)
                dve.tensor_copy(YO[:, par, :, :], PS[:, 4:6, 0:D]).then_inc(y_evac, 1)

            low_slot_rows(0, 0)
            low_slot_weights(0, 0, 0)
            low_slot_weights(0, 0, 1)
            with dve.Fori(0, (SLOTS - 1) // 2, 1) as i:
                for par in range(2):
                    s = i * 2 + par
                    for c in range(HC):
                        hidden_gate(s, c)
                        if c:
                            hidden_low(s, c - 1)
                        if c in (1, 3):
                            low_slot_weights(s + 1, (par + 1) % 2, (c - 1) // 2)
                        if c == 4:
                            low_slot_rows(s + 1, (par + 1) % 2)
                    hidden_low(s, HC - 1)
                    slot_output(s, par, i)
            for c in range(HC):
                hidden_gate(SLOTS - 1, c)
                if c:
                    hidden_low(SLOTS - 1, c - 1)
            hidden_low(SLOTS - 1, HC - 1)
            slot_output(SLOTS - 1, 0, SLOTS // 2)
            for t in range(T):
                dve.wait_ge(gathered[t % 2], 32 * (t // 2 + 1))
                link(dve.tensor_scalar(GT[:, 0, :], G0[:, t % 2, 0, :], W01[:, 0, t:t + 1], None, ALU.mult))
                dve.scalar_tensor_tensor(out=GT[:, 1, :], in0=G0[:, t % 2, 1, :], scalar=W01[:, 1, t:t + 1], in1=GT[:, 0, :],
                                         op0=ALU.mult, op1=ALU.add).then_inc(g_used, 1)
                dve.wait_ge(g_used, t + 1)
                link(dve.tensor_tensor(GT2[:, 0, :], GT[:, 1, :], MOD[:, t // TB, 2 * D:3 * D], ALU.mult))
                dve.tensor_tensor(X[:, t, :], X[:, t, :], GT2[:, 0, :], ALU.add).then_inc(x_new.sem, 1)

            spread(1)
            modulation(2)
            low_weights(1)
            for L, b in UNITS[2:]:
                project(L, b)
                attend(L, b)
            modulation(3)
            dve.wait_ge(gw_hi, 1)
            dve.tensor_tensor(GWL[:, :, :, :], GR[:, :, :, :], GWH[:, :, :, :].bitcast(F32), ALU.subtract).then_inc(gw_lo, 1)
            statistics(("F", 1))
            for s in range(T + 1):
                if s < T:
                    normalised(("F", 1), s, HR1[:, s % 2, :])
                if s:
                    transposed_lo(("F", 1), s - 1)
            for l in range(L1N):
                gt_tr.wait(dve, l)
                link(dve.tensor_copy(LGT[:, :, :], PS[:, 6, 0:T * E1].rearrange("p (t e) -> p t e", t=T)))
                for t in range(T):
                    last = dve.max(M8[:, t, :], LGT[:, t, :])
                link(last)
                dve.tensor_tensor(EX[:, :, :], LGT[:, :, :], M8[:, :, 0:1].to_broadcast([P, T, E1]),
                                  ALU.subtract).then_inc(gt_max.sem, 1)
                for t in range(T):
                    last = dve.match_replace(RPL[:, t, :], M8[:, t, :], LGT[:, t, :], -BIG)
                link(last)
                link(dve.tensor_tensor(MK[:, :, :], RPL[:, :, :], LGT[:, :, :], ALU.not_equal))
                gt_exp.wait(dve, l)
                link(dve.tensor_reduce(SU[:, 0, :], EX[:, :, :], AX_X, ALU.add))
                link(dve.reciprocal(SU[:, 1, :], SU[:, 0, :]))
                link(dve.tensor_tensor(WD[:, :, :], EX[:, :, :], MK[:, :, :], ALU.mult))
                link(dve.tensor_tensor(WD[:, :, :], WD[:, :, :], SU[:, 1, :, None].to_broadcast([P, T, E1]), ALU.mult))
                dve.wait_ge(acc_zero, l + 1)
                with dve.Fori(0, PAIRS // 2, 1) as i:
                    for par in range(2):
                        n = i * 2 + (l * PAIRS + par)
                        dve.tensor_copy(WP[:, par, :, :], WD[:, :, bass.ds(i * 4 + 2 * par, 2)]).then_inc(wp_ready, 1)
                        dve.wait_ge(wp_ready, n + 1)
                        for s in range(T + 1):
                            for e, t in ((0, s), (1, s - 1)):
                                if not 0 <= t < T:
                                    continue
                                if e == 0:
                                    dve.wait_ge(ex_mm, n * T + (2 * T + t + 1))
                                    dve.wait_ge(ev_b, n * T + (t + 1))
                                else:
                                    dve.wait_ge(ev_a, n * T + (t + 1))
                                acc = AC[:, l % 2, t, :]
                                dve.scalar_tensor_tensor(out=acc, in0=PS[:, 2 + t % 4, e * D:(e + 1) * D],
                                                         scalar=WP[:, par, t, e:e + 1], in1=acc, op0=ALU.mult,
                                                         op1=ALU.add).then_inc((ev_a, ev_b)[e], 1)
                for t in range(T if l < L1N - 1 else 0):
                    ln_hi.wait(dve, (l, t))
                    dve.tensor_tensor(XL[:, :, t * P:(t + 1) * P], PS[:, t % 2, 0:D].rearrange("p (k c) -> p k c", k=KC),
                                      XH[:, :, t * P:(t + 1) * P].bitcast(F32), ALU.subtract).then_inc(ln_lo.sem, 1)
            dve.wait_ge(ev_b, L1N * PAIRS * T + T)
            for t in range(T):
                if t >= 2:
                    dve.wait_ge(stored[t % 2], 16 * (t // 2))
                link(dve.tensor_tensor(GT2[:, t % 2, :], AC[:, (L1N - 1) % 2, t, :], MOD[:, t // TB, 2 * D:3 * D], ALU.mult))
                dve.tensor_tensor(OUT_T[:, t % 2, :], X[:, t, :], GT2[:, t % 2, :], ALU.add).then_inc(o_ready, 1)

        @block.tensor
        def _(pe):
            pe.sem_inc(dn_mm, 2)
            pe.sem_inc(ex_mm, 2 * T)

            def exact(out_, pairs, first=True, last=True):
                for n, (a, w) in enumerate(pairs):
                    ins = pe.matmul(out_, a, w, start=first and n == 0, stop=last and n == len(pairs) - 1,
                                    skip_group_check=True)
                return ins

            def modulation(n):
                mod_w.wait(pe, n)
                pe.wait_ge(cb_ready, n // 2 + 1)
                w = {0: wmraw, 1: WM0[:, :, :], 2: wmraw, 3: WM1[:, :, :]}[n]
                for b in range(B):
                    for c, (c0, width) in enumerate(((0, 512), (512, 256))):
                        for k in range(KC):
                            ins = pe.matmul(PS[:, 4 + 2 * b + c, 0:width], CB[:, k, b, :], w[:, k, c0:c0 + width],
                                            start=k == 0, stop=k == KC - 1)
                    ins.then_inc(mod_mm.sem, 1)

            def normalised_transposes(use, t, h):
                h_ready.wait(pe, (use, t))
                if t >= 2:
                    (ht_hi if use == ("F", 0) else ht_lo).wait(pe, (use, t - 2))
                for k in range(KC):
                    ins = pe.transpose(PS[:, t % 2, k * P:(k + 1) * P], h[:, k * P:(k + 1) * P], ident)
                ins.then_inc(tr_done.sem, 1)

            def project(L, b):
                use = ("A", L, b)
                w_ready.wait(pe, L)
                for s in range(TB + 3):
                    if s < TB:
                        normalised_transposes(use, s, HR[s % 2])
                    if 0 <= s - 1 < TB:
                        t = s - 1
                        ht_lo.wait(pe, (use, t))
                        if t >= 2:
                            q_ready.wait(pe, (L, b, t - 2))
                            v_ready.wait(pe, (L, b, t - 2))
                        qk, v = PS[:, 2 + t % 2, :], PS[:, 4 + t % 2, 0:D]
                        for dst, c0, c1 in ((qk, 0, 2 * D), (v, 2 * D, 3 * D)):
                            if L == 0:
                                exact(dst, [(BE[:, :], BZ[:, c0:c1])], last=False)
                            ins = exact(dst, [(a[:, t % 2, k, :], w[:, k, c0:c1]) for k in range(KC)
                                              for a, w in ((HTH, WH), (HTH, WL), (HTL, WH))], first=L == 1)
                        ins.then_inc(qkv_done.sem, 1)
                    if 0 <= s - 3 < TB:
                        t = s - 3
                        stage_lo.wait(pe, (L, b, t))
                        for n, (what, src) in enumerate((("q", QS), ("k", KS))):
                            for h in range(2):
                                if what == "k":
                                    stk_q.wait(pe, (L, b, t, h))
                                elif t:
                                    stk_k.wait(pe, (L, b, t - 1, h))
                                for a in range(4):
                                    pair = 4 * h + a
                                    ins = pe.transpose(PS[:, 6 + h, a * P:(a + 1) * P],
                                                       src[t % 2][:, 2 * pair:2 * pair + 2, :].rearrange("p h c -> p (h c)"),
                                                       ident)
                                ins.then_inc(stk_tr.sem, 1)
                stk_k.wait(pe, (L, b, TB - 1, 1))
                stk_q.wait(pe, (L, b, TB - 1, 1))

            def ring_free(n):
                if n >= 2:
                    ring_read[n - 2][0].wait(pe, ring_read[n - 2][1])

            def attend(L, b):
                for st in STEPS[L]:
                    key = (L, b) + st
                    if st[0] == "max":
                        _, g, i, j = st
                        pair, keys = 2 * g + j // 2, K[j % 2]
                        for c, (c0, w) in enumerate(max_chunks(i)):
                            n = ring[key + (c,)]
                            ring_free(n)
                            last = c0 + w == (i + 1) * P
                            ins = pe.matmul(PS[:, 6 + n % 2, 0:w], Q[:, pair, i * P:(i + 1) * P], keys[:, pair, c0:c0 + w],
                                            start=True, stop=not last, skip_group_check=True)
                            if last:
                                ins = pe.matmul(PS[:, 6 + n % 2, w - P:w], IDB[:, :], MQB[:, :], start=False, stop=True,
                                                skip_group_check=True)
                            ins.then_inc(max_mm.sem, 1)
                    elif st[0] == "ms":
                        n = ring[key]
                        ms_ready.wait(pe, key)
                        ring_free(n)
                        pe.transpose(PS[0:64, 6 + n % 2, 0:P], MS[:, :, :, :].rearrange("p j h i -> p (j h i)"),
                                     ident).then_inc(ms_tr.sem, 1)
                    elif st[0] == "st":
                        _, g, k, j = st
                        n = st_index(L, b, st)
                        if k == 0 and j == 0 and L == 0:
                            m_rows.wait(pe, (L, b, "ms", g))
                        prev = n - (L * B + b) * NQ * TB * 4 - 2
                        if prev >= 0:
                            old = ("st", prev // 32, prev // 4 % 8, prev % 4)
                            (p_dve if L == 1 and old[3] == 3 else p_act).wait(pe, (L, b) + old)
                        pair, keys = 2 * g + j // 2, K[j % 2]
                        mask_bank = 0 if k < 4 else 1
                        for c in range(2):
                            lo, hi = max(k * P, 512 * c), 512 * (c + 1)
                            if lo >= hi:
                                continue
                            bank = 2 * (n % 2) + c
                            masked = L == 0 and c == mask_bank
                            ins = pe.matmul(PS[:, bank, lo - 512 * c:512], keys[:, pair, k * P:(k + 1) * P], Q[:, pair, lo:hi],
                                            start=True, stop=not masked, skip_group_check=True)
                            if masked:
                                ins = pe.matmul(PS[:, bank, lo - 512 * c:lo - 512 * c + P], IDB[:, :], MKB[:, :],
                                                start=False, stop=True, skip_group_check=True)
                        ins.then_inc(st_done.sem, 1)
                    elif st[0] == "pv":
                        _, g, k = st
                        (p_mask if L else p_act).wait(pe, (L, b, "st", g, k, 3))
                        if k == 0 and g:
                            o_evac.wait(pe, (L, b, "pv", g - 1, TB - 1))
                        for c in range(2):
                            lo, hi = max(k * P, 512 * c), 512 * (c + 1)
                            if lo >= hi:
                                continue
                            for j in range(4):
                                ins = pe.matmul(PS[32 * j:32 * j + HD + 1, 4 + c, lo - 512 * c:512], V[:, k, 4 * g + j, :],
                                                PR[:, k % 2, j, lo:hi], start=k == 0, stop=k == 4 * c + 3,
                                                skip_group_check=True)
                        ins.then_inc(pv_done.sem, 1)
                    elif st[0] == "otr":
                        _, g, half = st
                        n = ring[key]
                        ring_free(n)
                        o_evac.wait(pe, (L, b, "pv", g, TB - 1))
                        for a in range(4):
                            t = 4 * half + a
                            ins = pe.transpose(PS[:, 6 + n % 2, a * P:(a + 1) * P], OT[:, t * P:(t + 1) * P], ident)
                        ins.then_inc(o_tr.sem, 1)
                on_ready.wait(pe, (L, b, "otr", NQ - 1, 1))
                for t in range(TB + 1):
                    if t < TB:
                        n = ring[(L, b, "ont", t)]
                        ring_free(n)
                        for k in range(KC):
                            ins = pe.transpose(PS[:, 6 + n % 2, k * P:(k + 1) * P], ON[:, t, k * P:(k + 1) * P], ident)
                        ins.then_inc(on_tr.sem, 1)
                    if t:
                        ont.wait(pe, (L, b, t - 1))
                        if t >= 3:
                            x_new.wait(pe, ("A", L, b, t - 3))
                        dst = PS[:, (t - 1) % 2, 0:D]
                        if L == 0:
                            exact(dst, [(BE[:, :], BOZ[:, :])], last=False)
                        exact(dst, [(a[:, (t - 1) % 2, k, :], w[:, k, :]) for k in range(KC)
                                    for a, w in ((HTH, WOH), (HTH, WOL), (HTL, WOH))], first=L == 1).then_inc(pr_done.sem, 1)

            pe.wait_ge(cvt, 7)
            pe.wait_ge(psum_zero, 1)
            modulation(0)
            for L, b in UNITS[:2]:
                mod_ready.wait(pe, (0, 1))
                project(L, b)
                attend(L, b)

            x_new.wait(pe, ("A", 0, 1, TB - 1))
            modulation(1)
            pe.wait_ge(wg_load, 16)
            for s in range(T + 1):
                if s < T:
                    normalised_transposes(("F", 0), s, HF[:, s, :])
                if s:
                    t = s - 1
                    ht_hi.wait(pe, (("F", 0), t))
                    for k in range(KC):
                        ins = pe.matmul(PS[:, 2, t * E0:(t + 1) * E0], HG[:, t % 2, k, :], WG[:, k, :],
                                        start=k == 0, stop=k == KC - 1)
                    ins.then_inc(lg_mm, 1)
            pe.wait_ge(route_in, 1)
            chosen = MM[:, :, :].rearrange("p t e -> p (t e)")
            pe.matmul(PS[:, 3, 0:P], CST[:, C_TRI:C_TRI + P], chosen, start=True, stop=True)
            pe.matmul(PS[:, 3, P:2 * P], CST[:, C_ONE:C_ONE + P], chosen, start=True, stop=True).then_inc(route_mm, 1)

            def slot_transposes(par, pair):
                pe.wait_ge(xs_load[par], pair * 16 + 16)
                for k in range(KC):
                    for a in range(2):
                        ins = pe.transpose(PS[:, 6, k * SLOT + a * P:k * SLOT + (a + 1) * P], XT[:, par, a, k * P:(k + 1) * P], ident)
                ins.then_inc(xs_tr, 1)

            def slot_up(s, par, c):
                if c == 0:
                    pe.wait_ge(xs_lo, s + 1)
                if c >= 4:
                    pe.wait_ge(up_gate, s * HC + (c - 3))
                for n in range(2):
                    if c == 0:
                        pe.wait_ge(ws_lo[n], s + 1)
                    cols = slice(c * P, (c + 1) * P)
                    ins = exact(PS[:, c % 4, n * SLOT:(n + 1) * SLOT],
                                [(w[:, par, n, k, cols], r[:, par, k, :]) for k in range(KC)
                                 for w, r in ((H13, XTH), (H13, XTL), (L13, XTH))])
                ins.then_inc(up_mm, 1)

            def slot_down(s, par):
                pe.wait_ge(y_evac, s + 1)
                pe.wait_ge(ws_lo[2], s + 1)
                for c in range(HC):
                    pe.wait_ge(up_lo, s * HC + (c + 1))
                    for a in range(2):
                        cols = slice(a * P, (a + 1) * P)
                        ins = exact(PS[:, 4 + a, 0:D], [(HH[:, c, cols], H2[:, par, c, :]), (HH[:, c, cols], L2[:, par, c, :]),
                                                        (HL[:, c, cols], H2[:, par, c, :])], first=c == 0, last=c == HC - 1)
                ins.then_inc(dn_mm, 1)

            slot_transposes(0, 0)
            with pe.Fori(0, (SLOTS - 1) // 2, 1) as i:
                for par in range(2):
                    s = i * 2 + par
                    for c in range(HC):
                        slot_up(s, par, c)
                        if c == 3:
                            slot_transposes((par + 1) % 2, i + par)
                    slot_down(s, par)
            for c in range(HC):
                slot_up(SLOTS - 1, 0, c)
            slot_down(SLOTS - 1, 0)

            x_new.wait(pe, ("F", 0, T - 1))
            modulation(2)
            for L, b in UNITS[2:]:
                mod_ready.wait(pe, (2, 1))
                project(L, b)
                attend(L, b)

            x_new.wait(pe, ("A", 1, 1, TB - 1))
            modulation(3)
            for t in range(T):
                normalised_transposes(("F", 1), t, HR1[:, t % 2, :])
            pe.wait_ge(gw_lo, 1)
            for l in range(L1N):
                for c in range(4):
                    last = 4 * c + 3
                    (ln_lo.wait(pe, (l - 1, last)) if l else ht_lo.wait(pe, (("F", 1), last)))
                    cols = slice(c * 512, (c + 1) * 512)
                    exact(PS[:, 2 + c, :], [(g[:, l, k, :], r[:, k, cols]) for k in range(KC)
                                            for g, r in ((GWH, XH), (GWH, XL), (GWL, XH))]).then_inc(gt_mm.sem, 1)
                gt_evac.wait(pe, (l, 3))
                for t in range(T):
                    ins = pe.transpose(PS[:, 6, t * E1:(t + 1) * E1], LT[:, t * P:(t + 1) * P], CST[0:E1, C_ID:C_ID + E1])
                ins.then_inc(gt_tr.sem, 1)
                with pe.Fori(0, PAIRS // 2, 1) as i:
                    for par in range(2):
                        n = i * 2 + (l * PAIRS + par)
                        pe.wait_ge(er_lo, n + 1)
                        for t in range(T):
                            pe.wait_ge(ev_b, n * T + (t + T - 3))
                            cols = slice(t * P, (t + 1) * P)
                            exact(PS[:, 2 + t % 4, :], [(r[:, k, cols], w[:, par, k, :, :].rearrange("p e m -> p (e m)"))
                                                        for k in range(KC) for r, w in ((XH, EH), (XH, EL), (XL, EH))]
                                  ).then_inc(ex_mm, 1)
                for t in range(T if l < L1N - 1 else 0):
                    pe.wait_ge(ev_b, ((l + 1) * PAIRS - 1) * T + T + t + 1)
                    if t >= 2:
                        ln_lo.wait(pe, (l, t - 2))
                    for k in range(KC):
                        ins = pe.transpose(PS[:, t % 2, k * P:(k + 1) * P], AC[:, l % 2, t, k * P:(k + 1) * P], ident)
                    ins.then_inc(ln_tr.sem, 1)


def constant_table():
    import numpy as np

    c = np.zeros((P, C_W), np.float32)
    r, k = np.arange(P)[:, None], np.arange(P)[None, :]
    c[:, C_ID:C_ID + P] = r == k
    c[:, C_TRI:C_TRI + P] = r < k
    c[:, C_ONE:C_ONE + P] = 1.0
    inv = np.float32(1.0) / np.float32(10000.0) ** (np.arange(HD // 2, dtype=np.float32) / np.float32(HD // 2))
    angle = np.arange(S, dtype=np.float32)[:, None] * inv[None, :].astype(np.float32)
    cos = np.repeat(np.cos(angle), 2, axis=-1).astype(np.float32)
    sin = np.repeat(np.sin(angle), 2, axis=-1).astype(np.float32)
    sin[:, 0::2] *= -1
    c[:, C_COS:C_COS + TB * HD] = cos.reshape(TB, P, HD).transpose(1, 0, 2).reshape(P, -1)
    c[:, C_SIN:C_SIN + TB * HD] = sin.reshape(TB, P, HD).transpose(1, 0, 2).reshape(P, -1)
    c[:, C_THR:C_THR + 8] = SLOT * np.arange(8)
    c[:, C_SLOT:C_SLOT + 24] = np.arange(24)
    c[1, C_SC] = -1.0
    c[0:2, C_BE:C_BE + P] = 1.0
    c[:, C_MQ:C_MQ + P] = np.where(k > r, -1e30, 0.0)
    c[:, C_MK:C_MK + P] = np.where(r > k, -1e30, 0.0)
    return c


def kernel(**inputs):
    import numpy as _np
    import concourse.bacc as _bacc
    from concourse import mybir as _mybir
    from concourse.bass_utils import run_bass_kernel_spmd as _run

    g = {k: _np.asarray(v) for k, v in inputs.items()}
    gates = _np.zeros((L1N, D, P), _np.float32)
    gates[:, :, 0:E1] = g["L1_ffn_gate_w"].transpose(0, 2, 1)
    a = {
        "x": g["L0_attn_x"].reshape(T * P, D),
        "cT0": g["L0_c"].T,
        "wmod0": g["L0_wmod"],
        "wqkv0": _np.concatenate([g["L0_attn_Wq"].T, g["L0_attn_Wk"].T, g["L0_attn_Wv"].T], axis=1),
        "bqkv0": _np.tile(_np.concatenate([g["L0_attn_bq"], g["L0_attn_bk"], g["L0_attn_bv"]])[None], (2, 1)),
        "wo0": g["L0_attn_Wo"].T,
        "bo0": _np.tile(g["L0_attn_bo"][None], (2, 1)),
        "wg": g["L0_ffn_Wg"],
        "w1": g["L0_ffn_w1"],
        "w3": g["L0_ffn_w3"],
        "w2": g["L0_ffn_w2"],
        "cT1": g["L1_c"].T,
        "wmod1": g["L1_wmod"],
        "wqkv1": _np.concatenate([g["L1_attn_Wq"].T, g["L1_attn_Wk"].T, g["L1_attn_Wv"].T], axis=1),
        "wo1": g["L1_attn_Wo"].T,
        "gamma": _np.tile(g["L1_attn_gamma"][None], (P, 1)),
        "beta": _np.tile(g["L1_attn_beta"][None], (P, 1)),
        "gw1": gates,
        "ew1": g["L1_ffn_expert_w"].transpose(0, 1, 3, 2).reshape(L1N * E1 * D, D),
        "consts": constant_table(),
    }
    nc = _bacc.Bacc("TRN2", target_bir_lowering=False, num_devices=1)
    arrays = {f"in_{k}": _np.ascontiguousarray(v) for k, v in a.items()}
    args = [nc.dram_tensor(k, v.shape, _mybir.dt.from_np(v.dtype), kind="ExternalInput").ap() for k, v in arrays.items()]
    out = nc.dram_tensor("out_x", (T * P, D), F32, kind="ExternalOutput").ap()
    adaln_kernel(nc, *args, out)
    r = _run(nc, [arrays], core_ids=[0])
    return r.results[0]["out_x"].reshape(B, S, D)
```

```python
from contextlib import ExitStack

import concourse.bass as bass
from concourse import mybir

F32 = mybir.dt.float32
F32R = mybir.dt.float32r
BF16 = mybir.dt.bfloat16
U32 = mybir.dt.uint32
I32 = mybir.dt.int32
ALU = mybir.AluOpType
ACT = mybir.ActivationFunctionType
AX_X = mybir.AxisListType.X

P = 128
D = 256
KC = D // P
B = 2
S = 1024
TB = S // P
T = B * TB
HN = 16
HD = D // HN
NQ = 4
E0 = 8
HID = 896
HC = HID // P
SLOT = 256
SLOTS = (T * P * 2 + E0 * (SLOT - 1)) // SLOT
E1 = 16
L1N = 4
PAIRS = E1 // 2
STK = 64
MH, ML = 48, 49
BIG = 3.0e38
LN_EPS = 1e-5
Z_EPS = 1e-5

C_ID, C_TRI, C_ONE, C_COS, C_SIN = 0, 128, 256, 384, 512
C_THR, C_SLOT, C_SC, C_BE, C_MQ, C_MK, C_W = 640, 648, 672, 673, 801, 929, 1057


class Tally:

    def __init__(self, sem):
        self.sem, self.n, self.at = sem, 0, {}

    def plan(self, label, k=1):
        self.n += k
        self.at[label] = self.n

    def wait(self, eng, label):
        eng.wait_ge(self.sem, self.at[label])


def adaln_kernel(nc, x, cT0, wmod0, wqkv0, bqkv0, wo0, bo0, wg, w1, w3, w2,
                 cT1, wmod1, wqkv1, wo1, gamma, beta, gw1, ew1, consts, out):
    ctx = ExitStack()
    with ctx:
        def sem(name):
            return ctx.enter_context(nc.semaphore(name))

        def tally(name):
            return Tally(sem(name))

        def sb(name, shape, dt, scope=ctx):
            return scope.enter_context(nc.sbuf_tensor(name, shape, dt))

        PS = ctx.enter_context(nc.psum_tensor("PS", [P, 8, 512], F32))

        slot_in = nc.dram_tensor("slot_in", [SLOTS * SLOT, D], F32, kind="Internal").ap()
        slot_out = nc.dram_tensor("slot_out", [SLOTS * SLOT, D], F32, kind="Internal").ap()
        max_rows = nc.dram_tensor("max_rows", [B * NQ, 64, P], F32, kind="Internal").ap()

        X = sb("X", [P, T, D], F32)
        CST = sb("CST", [P, C_W], F32)
        IDB = sb("IDB", [P, P], BF16)
        MQB = sb("MQB", [P, P], BF16)
        MKB = sb("MKB", [P, P], BF16)
        BE = sb("BE", [P, P], F32R)
        CS = sb("CS", [P, 2, KC, B], F32)
        CB = sb("CB", [P, KC, B, P], F32)
        MOD = sb("MOD", [P, B, 3 * D], F32)
        STAT = sb("STAT", [P, T, 6], F32)
        MV = sb("MV", [P, T, 2], F32)
        SM = sb("SM", [P, 6, T], F32)
        GT2 = sb("GT2", [P, 2, D], F32)
        ident = CST[:, C_ID:C_ID + P]

        sa = ExitStack()
        Q = sb("Q", [P, HN // 2, S], F32R, sa)
        K = [sb("KA", [P, HN // 2, S], F32R, sa), sb("KB", [P, HN // 2, S], F32R, sa)]
        V = sb("V", [P, TB, HN, HD + 1], F32, sa)
        PR = sb("PR", [P, 2, 4, S], F32, sa)
        HTH = sb("HTH", [P, 2, KC, P], F32R, sa)
        HTL = sb("HTL", [P, 2, KC, P], F32R, sa)
        WH = sb("WH", [P, KC, 3 * D], F32R, sa)
        WL = sb("WL", [P, KC, 3 * D], F32R, sa)
        WOH = sb("WOH", [P, KC, D], F32R, sa)
        WOL = sb("WOL", [P, KC, D], F32R, sa)
        BZ = sb("BZ", [P, 3 * D], F32R, sa)
        BOZ = sb("BOZ", [P, D], F32R, sa)
        OT = sb("OT", [P, S], F32, sa)
        ON = sb("ON", [P, TB, D], F32, sa)
        GB = sb("GB", [P, 2, HD], F32, sa)
        MP = sb("MP", [P, 4, TB, 2], F32, sa)
        MX = sb("MX", [P, 2, 4, TB], F32, sa)
        MS = sb("MS", [P, 4, 2, TB], F32, sa)
        MT = sb("MT", [64, P], F32, sa)
        RC = sb("RC", [P, 2, 16], F32, sa)
        sa.close()
        flat = PR[:, :, :, :].rearrange("p a b c -> p (a b c)")
        QS = [flat[:, g * 2048:g * 2048 + 1024].rearrange("p (h c) -> p h c", h=HN) for g in range(2)]
        KS = [flat[:, g * 2048 + 1024:g * 2048 + 2048].rearrange("p (h c) -> p h c", h=HN) for g in range(2)]
        TA = flat[:, 4096:4608]
        TB_ = flat[:, 4608:5120]
        SQ = [TA, TB_]
        TQ = [flat[:, 5120 + 512 * g:5632 + 512 * g] for g in range(2)]
        HR = [flat[:, 6144 + 256 * g:6400 + 256 * g] for g in range(2)]
        FS = flat[:, 6656:6912].rearrange("p (a b) -> p a b", b=32)
        wraw = flat[:, 0:1536].rearrange("p (k n) -> p k n", k=KC)
        woraw = flat[:, 1536:2048].rearrange("p (k n) -> p k n", k=KC)
        wmraw = flat[:, 2048:3584].rearrange("p (k n) -> p k n", k=KC)
        braw = flat[:, 3584:4352]
        boraw = flat[:, 4352:4608]

        zero_rows = OT[:, 0:2 * D]

        sf = ExitStack()
        HF = sb("HF", [P, T, D], F32, sf)
        WM0 = sb("WM0", [P, KC, 3 * D], F32, sf)
        HG = sb("HG", [P, 2, KC, P], F32, sf)
        WG = sb("WG", [P, KC, E0], F32, sf)
        LG = sb("LG", [P, T, 2 * E0], F32, sf)
        T8 = sb("T8", [P, T, 8], F32, sf)
        R2 = sb("R2", [P, T, 8], F32, sf)
        R1 = sb("R1", [P, T, 8], F32, sf)
        RP = sb("RP", [P, T, 2 * E0], F32, sf)
        RP1 = sb("RP1", [P, T, 2 * E0], F32, sf)
        MM = sb("MM", [P, T, E0], F32, sf)
        A0 = sb("A0", [P, T, E0], F32, sf)
        A1 = sb("A1", [P, T, E0], F32, sf)
        W01 = sb("W01", [P, 2, T], F32, sf)
        WT = sb("WT", [P, 2, T], F32, sf)
        WIN = sb("WIN", [P, T, E0], F32, sf)
        TOT = sb("TOT", [P, T, E0], F32, sf)
        PRE = sb("PRE", [P, T + 1, E0], F32, sf)
        CMP = sb("CMP", [P, E0, 8], F32, sf)
        NT = sb("NT", [P, E0], F32, sf)
        OF = sb("OF", [P, E0 + 1], F32, sf)
        POS = sb("POS", [P, T, E0], F32, sf)
        PA = sb("PA", [P, 2, T, E0], F32, sf)
        PF = sb("PF", [P, 2, T], F32, sf)
        IX = sb("IX", [P, 2, T], U32, sf)
        SE = sb("SE", [P, 24, E0], F32, sf)
        EF = sb("EF", [P, 24], F32, sf)
        EI = sb("EI", [P, 24], I32, sf)
        XT = sb("XT", [P, 2, 2, D], F32, sf)
        XTH = sb("XTH", [P, 2, KC, SLOT], F32R, sf)
        XTL = sb("XTL", [P, 2, KC, SLOT], F32R, sf)
        R13 = sb("R13", [P, 2, KC, HID], F32, sf)
        RW2 = sb("RW2", [P, HC, D], F32, sf)
        H13 = sb("H13", [P, 2, 2, KC, HID], F32R, sf)
        L13 = sb("L13", [P, 2, 2, KC, HID], F32R, sf)
        H2 = sb("H2", [P, 2, HC, D], F32R, sf)
        L2 = sb("L2", [P, 2, HC, D], F32R, sf)
        SI = sb("SI", [P, 2, SLOT], F32, sf)
        GG = sb("GG", [P, 3, SLOT], F32, sf)
        HH = sb("HH", [P, HC, SLOT], F32R, sf)
        HL = sb("HL", [P, HC, SLOT], F32R, sf)
        YO = sb("YO", [P, 2, 2, D], F32, sf)
        sf.close()
        G0 = R13[:, 0, :, :].rearrange("p k n -> p (k n)")[:, 0:4 * D].rearrange("p (a c d) -> p a c d", a=2, c=2)
        GT = R13[:, 1, :, :].rearrange("p k n -> p (k n)")[:, 0:2 * D].rearrange("p (a d) -> p a d", a=2)

        def split_steps(n, par):
            if n < 2:
                return [(R13[:, n, k, :], H13[:, par, n, k, :], L13[:, par, n, k, :]) for k in range(KC)]
            return [(RW2[:, a:b, :], H2[:, par, a:b, :], L2[:, par, a:b, :]) for a, b in ((0, HC // 2), (HC // 2, HC))]

        sg = ExitStack()
        WM1 = sb("WM1", [P, KC, 3 * D], F32, sg)
        HR1 = sb("HR1", [P, 2, D], F32, sg)
        XH = sb("XH", [P, KC, T * P], F32R, sg)
        XL = sb("XL", [P, KC, T * P], F32R, sg)
        AC = sb("AC", [P, 2, T, D], F32, sg)
        GR = sb("GR", [P, L1N, KC, P], F32, sg)
        GWH = sb("GWH", [P, L1N, KC, P], F32R, sg)
        GWL = sb("GWL", [P, L1N, KC, P], F32R, sg)
        LT = sb("LT", [E1, T * P], F32, sg)
        LGT = sb("LGT", [P, T, E1], F32, sg)
        M8 = sb("M8", [P, T, 8], F32, sg)
        RPL = sb("RPL", [P, T, E1], F32, sg)
        EX = sb("EX", [P, T, E1], F32, sg)
        SU = sb("SU", [P, 2, T], F32, sg)
        MK = sb("MK", [P, T, E1], F32, sg)
        WD = sb("WD", [P, 2, T, E1], F32, sg)
        WP = sb("WP", [P, 2, T, 2], F32, sg)
        ER = sb("ER", [P, 2, KC, 2, D], F32, sg)
        EH = sb("EH", [P, 2, KC, 2, D], F32R, sg)
        EL = sb("EL", [P, 2, KC, 2, D], F32R, sg)
        OUT_T = sb("OUT_T", [P, 2, D], F32, sg)
        sg.close()

        USES = [("A", 0, 0), ("A", 0, 1), ("F", 0), ("A", 1, 0), ("A", 1, 1), ("F", 1)]
        UNITS = [(L, b) for L in range(2) for b in range(B)]

        loaded = sem("loaded")
        cvt = sem("cvt")
        psum_zero = sem("psum_zero")
        chain = sem("chain")
        pool_chain = sem("pool_chain")
        stats_ready = tally("stats_ready")
        silu_c = sem("silu_c")
        cb_ready = sem("cb_ready")
        mod_w = tally("mod_w")
        mod_mm = tally("mod_mm")
        mod_ready = tally("mod_ready")
        w_load = tally("w_load")
        w_folded = sem("w_folded")
        w_hi = tally("w_hi")
        w_ready = tally("w_ready")
        sq_in = tally("sq_in")
        sq_out = tally("sq_out")
        fm_sq = tally("fm_sq")
        fm_in = tally("fm_in")
        fm_out = tally("fm_out")
        h_ready = tally("h_ready")
        tr_done = tally("tr_done")
        ht_hi = tally("ht_hi")
        ht_lo = tally("ht_lo")
        qkv_done = tally("qkv_done")
        q_ready = tally("q_ready")
        v_ready = tally("v_ready")
        stage_init = tally("stage_init")
        stage_hi = tally("stage_hi")
        stage_lo = tally("stage_lo")
        stk_tr = tally("stk_tr")
        stk_q = tally("stk_q")
        stk_ka = tally("stk_ka")
        stk_kb = tally("stk_kb")
        max_mm = tally("max_mm")
        max_red = tally("max_red")
        ms_ready = tally("ms_ready")
        ms_tr = tally("ms_tr")
        mt_ready = tally("mt_ready")
        m_out = tally("m_out")
        m_rows = tally("m_rows")
        st_done = tally("st_done")
        p_act = tally("p_act")
        p_dve = tally("p_dve")
        p_mask = tally("p_mask")
        pv_done = tally("pv_done")
        o_evac = tally("o_evac")
        o_tr = tally("o_tr")
        on_ready = tally("on_ready")
        on_tr = tally("on_tr")
        ont = tally("ont")
        pr_done = tally("pr_done")
        x_new = tally("x_new")
        wg_load = sem("wg_load")
        lg_mm = sem("lg_mm")
        gate_in = sem("gate_in")
        gate_exp = sem("gate_exp")
        route_in = sem("route_in")
        route_mm = sem("route_mm")
        zero_t = sem("zero_t")
        zeroed = sem("zeroed")
        idx_ready = sem("idx_ready")
        scattered = sem("scattered")
        xs_load = [sem(f"xs_load{n}") for n in range(2)]
        wr_load = [sem(f"wr_load{n}") for n in range(3)]
        xs_tr = sem("xs_tr")
        xs_hi = sem("xs_hi")
        xs_lo = sem("xs_lo")
        ws_hi = [sem(f"ws_hi{n}") for n in range(3)]
        ws_lo = [sem(f"ws_lo{n}") for n in range(3)]
        up_mm = sem("up_mm")
        up_silu = sem("up_silu")
        up_gate = sem("up_gate")
        up_hi = sem("up_hi")
        up_lo = sem("up_lo")
        dn_mm = sem("dn_mm")
        y_evac = sem("y_evac")
        y_out = [sem(f"y_out{n}") for n in range(2)]
        gathered = [sem(f"gathered{n}") for n in range(2)]
        g_used = sem("g_used")
        gw_load = sem("gw_load")
        gw_hi = sem("gw_hi")
        gw_lo = sem("gw_lo")
        gt_mm = tally("gt_mm")
        gt_evac = tally("gt_evac")
        gt_tr = tally("gt_tr")
        gt_read = tally("gt_read")
        gt_max = tally("gt_max")
        gt_exp = tally("gt_exp")
        acc_zero = sem("acc_zero")
        er_load = [sem("er_load0"), sem("er_load1")]
        er_hi = sem("er_hi")
        er_lo = sem("er_lo")
        ex_mm = sem("ex_mm")
        wp_ready = sem("wp_ready")
        ev_a = sem("ev_a")
        ev_b = sem("ev_b")
        ln_tr = tally("ln_tr")
        ln_hi = tally("ln_hi")
        ln_lo = tally("ln_lo")
        o_ready = sem("o_ready")
        stored = [sem(f"stored{n}") for n in range(2)]

        for n in range(4):
            mod_w.plan(n, 16)
            mod_mm.plan(n, B)
            for b in range(B):
                mod_ready.plan((n, b), 3)
        for L in range(2):
            w_load.plan(L, 16 * 4)
            w_hi.plan(L, 4 if L == 0 else 3)
            w_ready.plan(L, 4 if L == 0 else 3)
        for u in USES:
            if u[2:] != (1,):
                for what in (sq_in, sq_out, stats_ready):
                    what.plan(u[:2])
            for t in range(T if u[0] == "F" else TB):
                h_ready.plan((u, t))
                tr_done.plan((u, t))
                ht_hi.plan((u, t))
                if u != ("F", 0):
                    ht_lo.plan((u, t))
        for L, b in UNITS:
            for what in () if b else ("ones", "KA", "KB"):
                stage_init.plan((L, what))
            stage_init.plan((L, b), 6)
            for t in range(TB):
                qkv_done.plan((L, b, t))
                q_ready.plan((L, b, t))
                v_ready.plan((L, b, t))
                if L == 1:
                    fm_sq.plan((b, t))
                    fm_in.plan((b, t))
                    fm_out.plan((b, t))
                stage_hi.plan((L, b, t), 2)
                stage_lo.plan((L, b, t), 2)
                for what in ("q", "k"):
                    for h in range(2):
                        stk_tr.plan((L, b, t, what, h))
                for h in range(2):
                    stk_q.plan((L, b, t, h))
                    stk_ka.plan((L, b, t, h))
                    stk_kb.plan((L, b, t, h))

        def max_chunks(i):
            w = (i + 1) * P
            if w <= 512:
                return [(0, w)]
            return [(0, 384), (384, 256)] if w == 640 else [(0, 512), (512, w - 512)]

        COVER, SPREAD, ROWS_AT, PV_LAG = 8, 22, 24, (2, 3)

        def steps(L):
            order = [(i, j) for j in range(4) for i in (0, 7, 1, 6, 2, 5, 3, 4)]
            maxes = [[("max", g, i, j) for i, j in order] if L == 0 else [] for g in range(NQ)] + [[]]
            seq = []
            if L == 0:
                seq += maxes[0] + [("msc", 0)] + maxes[1][:3] + [("ms", 0)] + maxes[1][3:COVER]
                maxes[1] = maxes[1][COVER:]
            for g in range(NQ):
                todo = maxes[g + 1]
                count = len(todo)
                for n in range(TB * 4):
                    k, j = n // 4, n % 4
                    seq.append(("st", g, k, j))
                    if j == PV_LAG[L] and (g or k):
                        seq.append(("pv", g, k - 1) if k else ("pv", g - 1, TB - 1))
                    while count - len(todo) < min(count, -(-count * (n + 1) // SPREAD)):
                        seq.append(todo.pop(0))
                        if not todo:
                            seq.append(("msc", g + 1))
                    if n == ROWS_AT and count:
                        seq.append(("ms", g + 1))
                    if g and k == 2 and j == 1:
                        seq += [("otr", g - 1, 0), ("otr", g - 1, 1)]
            return seq + [("pv", NQ - 1, TB - 1), ("otr", NQ - 1, 0), ("otr", NQ - 1, 1)]

        STEPS = {L: steps(L) for L in range(2)}

        def on_vector(L, st):
            return L == 1 and (st[3] == 3 or (st[3] == 1 and st[2] % 4 == 1))

        bank, bank_free, last_reader = {}, {}, {}

        def take(key, banks, reader, label):
            bank[key] = banks[0]
            waits = []
            for k in banks:
                if k in last_reader and last_reader[k] not in waits:
                    waits.append(last_reader[k])
                last_reader[k] = (reader, label)
            bank_free[key] = waits

        for L, b in UNITS:
            last_reader.clear()
            rows_out = pairs_out = 0
            scores_begun = L == 1
            for st in STEPS[L]:
                key = (L, b) + st
                scores_begun = scores_begun or st[0] == "st"
                narrow = (6, 7) if scores_begun else (6, 7, 0, 1, 2, 3)
                wide = ((0, 1), (2, 3)) if L == 0 else ((0, 1), (2, 3), (6, 7))
                if st[0] == "max":
                    for c in range(len(max_chunks(st[2]))):
                        max_mm.plan(key + (c,))
                        max_red.plan(key + (c,))
                        take(key + (c,), (narrow[rows_out % len(narrow)],), max_red, key + (c,))
                        rows_out += 1
                elif st[0] == "msc":
                    ms_ready.plan((L, b, "ms", st[1]))
                elif st[0] == "ms":
                    for what in (ms_tr, mt_ready):
                        what.plan(key)
                    m_out.plan(key, 16)
                    m_rows.plan(key, 64)
                    take(key, (narrow[rows_out % len(narrow)],), mt_ready, key)
                    rows_out += 1
                elif st[0] == "st":
                    st_done.plan(key)
                    reader = p_dve if on_vector(L, st) else p_act
                    reader.plan(key)
                    if L == 1:
                        p_mask.plan(key)
                    take(key, wide[pairs_out % len(wide)], reader, key)
                    pairs_out += 1
                elif st[0] == "pv":
                    pv_done.plan(key)
                    if st[2] == TB - 1:
                        o_evac.plan(key)
                elif st[0] == "otr":
                    o_tr.plan(key)
                    on_ready.plan(key)
                    take(key, (6 + st[2],), on_ready, key)
            for t in range(TB):
                on_tr.plan((L, b, t))
                ont.plan((L, b, t))
                take((L, b, "ont", t), (6 + t % 2,), ont, (L, b, t))
                pr_done.plan((L, b, t))
                x_new.plan(("A", L, b, t))
            if (L, b) == (0, 1):
                for t in range(T):
                    x_new.plan(("F", 0, t))
        for l in range(L1N):
            for c in range(4):
                for what in (gt_mm, gt_evac, gt_tr, gt_read, gt_max, gt_exp):
                    what.plan((l, c))
            for t in range(T if l < L1N - 1 else 0):
                ln_tr.plan((l, t))
                ln_hi.plan((l, t))
                ln_lo.plan((l, t))

        def between():
            slots = [[] for _ in range(T + 12)]
            for t in range(T):
                slots[t].append(("product", t))
                slots[t].append(("evac0", t))
                slots[t + 1].append(("evac1", t))
                slots[t + 2] += [("transpose", t), ("hi", t)]
                slots[t + 3].append(("lo", t))
            for c in range(4):
                at = 4 * c + 6
                slots[at + 1] += [("gate", c), ("evac", c)]
                slots[at + 2] += [("gate_rows", c), ("top", c), ("exp", c)]
                slots[at + 3].append(("weights", c))
            return [x for slot in slots for x in slot]

        def run_between(l, do):
            for what, x in between():
                if l is None and what in ("product", "evac0", "evac1"):
                    continue
                do(what, x)

        def normalised(eng, use, t, h, steps_done):
            t0 = 0 if use[0] == "F" else use[2] * TB
            b = (t0 + t) // TB
            if t >= 2 and use != ("F", 0):
                tr_done.wait(eng, (use, t - 2))
            steps_done(eng.tensor_scalar(h, X[:, t0 + t, :], SM[:, 2, t0 + t:t0 + t + 1], SM[:, 4, t0 + t:t0 + t + 1], ALU.mult, ALU.add))
            steps_done(eng.tensor_tensor(h, h, MOD[:, b, D:2 * D], ALU.mult))
            eng.tensor_tensor(h, h, MOD[:, b, 0:D], ALU.add).then_inc(h_ready.sem, 1)

        class Links:

            def __init__(self, eng, sem_):
                self.eng, self.sem, self.n = eng, sem_, 0

            def __call__(self, ins):
                self.n += 1
                ins.then_inc(self.sem, 1)
                self.eng.wait_ge(self.sem, self.n)

        block = ctx.enter_context(nc.Block())

        @block.sync
        def _(sp):
            for par in range(2):
                sp.sem_inc(y_out[par], 16)
            sp.dma_start(CST[:, :], consts).then_inc(loaded, 16)
            sp.dma_start(CS[:, 0, :, :], cT0.rearrange("(k p) b -> p k b", p=P)).then_inc(loaded, 16)
            sp.dma_start(CS[:, 1, :, :], cT1.rearrange("(k p) b -> p k b", p=P)).then_inc(loaded, 16)
            sp.dma_start(X[:, :, :], x.rearrange("(t p) d -> p t d", p=P)).then_inc(loaded, 16)

            def attention_loads(L):
                wm, w, wo = (wmod0, wqkv0, wo0) if L == 0 else (wmod1, wqkv1, wo1)
                sp.dma_start(wmraw, wm[:, 0:3 * D].rearrange("(k p) n -> p k n", p=P)).then_inc(mod_w.sem, 16)
                sp.dma_start(wraw, w.rearrange("(k p) n -> p k n", p=P)).then_inc(w_load.sem, 16)
                sp.dma_start(woraw, wo.rearrange("(k p) n -> p k n", p=P)).then_inc(w_load.sem, 16)
                if L == 0:
                    sp.dma_start(braw[0:2, :], bqkv0).then_inc(w_load.sem, 16)
                    sp.dma_start(boraw[0:2, :], bo0).then_inc(w_load.sem, 16)
                else:
                    sp.dma_start(GB[:, 0, :], gamma).then_inc(w_load.sem, 16)
                    sp.dma_start(GB[:, 1, :], beta).then_inc(w_load.sem, 16)

            attention_loads(0)
            sp.wait_ge(zero_t, 1)
            zrows = slot_in.rearrange("(c p r) d -> c p (r d)", p=P, r=2)
            for c in range(SLOTS):
                sp.dma_start(zrows[c], zero_rows).then_inc(zeroed, 16)
            for b in range(B):
                for st in STEPS[0]:
                    if st[0] != "ms":
                        continue
                    g, key = st[1], (0, b) + st
                    scratch = max_rows[b * NQ + g, :, :]
                    mt_ready.wait(sp, key)
                    sp.dma_start(scratch, MT[:, :]).then_inc(m_out.sem, 16)
                    m_out.wait(sp, key)
                    for j in range(4):
                        row = STK * (j % 2) + MH
                        sp.dma_start(Q[row:row + 2, 2 * g + j // 2, :].bitcast(F32),
                                     scratch[16 * j:16 * j + 16, :].rearrange("(h i) q -> h (i q)", h=2)
                                     ).then_inc(m_rows.sem, 16)

            x_new.wait(sp, ("A", 0, 1, TB - 1))
            sp.dma_start(WM0[:, :, :], wmod0[:, 3 * D:].rearrange("(k p) n -> p k n", p=P)).then_inc(mod_w.sem, 16)
            sp.dma_start(WG[:, :, :], wg.rearrange("(k p) e -> p k e", p=P)).then_inc(wg_load, 16)

            def slot_rows(s, par):
                sp.dma_start(XT[:, par, :, :], slot_in[bass.ds(s * SLOT, SLOT), :]
                             .rearrange("(a p) d -> p a d", p=P)).then_inc(xs_load[par], 16)

            def slot_weights(s, wait):
                e = sp.value_load(EI[0:1, bass.ds(s, 1)], min_val=0, max_val=E0 - 1)
                for n, w in enumerate((w1, w3, w2)):
                    if wait:
                        sp.wait_ge(ws_hi[n], s * 2)
                        sp.wait_ge(ws_lo[n], s * 2)
                    dst = R13[:, n, :, :] if n < 2 else RW2[:, :, :]
                    sp.dma_start(dst, w[bass.ds(e, 1), :, :].rearrange("a (k p) n -> p (a k) n", p=P)
                                 ).then_inc(wr_load[n], 16)

            def slot_store(s, par):
                sp.wait_ge(y_evac, s + 2)
                sp.dma_start(slot_out[bass.ds(s * SLOT, SLOT), :].rearrange("(a p) d -> p a d", p=P),
                             YO[:, par, :, :]).then_inc(y_out[par], 16)

            sp.wait_ge(idx_ready, 3)
            slot_weights(0, False)
            sp.wait_ge(scattered, 16 * 2 * T)
            slot_rows(0, 0)
            slot_rows(1, 1)
            slot_weights(1, True)
            with sp.Fori(0, (SLOTS - 3) // 2, 1) as i:
                for par in range(2):
                    s = i * 2 + par
                    sp.wait_ge(xs_tr, s + 1)
                    slot_rows(s + 2, par)
                    slot_weights(s + 2, True)
                    slot_store(s, par)
            sp.wait_ge(xs_tr, SLOTS - 2)
            slot_rows(SLOTS - 1, (SLOTS - 1) % 2)
            slot_weights(SLOTS - 1, True)
            for s in range(SLOTS - 3, SLOTS):
                slot_store(s, s % 2)

            x_new.wait(sp, ("F", 0, T - 1))
            attention_loads(1)

            x_new.wait(sp, ("A", 1, 1, TB - 1))
            sp.dma_start(WM1[:, :, :], wmod1[:, 3 * D:].rearrange("(k p) n -> p k n", p=P)).then_inc(mod_w.sem, 16)
            for l in range(L1N):
                sp.dma_start(GR[:, l, :, :], gw1[l].rearrange("(k p) e -> p k e", p=P)).then_inc(gw_load, 16)
            ew_pairs = ew1.rearrange("(n e k p) m -> n k p e m", e=2, k=KC, p=P)
            for par in range(2):
                for k in range(KC):
                    sp.dma_start(ER[:, par, k, :, :], ew_pairs[par, k]).then_inc(er_load[par], 16)
            with sp.Fori(0, L1N * PAIRS // 2 - 1, 1) as i:
                for par in range(2):
                    sp.wait_ge(er_lo, i * 2 + (par + 1))
                    for k in range(KC):
                        sp.dma_start(ER[:, par, k, :, :],
                                     ew_pairs[bass.ds(i * 2 + (2 + par), 1), k, :, :, :]
                                     .rearrange("a p e m -> p (a e) m")).then_inc(er_load[par], 16)
            for t in range(T):
                sp.wait_ge(o_ready, t + 1)
                sp.dma_start(out[t * P:(t + 1) * P, :], OUT_T[:, t % 2, :]).then_inc(stored[t % 2], 16)
            for par in range(2):
                sp.wait_ge(stored[par], 16 * T // 2)

        @block.gpsimd
        def _(pool):
            def stage(L, b):
                if b == 0:
                    if L == 1:
                        x_new.wait(pool, ("F", 0, T - 1))
                    pool.memset(V[:, :, :, HD:HD + 1], 1.0).then_inc(stage_init.sem, 1)
                    stage_init.wait(pool, (L, "ones"))
                    pool.memset(K[0][STK:P, :, :].bitcast(F32), 0.0).then_inc(stage_init.sem, 1)
                    stage_init.wait(pool, (L, "KA"))
                    pool.memset(K[1][0:STK, :, :].bitcast(F32), 0.0).then_inc(stage_init.sem, 1)
                    stage_init.wait(pool, (L, "KB"))
                    w_ready.wait(pool, L)
                    mod_mm.wait(pool, 2 * L)
                else:
                    pv_done.wait(pool, (L, 0, "pv", NQ - 1, TB - 1))
                for g in range(2):
                    pool.memset(QS[g][:, :, MH:STK], 0.0).then_inc(stage_init.sem, 1)
                    pool.memset(KS[g][:, :, MH:MH + 2], 1.0).then_inc(stage_init.sem, 1)
                    pool.memset(KS[g][:, :, MH + 2:STK], 0.0).then_inc(stage_init.sem, 1)

            link = Links(pool, pool_chain)

            def project(L, b):
                stage(L, b)
                stats_ready.wait(pool, ("A", L))
                mod_ready.wait(pool, (2 * L, b))
                for s in range(TB + 2):
                    if s < TB:
                        normalised(pool, ("A", L, b), s, HR[s % 2], link)
                    if s >= 2:
                        t = s - 2
                        stage_hi.wait(pool, (L, b, t))
                        src = TQ[t % 2].rearrange("p (a h c) -> p a h c", a=2, h=HN)
                        pool.tensor_tensor(QS[t % 2][:, :, 2 * HD:3 * HD].bitcast(F32R), src[:, 0, :, :], QS[t % 2][:, :, 0:HD],
                                           ALU.subtract).then_inc(stage_lo.sem, 1)
                        pool.tensor_tensor(KS[t % 2][:, :, HD:2 * HD].bitcast(F32R), src[:, 1, :, :], KS[t % 2][:, :, 0:HD],
                                           ALU.subtract).then_inc(stage_lo.sem, 1)

            project(0, 0)
            project(0, 1)
            pool.wait_ge(idx_ready, 3)
            pool.wait_ge(zeroed, 16 * SLOTS)
            for t in range(T):
                for c in range(2):
                    pool.indirect_dma_start(slot_in[:, :], bass.IndirectOffsetOnAxis(ap=IX[:, c, t:t + 1], axis=0),
                                            HF[:, t, :], None).then_inc(scattered, 16)

            def low_slot_weights(s, par):
                pool.wait_ge(dn_mm, s + 1)
                for n in (1, 2):
                    for h, (raw, hi, lo) in enumerate(split_steps(n, par)):
                        pool.wait_ge(ws_hi[n], s * 2 + (h + 1))
                        pool.tensor_tensor(lo, raw, hi.bitcast(F32), ALU.subtract).then_inc(ws_lo[n], 1)

            with pool.Fori(0, (SLOTS - 1) // 2, 1) as i:
                for par in range(2):
                    low_slot_weights(i * 2 + par, par)
            low_slot_weights(SLOTS - 1, 0)
            for par in range(2):
                pool.wait_ge(y_out[par], 16 + 16 * ((SLOTS + 1 - par) // 2))
            for t in range(T):
                if t >= 2:
                    pool.wait_ge(g_used, t - 1)
                for c in range(2):
                    pool.indirect_dma_start(G0[:, t % 2, c, :], None, slot_out[:, :],
                                            bass.IndirectOffsetOnAxis(ap=IX[:, c, t:t + 1], axis=0)
                                            ).then_inc(gathered[t % 2], 16)
            for b in range(B):
                project(1, b)
                for st in STEPS[1]:
                    if st[0] != "st":
                        continue
                    _, g, k, j = st
                    key = (1, b) + st
                    (p_dve if on_vector(1, st) else p_act).wait(pool, key)
                    diag = PR[:, k % 2, j, k * P:(k + 1) * P]
                    pool.affine_select(out=diag, in_=diag, compare_op=ALU.is_ge, fill=0.0, base=0,
                                       pattern=[[1, P]], channel_multiplier=-1).then_inc(p_mask.sem, 1)
            x_new.wait(pool, ("A", 1, 1, TB - 1))
            for l in range(L1N):
                if l >= 2:
                    ln_tr.wait(pool, (l - 2, T - 1))
                pool.memset(AC[:, l % 2, :, :], 0.0).then_inc(acc_zero, 1)
                with pool.Fori(0, PAIRS // 2, 1) as i:
                    for par in range(2):
                        n = i * 2 + (l * PAIRS + par)
                        pool.wait_ge(er_hi, n + 1)
                        pool.wait_ge(ex_mm, n * T + T)
                        pool.tensor_tensor(EL[:, par, :, :, :], ER[:, par, :, :, :],
                                           EH[:, par, :, :, :].bitcast(F32), ALU.subtract).then_inc(er_lo, 1)

        @block.scalar
        def _(act):
            act.wait_ge(loaded, 64)
            act.activation(CS[:, :, :, :], CS[:, :, :, :], ACT.Silu).then_inc(silu_c, 1)

            def high_weights(L):
                w_load.wait(act, L)
                if L == 1:
                    act.wait_ge(w_folded, 3)
                act.activation(WH[:, :, :], wraw, ACT.Copy).then_inc(w_hi.sem, 1)
                act.activation(WOH[:, :, :], woraw, ACT.Copy).then_inc(w_hi.sem, 1)
                act.activation(BZ[0:2, :], braw[0:2, :], ACT.Copy).then_inc(w_hi.sem, 1)
                if L == 0:
                    act.activation(BOZ[0:2, :], boraw[0:2, :], ACT.Copy).then_inc(w_hi.sem, 1)

            def root(use):
                sq_in.wait(act, use)
                act.activation(SM[:, 1, :], SM[:, 0, :], ACT.Sqrt).then_inc(sq_out.sem, 1)

            def transposed_hi(use, t):
                tr_done.wait(act, (use, t))
                if use == ("F", 0):
                    if t >= 2:
                        act.wait_ge(lg_mm, t - 1)
                    dst = HG[:, t % 2, :, :]
                elif use == ("F", 1):
                    dst = XH[:, :, t * P:(t + 1) * P]
                else:
                    if t >= 2:
                        qkv_done.wait(act, use[1:] + (t - 2,))
                    dst = HTH[:, t % 2, :, :]
                act.activation(dst, PS[:, t % 2, 0:D].rearrange("p (k c) -> p k c", k=KC),
                               ACT.Copy).then_inc(ht_hi.sem, 1)

            def project(L, b):
                if b == 0:
                    root(("A", L))
                stage_init.wait(act, (L, b))
                for s in range(TB + 3):
                    if s < TB:
                        transposed_hi(("A", L, b), s)
                    if 0 <= s - 1 < TB:
                        t = s - 1
                        qkv_done.wait(act, (L, b, t))
                        act.activation(V[:, t, :, 0:HD], PS[:, 4 + t % 2, 0:D].rearrange("p (h c) -> p h c", h=HN),
                                       ACT.Copy).then_inc(v_ready.sem, 1)
                        if L == 1:
                            if t >= 2:
                                fm_in.wait(act, (b, t - 2))
                            act.activation(SQ[t % 2], PS[:, 2 + t % 2, :], ACT.Square).then_inc(fm_sq.sem, 1)
                    if 0 <= s - 2 < TB:
                        t = s - 2
                        if L == 1:
                            fm_in.wait(act, (b, t))
                            act.activation(FS[:, 1, :], FS[:, 0, :], ACT.Sqrt).then_inc(fm_out.sem, 1)
                        q_ready.wait(act, (L, b, t))
                        if t >= 2:
                            stk_tr.wait(act, (L, b, t - 2, "k", 1))
                        src = TQ[t % 2].rearrange("p (a h c) -> p a h c", a=2, h=HN)
                        for a, dst in ((0, QS[t % 2][:, :, 0:2 * HD].rearrange("p h (r c) -> p h r c", r=2)),
                                       (1, KS[t % 2][:, :, 0:4 * HD].rearrange("p h (r c) -> p h r c", r=4)[:, :, 0:3:2, :])):
                            act.activation(dst.bitcast(F32R), src[:, a, :, None, :].to_broadcast([P, HN, 2, HD]),
                                           ACT.Copy).then_inc(stage_hi.sem, 1)
                    if 0 <= s - 3 < TB:
                        t = s - 3
                        for h in range(2):
                            stk_tr.wait(act, (L, b, t, "q", h))
                            act.activation(Q[:, 4 * h:4 * h + 4, t * P:(t + 1) * P],
                                           PS[:, 6 + h, :].rearrange("p (a c) -> p a c", a=4),
                                           ACT.Copy).then_inc(stk_q.sem, 1)
                        for h in range(2):
                            stk_tr.wait(act, (L, b, t, "k", h))
                            act.activation(K[0][0:STK, 4 * h:4 * h + 4, t * P:(t + 1) * P],
                                           PS[0:STK, 6 + h, :].rearrange("p (a c) -> p a c", a=4),
                                           ACT.Copy).then_inc(stk_ka.sem, 1)

            def attend(L, b):
                for st in STEPS[L]:
                    key = (L, b) + st
                    if st[0] == "st" and not on_vector(L, st):
                        _, g, k, j = st
                        st_done.wait(act, key)
                        if g or k >= 2:
                            pv_done.wait(act, (L, b, "pv") + ((g, k - 2) if k >= 2 else (g - 1, k + 6)))
                        else:
                            stk_kb.wait(act, (L, b, TB - 1, 1))
                        src = PS[:, bank[key]:bank[key] + 2, :].rearrange("p a c -> p (a c)")[:, k * P:S]
                        act.activation(PR[:, k % 2, j, k * P:S], src, ACT.Exp if L == 0 else ACT.Square,
                                       scale=1.0 if L else 0.25).then_inc(p_act.sem, 1)
                    if st[0] == "pv" and st[2] == TB - 1:
                        pv_done.wait(act, key)
                        if st[1] > 0:
                            o_tr.wait(act, (L, b, "otr", st[1] - 1, 1))
                        if key == (0, 0, "pv", 0, TB - 1):
                            act.wait_ge(zeroed, 16 * SLOTS)
                        act.activation(OT[:, :], PS[:, 4:6, :].rearrange("p a c -> p (a c)"),
                                       ACT.Copy).then_inc(o_evac.sem, 1)

            act.wait_ge(cvt, 6)
            high_weights(0)
            for L, b in UNITS[:2]:
                project(L, b)
                attend(L, b)

            root(("F", 0))
            for t in range(T):
                transposed_hi(("F", 0), t)
            act.wait_ge(gate_in, 1)
            act.activation(WT[:, 0, :], WT[:, 1, :], ACT.Exp).then_inc(gate_exp, 1)

            def high_slot_weights(s, par, n, h):
                act.wait_ge(wr_load[n], s * 16 + 16)
                act.wait_ge(dn_mm, s + 1)
                raw, hi, _ = split_steps(n, par)[h]
                act.activation(hi, raw, ACT.Copy).then_inc(ws_hi[n], 1)

            def high_slot_rows(s, par):
                act.wait_ge(xs_tr, s + 1)
                act.activation(XTH[:, par, :, :], PS[:, 6, :].rearrange("p (k c) -> p k c", k=KC), ACT.Copy).then_inc(xs_hi, 1)

            def hidden_silu(s, c):
                act.wait_ge(up_mm, s * HC + (c + 1))
                act.activation(SI[:, c % 2, :], PS[:, c % 4, 0:SLOT], ACT.Silu).then_inc(up_silu, 1)

            def hidden_high(s, c):
                act.wait_ge(up_gate, s * HC + (c + 1))
                act.activation(HH[:, c, :], GG[:, c % 3, :], ACT.Copy).then_inc(up_hi, 1)

            for n in range(3):
                for h in range(2):
                    high_slot_weights(0, 0, n, h)
            high_slot_rows(0, 0)
            with act.Fori(0, (SLOTS - 1) // 2, 1) as i:
                for par in range(2):
                    s = i * 2 + par
                    for c in range(HC):
                        hidden_silu(s, c)
                        if c:
                            hidden_high(s, c - 1)
                        if c < 6:
                            high_slot_weights(s + 1, (par + 1) % 2, c // 2, c % 2)
                        if c == 4:
                            high_slot_rows(s + 1, (par + 1) % 2)
                    hidden_high(s, HC - 1)
            for c in range(HC):
                hidden_silu(SLOTS - 1, c)
                if c:
                    hidden_high(SLOTS - 1, c - 1)
            hidden_high(SLOTS - 1, HC - 1)

            high_weights(1)
            for L, b in UNITS[2:]:
                project(L, b)
                attend(L, b)
            act.wait_ge(gw_load, 16 * L1N)
            act.activation(GWH[:, :, :, :], GR[:, :, :, :], ACT.Copy).then_inc(gw_hi, 1)

            def high_pair(n, par, count):
                act.wait_ge(er_load[par], count)
                act.wait_ge(ex_mm, n * T + T)
                act.activation(EH[:, par, :, :, :], ER[:, par, :, :, :], ACT.Copy).then_inc(er_hi, 1)

            def gate_evac(l, c):
                gt_mm.wait(act, (l, c))
                if l:
                    gt_tr.wait(act, (l - 1, c))
                act.activation(LT[:, c * 512:(c + 1) * 512], PS[0:E1, 6, :], ACT.Copy).then_inc(gt_evac.sem, 1)

            def gate_exp_(l, c):
                gt_max.wait(act, (l, c))
                tiles = EX[:, 4 * c:4 * c + 4, :]
                act.activation(tiles, tiles, ACT.Exp).then_inc(gt_exp.sem, 1)

            def layer_input_hi(l, t):
                ln_tr.wait(act, (l, t))
                act.activation(XH[:, :, t * P:(t + 1) * P], PS[:, t % 2, 0:D].rearrange("p (k c) -> p k c", k=KC),
                               ACT.Copy).then_inc(ln_hi.sem, 1)

            root(("F", 1))
            high_pair(0, 0, 32)
            run_between(None, lambda what, x: {"hi": lambda t: transposed_hi(("F", 1), t), "evac": lambda c: gate_evac(0, c),
                                               "exp": lambda c: gate_exp_(0, c)}.get(what, lambda x: None)(x))
            for l in range(L1N):
                with act.Fori(0, PAIRS // 2 - 1, 1) as i:
                    for par in range(2):
                        high_pair(i * 2 + (l * PAIRS + 1 + par), 1 - par, i * 32 + 32 * (l * PAIRS // 2 + 1 + par))
                high_pair(l * PAIRS + PAIRS - 1, 1, 32 * (l + 1) * PAIRS // 2)
                if l < L1N - 1:
                    high_pair((l + 1) * PAIRS, 0, 32 * ((l + 1) * PAIRS // 2 + 1))
                    run_between(l, lambda what, x: {"hi": lambda t: layer_input_hi(l, t), "evac": lambda c: gate_evac(l + 1, c),
                                                    "exp": lambda c: gate_exp_(l + 1, c)}.get(what, lambda x: None)(x))

        @block.vector
        def _(dve):
            link = Links(dve, chain)

            dve.sem_inc(ev_b, T)
            dve.sem_inc(y_evac, 1)
            dve.memset(zero_rows, 0.0).then_inc(zero_t, 1)
            dve.memset(PS[:, 4:6, :], 0.0).then_inc(psum_zero, 1)
            dve.memset(BZ[:, :].bitcast(F32), 0.0).then_inc(cvt, 1)
            dve.memset(BOZ[:, :].bitcast(F32), 0.0).then_inc(cvt, 1)
            dve.memset(MP[:, :, :, :], -BIG).then_inc(cvt, 1)
            dve.wait_ge(loaded, 64)
            dve.tensor_copy(IDB[:, :], ident).then_inc(cvt, 1)
            dve.tensor_copy(MQB[:, :], CST[:, C_MQ:C_MQ + P]).then_inc(cvt, 1)
            dve.tensor_copy(MKB[:, :], CST[:, C_MK:C_MK + P]).then_inc(cvt, 1)
            dve.tensor_copy(BE[:, :], CST[:, C_BE:C_BE + P]).then_inc(cvt, 1)
            dve.wait_ge(silu_c, 1)

            def spread(L):
                dve.tensor_copy(CB[:, :, :, :].rearrange("p k b c -> p (k b) c"),
                                CS[:, L, :, :].rearrange("p k b -> p (k b)")[:, :, None].to_broadcast([P, KC * B, P])
                                ).then_inc(cb_ready, 1)

            def modulation(n):
                mod_mm.wait(dve, n)
                for b in range(B):
                    src = PS[:, 4 + 2 * b:6 + 2 * b, :].rearrange("p a c -> p (a c)")
                    gate = src[:, 2 * D:3 * D]
                    dve.tensor_copy(MOD[:, b, 0:D], src[:, 0:D]).then_inc(mod_ready.sem, 1)
                    dve.tensor_scalar(MOD[:, b, D:2 * D], src[:, D:2 * D], 1.0, None, ALU.add).then_inc(mod_ready.sem, 1)
                    dve.tensor_scalar(GT2[:, 1, :], gate, 0.0, 2.0, ALU.is_ge, ALU.mult)
                    link(dve.tensor_scalar(GT2[:, 0, :], gate, -1.0, None, ALU.mult))
                    link(dve.tensor_tensor(GT2[:, 0, :], gate, GT2[:, 0, :], ALU.max))
                    link(dve.tensor_scalar(GT2[:, 0, :], GT2[:, 0, :], 0.25, None, ALU.max))
                    dve.scalar_tensor_tensor(out=MOD[:, b, 2 * D:3 * D], in0=GT2[:, 1, :], scalar=-1.0,
                                             in1=GT2[:, 0, :], op0=ALU.add, op1=ALU.mult).then_inc(mod_ready.sem, 1)
                    mod_ready.wait(dve, (n, b))

            def fold_feature_map():
                w_load.wait(dve, 1)
                heads = {k: wraw[:, k, 0:2 * D].rearrange("p (h c) -> p h c", c=HD) for k in range(KC)}
                for k in range(KC):
                    link(dve.tensor_tensor(heads[k], heads[k], GB[:, 0, None, :].to_broadcast([P, 2 * HN, HD]), ALU.mult))
                    link(dve.tensor_reduce(FS[:, k, :], heads[k], AX_X, ALU.add))
                    dve.scalar_tensor_tensor(out=heads[k], in0=FS[:, k, :, None].to_broadcast([P, 2 * HN, HD]), scalar=-1.0 / HD,
                                             in1=heads[k], op0=ALU.mult, op1=ALU.add).then_inc(w_folded, 1)
                dve.memset(BZ[:, :].bitcast(F32), 0.0)
                dve.memset(braw[0:2, 2 * D:3 * D], 0.0)
                link(dve.tensor_reduce(FS[:, KC, 0:1], GB[:, 1, :], AX_X, ALU.add))
                link(dve.tensor_scalar(FS[:, KC, 1:2], FS[:, KC, 0:1], -1.0 / HD, None, ALU.mult))
                dve.tensor_scalar(braw[0:2, 0:2 * D].rearrange("p (h c) -> p h c", c=HD),
                                  GB[0:2, 1, None, :].to_broadcast([2, 2 * HN, HD]), FS[0:2, KC, 1:2], None,
                                  ALU.add).then_inc(w_folded, 1)

            def low_weights(L):
                w_hi.wait(dve, L)
                dve.tensor_tensor(WL[:, :, :], wraw, WH[:, :, :].bitcast(F32), ALU.subtract).then_inc(w_ready.sem, 1)
                dve.tensor_tensor(WOL[:, :, :], woraw, WOH[:, :, :].bitcast(F32), ALU.subtract).then_inc(w_ready.sem, 1)
                for dst, raw in ((BZ, braw), (BOZ, boraw))[:2 - L]:
                    dve.scalar_tensor_tensor(out=dst[0:2, :], in0=dst[0:2, :].bitcast(F32), scalar=CST[0:2, C_SC:C_SC + 1],
                                             in1=raw[0:2, :], op0=ALU.mult, op1=ALU.add).then_inc(w_ready.sem, 1)

            def refine(y, v, tmp):
                link(dve.tensor_tensor(tmp, y, y, ALU.mult))
                link(dve.tensor_tensor(tmp, tmp, v, ALU.mult))
                link(dve.tensor_scalar(tmp, tmp, -0.5, 1.5, ALU.mult, ALU.add))
                link(dve.tensor_tensor(y, y, tmp, ALU.mult))

            def statistics(use):
                before = {("A", 0): None, ("F", 0): ("A", 0, 1, TB - 1), ("A", 1): ("F", 0, T - 1), ("F", 1): ("A", 1, 1, TB - 1)}[use]
                if before:
                    x_new.wait(dve, before)
                for t in range(T):
                    last = dve.bn_stats(STAT[:, t, :], X[:, t, :])
                link(last)
                for t in range(T):
                    last = dve.bn_aggr(MV[:, t, :], STAT[:, t, :])
                link(last)
                dve.tensor_scalar(SM[:, 0, :], MV[:, :, 1], LN_EPS, None, ALU.add).then_inc(sq_in.sem, 1)
                sq_out.wait(dve, use)
                link(dve.reciprocal(SM[:, 2, :], SM[:, 1, :]))
                refine(SM[:, 2, :], SM[:, 0, :], SM[:, 3, :])
                dve.scalar_tensor_tensor(out=SM[:, 4, :], in0=MV[:, :, 0], scalar=-1.0, in1=SM[:, 2, :],
                                         op0=ALU.mult, op1=ALU.mult).then_inc(stats_ready.sem, 1)
                stats_ready.wait(dve, use)

            def transposed_lo(use, t):
                ht_hi.wait(dve, (use, t))
                hi, lo = ((XH[:, :, t * P:(t + 1) * P], XL[:, :, t * P:(t + 1) * P]) if use == ("F", 1)
                          else (HTH[:, t % 2, :, :], HTL[:, t % 2, :, :]))
                dve.tensor_tensor(lo, PS[:, t % 2, 0:D].rearrange("p (k c) -> p k c", k=KC), hi.bitcast(F32),
                                  ALU.subtract).then_inc(ht_lo.sem, 1)

            def rotate(b, t):
                qkv_done.wait(dve, (0, b, t))
                if t:
                    q_ready.wait(dve, (0, b, t - 1))
                src = PS[:, 2 + t % 2, :].rearrange("p (h c) -> p h c", c=HD)
                cos = CST[:, C_COS + t * HD:C_COS + (t + 1) * HD]
                sin = CST[:, C_SIN + t * HD:C_SIN + (t + 1) * HD]
                dve.tensor_tensor(TA.rearrange("p (h c) -> p h c", c=HD), src,
                                  cos[:, None, :].to_broadcast([P, 2 * HN, HD]), ALU.mult)
                tb = TB_.rearrange("p (h c) -> p h c", c=HD)
                for o in range(2):
                    last = dve.tensor_tensor(tb[:, :, o:HD:2], src[:, :, 1 - o:HD:2],
                                             sin[:, None, o:HD:2].to_broadcast([P, 2 * HN, HD // 2]), ALU.mult)
                link(last)
                dve.tensor_tensor(TQ[t % 2], TA, TB_, ALU.add).then_inc(q_ready.sem, 1)

            def feature_map(b, t):
                fm_sq.wait(dve, (b, t))
                link(dve.tensor_reduce(FS[:, 3, :], SQ[t % 2].rearrange("p (h c) -> p h c", c=HD), AX_X, ALU.add))
                dve.tensor_scalar(FS[:, 0, :], FS[:, 3, :], 1.0 / HD, LN_EPS, ALU.mult, ALU.add).then_inc(fm_in.sem, 1)
                fm_out.wait(dve, (b, t))
                link(dve.reciprocal(FS[:, 4, :], FS[:, 1, :]))
                refine(FS[:, 4, :], FS[:, 0, :], FS[:, 5, :])
                link(dve.tensor_scalar(FS[:, 4, 0:HN], FS[:, 4, 0:HN], 0.25, None, ALU.mult))
                dve.tensor_tensor(TQ[t % 2].rearrange("p (h c) -> p h c", c=HD),
                                  PS[:, 2 + t % 2, :].rearrange("p (h c) -> p h c", c=HD),
                                  FS[:, 4, :, None].to_broadcast([P, 2 * HN, HD]), ALU.mult).then_inc(q_ready.sem, 1)

            def project(L, b):
                use = ("A", L, b)
                if b == 0:
                    statistics(("A", L))
                stage_init.wait(dve, (L, b))
                for s in range(TB + 3):
                    if 0 <= s - 1 < TB:
                        if s - 1 >= 2:
                            qkv_done.wait(dve, (L, b, s - 3))
                        transposed_lo(use, s - 1)
                    if 0 <= s - 2 < TB:
                        (feature_map if L else rotate)(b, s - 2)
                    if 0 <= s - 3 < TB:
                        t = s - 3
                        for h in range(2):
                            stk_tr.wait(dve, (L, b, t, "k", h))
                            dve.tensor_copy(K[1][STK:P, 4 * h:4 * h + 4, t * P:(t + 1) * P],
                                            PS[STK:P, 6 + h, :].rearrange("p (a c) -> p a c", a=4)).then_inc(stk_kb.sem, 1)

            def attend(L, b):
                for st in STEPS[L]:
                    key = (L, b) + st
                    if st[0] == "max":
                        _, g, i, j = st
                        for c, (c0, w) in enumerate(max_chunks(i)):
                            max_mm.wait(dve, key + (c,))
                            last_max = key + (c,)
                            dve.tensor_reduce(MP[:, j, i, c:c + 1], PS[:, bank[key + (c,)], 0:w], AX_X,
                                              ALU.max).then_inc(max_red.sem, 1)
                    elif st[0] == "msc":
                        g = st[1]
                        max_red.wait(dve, last_max)
                        link(dve.tensor_reduce(MX[:, 0, :, :], MP[:, :, :, :], AX_X, ALU.max))
                        link(dve.tensor_scalar(MX[:, 1, :, :], MX[:, 0, :, :], -1.0, None, ALU.mult))
                        link(dve.tensor_copy(MS[:, :, 0, :].bitcast(F32R), MX[:, 1, :, :]))
                        dve.tensor_tensor(MS[:, :, 1, :].bitcast(F32R), MX[:, 1, :, :], MS[:, :, 0, :],
                                          ALU.subtract).then_inc(ms_ready.sem, 1)
                    elif st[0] == "ms":
                        ms_tr.wait(dve, key)
                        if b or st[1]:
                            m_out.wait(dve, (L, b, "ms", st[1] - 1) if st[1] else (L, 0, "ms", NQ - 1))
                        dve.tensor_copy(MT[:, :], PS[0:64, bank[key], 0:P]).then_inc(mt_ready.sem, 1)
                    elif st[0] == "st" and on_vector(L, st):
                        _, g, k, j = st
                        st_done.wait(dve, key)
                        if g or k >= 2:
                            pv_done.wait(dve, (L, b, "pv") + ((g, k - 2) if k >= 2 else (g - 1, k + 6)))
                        else:
                            stk_ka.wait(dve, (L, b, TB - 1, 1))
                        src = PS[:, bank[key]:bank[key] + 2, :].rearrange("p a c -> p (a c)")[:, k * P:S]
                        dst = PR[:, k % 2, j, k * P:S]
                        link(dve.tensor_copy(dst, src))
                        dve.tensor_tensor(dst, src, dst, ALU.mult).then_inc(p_dve.sem, 1)
                    elif st[0] == "otr":
                        _, g, half = st
                        o_tr.wait(dve, key)
                        if g or half:
                            on_ready.wait(dve, (L, b, "otr") + ((g, 0) if half else (g - 1, 1)))
                        src = PS[:, bank[key], :].rearrange("p (t j c) -> p t j c", t=4, j=4)
                        sums = src[:, :, :, HD:HD + 1].rearrange("p t j a -> p t (j a)")
                        rc = RC[:, 0, :].rearrange("p (t j) -> p t j", t=4)
                        if L == 1:
                            link(dve.tensor_scalar(RC[:, 1, :].rearrange("p (t j) -> p t j", t=4), sums, Z_EPS, None, ALU.add))
                            sums = RC[:, 1, :].rearrange("p (t j) -> p t j", t=4)
                        link(dve.reciprocal(rc, sums))
                        dve.tensor_tensor(ON[:, 4 * half:4 * half + 4, 64 * g:64 * g + 64].rearrange("p t (j c) -> p t j c", j=4),
                                          src[:, :, :, 0:HD], rc[:, :, :, None].to_broadcast([P, 4, 4, HD]),
                                          ALU.mult).then_inc(on_ready.sem, 1)
                for t in range(TB + 1):
                    if t < TB:
                        on_tr.wait(dve, (L, b, t))
                        if t >= 2:
                            pr_done.wait(dve, (L, b, t - 2))
                        src = PS[:, bank[(L, b, "ont", t)], 0:D].rearrange("p (k c) -> p k c", k=KC)
                        link(dve.tensor_copy(HTH[:, t % 2, :, :], src))
                        dve.tensor_tensor(HTL[:, t % 2, :, :], src, HTH[:, t % 2, :, :].bitcast(F32),
                                          ALU.subtract).then_inc(ont.sem, 1)
                    if t >= 1:
                        pr_done.wait(dve, (L, b, t - 1))
                        if t >= 3:
                            x_new.wait(dve, ("A", L, b, t - 3))
                        gated = GT2[:, (t - 1) % 2, :]
                        link(dve.tensor_tensor(gated, PS[:, (t - 1) % 2, 0:D], MOD[:, b, 2 * D:3 * D], ALU.mult))
                        dve.tensor_tensor(X[:, b * TB + t - 1, :], X[:, b * TB + t - 1, :], gated,
                                          ALU.add).then_inc(x_new.sem, 1)

            spread(0)
            modulation(0)
            low_weights(0)
            for L, b in UNITS[:2]:
                project(L, b)
                attend(L, b)

            dve.memset(LG[:, :, :], BIG)
            dve.memset(R1[:, :, :], BIG)
            dve.memset(R2[:, :, :], BIG)
            link(dve.memset(PRE[:, :, :], 0.0))
            link(dve.memset(OF[:, :], 0.0))
            modulation(1)
            statistics(("F", 0))
            for t in range(T):
                normalised(dve, ("F", 0), t, HF[:, t, :], link)
            dve.wait_ge(lg_mm, T)
            link(dve.tensor_copy(LG[:, :, 0:E0], PS[:, 2, 0:T * E0].rearrange("p (t e) -> p t e", t=T)))
            for t in range(T):
                last = dve.max(T8[:, t, :], LG[:, t, 0:E0])
            link(last)
            dve.tensor_copy(R2[:, :, 0:2], T8[:, :, 0:2])
            dve.tensor_copy(R1[:, :, 0:1], T8[:, :, 0:1])
            link(dve.tensor_tensor(WT[:, 1, :], T8[:, :, 1], T8[:, :, 0], ALU.subtract))
            dve.tensor_copy(WT[:, 1, :], WT[:, 1, :]).then_inc(gate_in, 1)
            for t in range(T):
                dve.match_replace(RP[:, t, :], R2[:, t, :], LG[:, t, :], -BIG)
                last = dve.match_replace(RP1[:, t, :], R1[:, t, :], LG[:, t, :], -BIG)
            link(last)
            dve.tensor_tensor(MM[:, :, :], RP[:, :, 0:E0], LG[:, :, 0:E0], ALU.not_equal).then_inc(route_in, 1)
            link(dve.tensor_tensor(A0[:, :, :], RP1[:, :, 0:E0], LG[:, :, 0:E0], ALU.not_equal))
            dve.wait_ge(route_in, 1)
            link(dve.tensor_tensor(A1[:, :, :], MM[:, :, :], A0[:, :, :], ALU.subtract))
            dve.wait_ge(gate_exp, 1)
            link(dve.tensor_scalar(WT[:, 1, :], WT[:, 0, :], 1.0, None, ALU.add))
            link(dve.reciprocal(W01[:, 0, :], WT[:, 1, :]))
            link(dve.tensor_tensor(W01[:, 1, :], W01[:, 0, :], WT[:, 0, :], ALU.mult))
            dve.wait_ge(route_mm, 1)
            dve.tensor_copy(WIN[:, :, :], PS[:, 3, 0:T * E0].rearrange("p (t e) -> p t e", t=T))
            link(dve.tensor_copy(TOT[:, :, :], PS[:, 3, P:P + T * E0].rearrange("p (t e) -> p t e", t=T)))
            for t in range(T):
                link(dve.tensor_tensor(PRE[:, t + 1, :], PRE[:, t, :], TOT[:, t, :], ALU.add))
            link(dve.tensor_tensor(CMP[:, :, :], PRE[:, T, :, None].to_broadcast([P, E0, 8]),
                                   CST[:, None, C_THR:C_THR + 8].to_broadcast([P, E0, 8]), ALU.is_gt))
            link(dve.tensor_reduce(NT[:, :], CMP[:, :, :], AX_X, ALU.add))
            for e in range(E0):
                link(dve.tensor_tensor(OF[:, e + 1:e + 2], OF[:, e:e + 1], NT[:, e:e + 1], ALU.add))
            link(dve.tensor_tensor(POS[:, :, :], WIN[:, :, :], PRE[:, 0:T, :], ALU.add))
            link(dve.scalar_tensor_tensor(out=POS[:, :, :], in0=OF[:, None, 0:E0].to_broadcast([P, T, E0]), scalar=float(SLOT),
                                          in1=POS[:, :, :], op0=ALU.mult, op1=ALU.add))
            dve.tensor_tensor(PA[:, 0, :, :], POS[:, :, :], A0[:, :, :], ALU.mult)
            link(dve.tensor_tensor(PA[:, 1, :, :], POS[:, :, :], A1[:, :, :], ALU.mult))
            link(dve.tensor_reduce(PF[:, :, :], PA[:, :, :, :], AX_X, ALU.add))
            dve.tensor_copy(IX[:, :, :], PF[:, :, :]).then_inc(idx_ready, 1)
            link(dve.tensor_tensor(SE[:, :, :], CST[:, C_SLOT:C_SLOT + 24, None].to_broadcast([P, 24, E0]),
                                   OF[:, None, 1:E0 + 1].to_broadcast([P, 24, E0]), ALU.is_ge))
            link(dve.tensor_reduce(EF[:, :], SE[:, :, :], AX_X, ALU.add))
            dve.tensor_scalar(EF[:, :], EF[:, :], float(E0 - 1), None, ALU.min).then_inc(idx_ready, 1)
            dve.wait_ge(idx_ready, 2)
            dve.tensor_copy(EI[:, :], EF[:, :]).then_inc(idx_ready, 1)

            def low_slot_weights(s, par, h):
                dve.wait_ge(ws_hi[0], s * 2 + (h + 1))
                raw, hi, lo = split_steps(0, par)[h]
                dve.tensor_tensor(lo, raw, hi.bitcast(F32), ALU.subtract).then_inc(ws_lo[0], 1)

            def low_slot_rows(s, par):
                dve.wait_ge(xs_hi, s + 1)
                dve.tensor_tensor(XTL[:, par, :, :], PS[:, 6, :].rearrange("p (k c) -> p k c", k=KC),
                                  XTH[:, par, :, :].bitcast(F32), ALU.subtract).then_inc(xs_lo, 1)

            def hidden_gate(s, c):
                dve.wait_ge(up_silu, s * HC + (c + 1))
                if c >= 3:
                    dve.wait_ge(up_lo, s * HC + (c - 2))
                dve.tensor_tensor(GG[:, c % 3, :], PS[:, c % 4, SLOT:2 * SLOT], SI[:, c % 2, :], ALU.mult).then_inc(up_gate, 1)

            def hidden_low(s, c):
                dve.wait_ge(up_hi, s * HC + (c + 1))
                dve.tensor_tensor(HL[:, c, :], GG[:, c % 3, :], HH[:, c, :].bitcast(F32), ALU.subtract).then_inc(up_lo, 1)

            def slot_output(s, par, pair):
                dve.wait_ge(dn_mm, s + 3)
                dve.wait_ge(y_out[par], pair * 16 + 16)
                dve.tensor_copy(YO[:, par, :, :], PS[:, 4:6, 0:D]).then_inc(y_evac, 1)

            low_slot_weights(0, 0, 0)
            low_slot_weights(0, 0, 1)
            low_slot_rows(0, 0)
            with dve.Fori(0, (SLOTS - 1) // 2, 1) as i:
                for par in range(2):
                    s = i * 2 + par
                    for c in range(HC):
                        hidden_gate(s, c)
                        if c >= 2:
                            hidden_low(s, c - 2)
                        if c in (2, 3):
                            low_slot_weights(s + 1, (par + 1) % 2, c - 2)
                        if c == 5:
                            low_slot_rows(s + 1, (par + 1) % 2)
                    hidden_low(s, HC - 2)
                    hidden_low(s, HC - 1)
                    slot_output(s, par, i)
            for c in range(HC):
                hidden_gate(SLOTS - 1, c)
                if c >= 2:
                    hidden_low(SLOTS - 1, c - 2)
            hidden_low(SLOTS - 1, HC - 2)
            hidden_low(SLOTS - 1, HC - 1)
            slot_output(SLOTS - 1, 0, SLOTS // 2)
            for t in range(T):
                dve.wait_ge(gathered[t % 2], 32 * (t // 2 + 1))
                link(dve.tensor_scalar(GT[:, 0, :], G0[:, t % 2, 0, :], W01[:, 0, t:t + 1], None, ALU.mult))
                dve.scalar_tensor_tensor(out=GT[:, 1, :], in0=G0[:, t % 2, 1, :], scalar=W01[:, 1, t:t + 1], in1=GT[:, 0, :],
                                         op0=ALU.mult, op1=ALU.add).then_inc(g_used, 1)
                dve.wait_ge(g_used, t + 1)
                link(dve.tensor_tensor(GT2[:, 0, :], GT[:, 1, :], MOD[:, t // TB, 2 * D:3 * D], ALU.mult))
                dve.tensor_tensor(X[:, t, :], X[:, t, :], GT2[:, 0, :], ALU.add).then_inc(x_new.sem, 1)

            spread(1)
            modulation(2)
            fold_feature_map()
            low_weights(1)
            for L, b in UNITS[2:]:
                project(L, b)
                attend(L, b)
            modulation(3)
            dve.wait_ge(gw_hi, 1)
            dve.tensor_tensor(GWL[:, :, :, :], GR[:, :, :, :], GWH[:, :, :, :].bitcast(F32), ALU.subtract).then_inc(gw_lo, 1)
            statistics(("F", 1))
            def gate_top(l, c):
                gt_tr.wait(dve, (l, c))
                tiles = slice(4 * c, 4 * c + 4)
                dve.tensor_copy(LGT[:, tiles, :], PS[:, 7, 0:4 * E1].rearrange("p (t e) -> p t e", t=4)).then_inc(gt_read.sem, 1)
                gt_read.wait(dve, (l, c))
                for t in range(4 * c, 4 * c + 4):
                    last = dve.max(M8[:, t, :], LGT[:, t, :])
                link(last)
                dve.tensor_tensor(EX[:, tiles, :], LGT[:, tiles, :], M8[:, tiles, 0:1].to_broadcast([P, 4, E1]),
                                  ALU.subtract).then_inc(gt_max.sem, 1)
                for t in range(4 * c, 4 * c + 4):
                    last = dve.match_replace(RPL[:, t, :], M8[:, t, :], LGT[:, t, :], -BIG)
                link(last)
                dve.tensor_tensor(MK[:, tiles, :], RPL[:, tiles, :], LGT[:, tiles, :], ALU.not_equal)

            def gate_weights(l, c):
                gt_exp.wait(dve, (l, c))
                tiles = slice(4 * c, 4 * c + 4)
                link(dve.tensor_reduce(SU[:, 0, tiles], EX[:, tiles, :], AX_X, ALU.add))
                link(dve.reciprocal(SU[:, 1, tiles], SU[:, 0, tiles]))
                weights = WD[:, l % 2, tiles, :]
                link(dve.tensor_tensor(weights, EX[:, tiles, :], MK[:, tiles, :], ALU.mult))
                link(dve.tensor_tensor(weights, weights, SU[:, 1, tiles, None].to_broadcast([P, 4, E1]), ALU.mult))

            def accumulate(l, n, par, e, t):
                if e == 0:
                    dve.wait_ge(ex_mm, n * T + (2 * T + t + 1))
                    dve.wait_ge(ev_b, n * T + (t + 1))
                else:
                    dve.wait_ge(ev_a, n * T + (t + 1))
                acc = AC[:, l % 2, t, :]
                dve.scalar_tensor_tensor(out=acc, in0=PS[:, 2 + t % 4, e * D:(e + 1) * D],
                                         scalar=WP[:, par, t, e:e + 1], in1=acc, op0=ALU.mult,
                                         op1=ALU.add).then_inc((ev_a, ev_b)[e], 1)

            def pair_weights(l, n, par, first):
                dve.tensor_copy(WP[:, par, :, :], WD[:, l % 2, :, bass.ds(first, 2)]).then_inc(wp_ready, 1)
                dve.wait_ge(wp_ready, n + 1)

            def whole_pair(l, n, par, first):
                pair_weights(l, n, par, first)
                for s in range(T + 1):
                    if s < T:
                        accumulate(l, n, par, 0, s)
                    if s:
                        accumulate(l, n, par, 1, s - 1)

            def layer_input_lo(l, t):
                ln_hi.wait(dve, (l, t))
                dve.tensor_tensor(XL[:, :, t * P:(t + 1) * P], PS[:, t % 2, 0:D].rearrange("p (k c) -> p k c", k=KC),
                                  XH[:, :, t * P:(t + 1) * P].bitcast(F32), ALU.subtract).then_inc(ln_lo.sem, 1)

            def first_layer(what, x):
                if what == "transpose":
                    normalised(dve, ("F", 1), x, HR1[:, x % 2, :], link)
                elif what == "lo":
                    transposed_lo(("F", 1), x)
                elif what == "top":
                    gate_top(0, x)
                elif what == "weights":
                    gate_weights(0, x)

            run_between(None, first_layer)
            for l in range(L1N):
                dve.wait_ge(acc_zero, l + 1)
                with dve.Fori(0, PAIRS // 2 - 1, 1) as i:
                    for par in range(2):
                        whole_pair(l, i * 2 + (l * PAIRS + par), par, i * 4 + 2 * par)
                n = (l + 1) * PAIRS - 2
                whole_pair(l, n, 0, E1 - 4)
                n += 1
                pair_weights(l, n, 1, E1 - 2)

                def next_layer(what, x):
                    if what in ("evac0", "evac1"):
                        accumulate(l, n, 1, int(what[-1]), x)
                    elif l < L1N - 1 and what == "lo":
                        layer_input_lo(l, x)
                    elif l < L1N - 1 and what == "top":
                        gate_top(l + 1, x)
                    elif l < L1N - 1 and what == "weights":
                        gate_weights(l + 1, x)
                    elif l == L1N - 1 and what == "lo":
                        dve.wait_ge(ev_b, (L1N * PAIRS - 1) * T + T + x + 1)
                        if x >= 2:
                            dve.wait_ge(stored[x % 2], 16 * (x // 2))
                        link(dve.tensor_tensor(GT2[:, x % 2, :], AC[:, l % 2, x, :], MOD[:, x // TB, 2 * D:3 * D], ALU.mult))
                        dve.tensor_tensor(OUT_T[:, x % 2, :], X[:, x, :], GT2[:, x % 2, :], ALU.add).then_inc(o_ready, 1)

                run_between(l, next_layer)

        @block.tensor
        def _(pe):
            pe.sem_inc(dn_mm, 2)
            pe.sem_inc(ex_mm, 2 * T)

            def exact(out_, pairs, first=True, last=True):
                for n, (a, w) in enumerate(pairs):
                    ins = pe.matmul(out_, a, w, start=first and n == 0, stop=last and n == len(pairs) - 1,
                                    skip_group_check=True)
                return ins

            def modulation(n):
                mod_w.wait(pe, n)
                pe.wait_ge(cb_ready, n // 2 + 1)
                w = {0: wmraw, 1: WM0[:, :, :], 2: wmraw, 3: WM1[:, :, :]}[n]
                for b in range(B):
                    for c, (c0, width) in enumerate(((0, 512), (512, 256))):
                        for k in range(KC):
                            ins = pe.matmul(PS[:, 4 + 2 * b + c, 0:width], CB[:, k, b, :], w[:, k, c0:c0 + width],
                                            start=k == 0, stop=k == KC - 1)
                    ins.then_inc(mod_mm.sem, 1)

            def normalised_transposes(use, t, h):
                h_ready.wait(pe, (use, t))
                if t >= 2:
                    (ht_hi if use == ("F", 0) else ht_lo).wait(pe, (use, t - 2))
                for k in range(KC):
                    ins = pe.transpose(PS[:, t % 2, k * P:(k + 1) * P], h[:, k * P:(k + 1) * P], ident)
                ins.then_inc(tr_done.sem, 1)

            def project(L, b):
                use = ("A", L, b)
                w_ready.wait(pe, L)
                if b:
                    x_new.wait(pe, ("A", L, 0, TB - 1))
                for s in range(TB + 3):
                    if s < TB:
                        normalised_transposes(use, s, HR[s % 2])
                    if 0 <= s - 1 < TB:
                        t = s - 1
                        ht_lo.wait(pe, (use, t))
                        if t >= 2:
                            q_ready.wait(pe, (L, b, t - 2))
                            v_ready.wait(pe, (L, b, t - 2))
                        qk, v = PS[:, 2 + t % 2, :], PS[:, 4 + t % 2, 0:D]
                        for dst, c0, c1 in ((qk, 0, 2 * D), (v, 2 * D, 3 * D)):
                            biased = L == 0 or c0 == 0
                            if biased:
                                exact(dst, [(BE[:, :], BZ[:, c0:c1])], last=False)
                            ins = exact(dst, [(a[:, t % 2, k, :], w[:, k, c0:c1]) for k in range(KC)
                                              for a, w in ((HTH, WH), (HTH, WL), (HTL, WH))], first=not biased)
                        ins.then_inc(qkv_done.sem, 1)
                    if 0 <= s - 3 < TB:
                        t = s - 3
                        stage_lo.wait(pe, (L, b, t))
                        for n, (what, src) in enumerate((("q", QS), ("k", KS))):
                            for h in range(2):
                                if what == "k":
                                    stk_q.wait(pe, (L, b, t, h))
                                elif t:
                                    stk_ka.wait(pe, (L, b, t - 1, h))
                                    stk_kb.wait(pe, (L, b, t - 1, h))
                                for a in range(4):
                                    pair = 4 * h + a
                                    ins = pe.transpose(PS[:, 6 + h, a * P:(a + 1) * P],
                                                       src[t % 2][:, 2 * pair:2 * pair + 2, :].rearrange("p h c -> p (h c)"),
                                                       ident)
                                ins.then_inc(stk_tr.sem, 1)
                stk_ka.wait(pe, (L, b, TB - 1, 1))
                stk_kb.wait(pe, (L, b, TB - 1, 1))
                stk_q.wait(pe, (L, b, TB - 1, 1))

            def free(key):
                for reader, label in bank_free[key]:
                    reader.wait(pe, label)

            def attend(L, b):
                for st in STEPS[L]:
                    key = (L, b) + st
                    if st[0] == "max":
                        _, g, i, j = st
                        pair, keys = 2 * g + j // 2, K[j % 2]
                        for c, (c0, w) in enumerate(max_chunks(i)):
                            free(key + (c,))
                            to = bank[key + (c,)]
                            last = c0 + w == (i + 1) * P
                            ins = pe.matmul(PS[:, to, 0:w], Q[:, pair, i * P:(i + 1) * P], keys[:, pair, c0:c0 + w],
                                            start=True, stop=not last, skip_group_check=True)
                            if last:
                                ins = pe.matmul(PS[:, to, w - P:w], IDB[:, :], MQB[:, :], start=False, stop=True,
                                                skip_group_check=True)
                            ins.then_inc(max_mm.sem, 1)
                    elif st[0] == "ms":
                        ms_ready.wait(pe, key)
                        free(key)
                        pe.transpose(PS[0:64, bank[key], 0:P], MS[:, :, :, :].rearrange("p j h i -> p (j h i)"),
                                     ident).then_inc(ms_tr.sem, 1)
                    elif st[0] == "st":
                        _, g, k, j = st
                        if k == 0 and j == 0 and L == 0:
                            m_rows.wait(pe, (L, b, "ms", g))
                        free(key)
                        pair, keys = 2 * g + j // 2, K[j % 2]
                        mask_bank = 0 if k < 4 else 1
                        for c in range(2):
                            lo, hi = max(k * P, 512 * c), 512 * (c + 1)
                            if lo >= hi:
                                continue
                            to = bank[key] + c
                            masked = L == 0 and c == mask_bank
                            ins = pe.matmul(PS[:, to, lo - 512 * c:512], keys[:, pair, k * P:(k + 1) * P], Q[:, pair, lo:hi],
                                            start=True, stop=not masked, skip_group_check=True)
                            if masked:
                                ins = pe.matmul(PS[:, to, lo - 512 * c:lo - 512 * c + P], IDB[:, :], MKB[:, :],
                                                start=False, stop=True, skip_group_check=True)
                        ins.then_inc(st_done.sem, 1)
                    elif st[0] == "pv":
                        _, g, k = st
                        if L == 0:
                            p_act.wait(pe, (L, b, "st", g, k, 3))
                        else:
                            p_mask.wait(pe, (L, b, "st", g, k, 3))
                        if k == 0 and g:
                            o_evac.wait(pe, (L, b, "pv", g - 1, TB - 1))
                        for c in range(2):
                            lo, hi = max(k * P, 512 * c), 512 * (c + 1)
                            if lo >= hi:
                                continue
                            for j in range(4):
                                ins = pe.matmul(PS[32 * j:32 * j + HD + 1, 4 + c, lo - 512 * c:512], V[:, k, 4 * g + j, :],
                                                PR[:, k % 2, j, lo:hi], start=k == 0, stop=k == 4 * c + 3,
                                                skip_group_check=True)
                        ins.then_inc(pv_done.sem, 1)
                    elif st[0] == "otr":
                        _, g, half = st
                        free(key)
                        o_evac.wait(pe, (L, b, "pv", g, TB - 1))
                        for a in range(4):
                            t = 4 * half + a
                            ins = pe.transpose(PS[:, bank[key], a * P:(a + 1) * P], OT[:, t * P:(t + 1) * P], ident)
                        ins.then_inc(o_tr.sem, 1)
                on_ready.wait(pe, (L, b, "otr", NQ - 1, 1))
                for t in range(TB + 1):
                    if t < TB:
                        free((L, b, "ont", t))
                        for k in range(KC):
                            ins = pe.transpose(PS[:, bank[(L, b, "ont", t)], k * P:(k + 1) * P], ON[:, t, k * P:(k + 1) * P], ident)
                        ins.then_inc(on_tr.sem, 1)
                    if t:
                        ont.wait(pe, (L, b, t - 1))
                        if t >= 3:
                            x_new.wait(pe, ("A", L, b, t - 3))
                        dst = PS[:, (t - 1) % 2, 0:D]
                        if L == 0:
                            exact(dst, [(BE[:, :], BOZ[:, :])], last=False)
                        exact(dst, [(a[:, (t - 1) % 2, k, :], w[:, k, :]) for k in range(KC)
                                    for a, w in ((HTH, WOH), (HTH, WOL), (HTL, WOH))], first=L == 1).then_inc(pr_done.sem, 1)

            pe.wait_ge(cvt, 7)
            pe.wait_ge(psum_zero, 1)
            modulation(0)
            for L, b in UNITS[:2]:
                mod_ready.wait(pe, (0, 1))
                project(L, b)
                attend(L, b)

            x_new.wait(pe, ("A", 0, 1, TB - 1))
            modulation(1)
            pe.wait_ge(wg_load, 16)
            for s in range(T + 1):
                if s < T:
                    normalised_transposes(("F", 0), s, HF[:, s, :])
                if s:
                    t = s - 1
                    ht_hi.wait(pe, (("F", 0), t))
                    for k in range(KC):
                        ins = pe.matmul(PS[:, 2, t * E0:(t + 1) * E0], HG[:, t % 2, k, :], WG[:, k, :],
                                        start=k == 0, stop=k == KC - 1)
                    ins.then_inc(lg_mm, 1)
            pe.wait_ge(route_in, 1)
            chosen = MM[:, :, :].rearrange("p t e -> p (t e)")
            pe.matmul(PS[:, 3, 0:P], CST[:, C_TRI:C_TRI + P], chosen, start=True, stop=True)
            pe.matmul(PS[:, 3, P:2 * P], CST[:, C_ONE:C_ONE + P], chosen, start=True, stop=True).then_inc(route_mm, 1)

            def slot_transposes(par, pair):
                pe.wait_ge(xs_load[par], pair * 16 + 16)
                for k in range(KC):
                    for a in range(2):
                        ins = pe.transpose(PS[:, 6, k * SLOT + a * P:k * SLOT + (a + 1) * P], XT[:, par, a, k * P:(k + 1) * P], ident)
                ins.then_inc(xs_tr, 1)

            def slot_up(s, par, c):
                if c == 0:
                    pe.wait_ge(xs_lo, s + 1)
                if c >= 4:
                    pe.wait_ge(up_gate, s * HC + (c - 3))
                for n in range(2):
                    if c == 0:
                        pe.wait_ge(ws_lo[n], s * 2 + 2)
                    cols = slice(c * P, (c + 1) * P)
                    ins = exact(PS[:, c % 4, n * SLOT:(n + 1) * SLOT],
                                [(w[:, par, n, k, cols], r[:, par, k, :]) for k in range(KC)
                                 for w, r in ((H13, XTH), (H13, XTL), (L13, XTH))])
                ins.then_inc(up_mm, 1)

            def slot_down(s, par):
                pe.wait_ge(y_evac, s + 1)
                pe.wait_ge(ws_lo[2], s * 2 + 2)
                for c in range(HC):
                    pe.wait_ge(up_lo, s * HC + (c + 1))
                    for a in range(2):
                        cols = slice(a * P, (a + 1) * P)
                        ins = exact(PS[:, 4 + a, 0:D], [(HH[:, c, cols], H2[:, par, c, :]), (HH[:, c, cols], L2[:, par, c, :]),
                                                        (HL[:, c, cols], H2[:, par, c, :])], first=c == 0, last=c == HC - 1)
                ins.then_inc(dn_mm, 1)

            slot_transposes(0, 0)
            with pe.Fori(0, (SLOTS - 1) // 2, 1) as i:
                for par in range(2):
                    s = i * 2 + par
                    for c in range(HC):
                        slot_up(s, par, c)
                        if c == 3:
                            slot_transposes((par + 1) % 2, i + par)
                    slot_down(s, par)
            for c in range(HC):
                slot_up(SLOTS - 1, 0, c)
            slot_down(SLOTS - 1, 0)

            x_new.wait(pe, ("F", 0, T - 1))
            modulation(2)
            for L, b in UNITS[2:]:
                mod_ready.wait(pe, (2, 1))
                project(L, b)
                attend(L, b)

            x_new.wait(pe, ("A", 1, 1, TB - 1))
            modulation(3)
            pe.wait_ge(gw_lo, 1)

            def gate_logits(l, c):
                last = 4 * c + 3
                if l:
                    ln_lo.wait(pe, (l - 1, last))
                else:
                    ht_lo.wait(pe, (("F", 1), last))
                if c or l:
                    gt_evac.wait(pe, (l, c - 1) if c else (l - 1, 3))
                cols = slice(c * 512, (c + 1) * 512)
                exact(PS[:, 6, :], [(g[:, l, k, :], r[:, k, cols]) for k in range(KC)
                                    for g, r in ((GWH, XH), (GWH, XL), (GWL, XH))]).then_inc(gt_mm.sem, 1)

            def gate_rows(l, c):
                gt_evac.wait(pe, (l, c))
                if c or l:
                    gt_read.wait(pe, (l, c - 1) if c else (l - 1, 3))
                for a in range(4):
                    t = 4 * c + a
                    ins = pe.transpose(PS[:, 7, a * E1:(a + 1) * E1], LT[:, t * P:(t + 1) * P], CST[0:E1, C_ID:C_ID + E1])
                ins.then_inc(gt_tr.sem, 1)

            def product(n, par, t):
                pe.wait_ge(ev_b, n * T + (t + T - 3))
                cols = slice(t * P, (t + 1) * P)
                exact(PS[:, 2 + t % 4, :], [(r[:, k, cols], w[:, par, k, :, :].rearrange("p e m -> p (e m)"))
                                            for k in range(KC) for r, w in ((XH, EH), (XH, EL), (XL, EH))]
                      ).then_inc(ex_mm, 1)

            def output_transposes(l, t):
                pe.wait_ge(ev_b, ((l + 1) * PAIRS - 1) * T + T + t + 1)
                if t >= 2:
                    ln_lo.wait(pe, (l, t - 2))
                for k in range(KC):
                    ins = pe.transpose(PS[:, t % 2, k * P:(k + 1) * P], AC[:, l % 2, t, k * P:(k + 1) * P], ident)
                ins.then_inc(ln_tr.sem, 1)

            def first_layer(what, x):
                if what == "transpose":
                    normalised_transposes(("F", 1), x, HR1[:, x % 2, :])
                elif what == "gate":
                    gate_logits(0, x)
                elif what == "gate_rows":
                    gate_rows(0, x)

            run_between(None, first_layer)
            for l in range(L1N):
                with pe.Fori(0, PAIRS // 2 - 1, 1) as i:
                    for par in range(2):
                        n = i * 2 + (l * PAIRS + par)
                        pe.wait_ge(er_lo, n + 1)
                        for t in range(T):
                            product(n, par, t)
                n = (l + 1) * PAIRS - 2
                pe.wait_ge(er_lo, n + 1)
                for t in range(T):
                    product(n, 0, t)
                pe.wait_ge(er_lo, n + 2)

                def next_layer(what, x):
                    if what == "product":
                        product(n + 1, 1, x)
                    elif l < L1N - 1 and what == "transpose":
                        output_transposes(l, x)
                    elif l < L1N - 1 and what == "gate":
                        gate_logits(l + 1, x)
                    elif l < L1N - 1 and what == "gate_rows":
                        gate_rows(l + 1, x)

                run_between(l, next_layer)


def constant_table():
    import numpy as np

    c = np.zeros((P, C_W), np.float32)
    r, k = np.arange(P)[:, None], np.arange(P)[None, :]
    c[:, C_ID:C_ID + P] = r == k
    c[:, C_TRI:C_TRI + P] = r < k
    c[:, C_ONE:C_ONE + P] = 1.0
    inv = np.float32(1.0) / np.float32(10000.0) ** (np.arange(HD // 2, dtype=np.float32) / np.float32(HD // 2))
    angle = np.arange(S, dtype=np.float32)[:, None] * inv[None, :].astype(np.float32)
    cos = np.repeat(np.cos(angle), 2, axis=-1).astype(np.float32)
    sin = np.repeat(np.sin(angle), 2, axis=-1).astype(np.float32)
    sin[:, 0::2] *= -1
    c[:, C_COS:C_COS + TB * HD] = cos.reshape(TB, P, HD).transpose(1, 0, 2).reshape(P, -1)
    c[:, C_SIN:C_SIN + TB * HD] = sin.reshape(TB, P, HD).transpose(1, 0, 2).reshape(P, -1)
    c[:, C_THR:C_THR + 8] = SLOT * np.arange(8)
    c[:, C_SLOT:C_SLOT + 24] = np.arange(24)
    c[1, C_SC] = -1.0
    c[0:2, C_BE:C_BE + P] = 1.0
    c[:, C_MQ:C_MQ + P] = np.where(k > r, -1e30, 0.0)
    c[:, C_MK:C_MK + P] = np.where(r > k, -1e30, 0.0)
    return c


def kernel(**inputs):
    import numpy as _np
    import concourse.bacc as _bacc
    from concourse import mybir as _mybir
    from concourse.bass_utils import run_bass_kernel_spmd as _run

    g = {k: _np.asarray(v) for k, v in inputs.items()}
    gates = _np.zeros((L1N, D, P), _np.float32)
    gates[:, :, 0:E1] = g["L1_ffn_gate_w"].transpose(0, 2, 1)
    a = {
        "x": g["L0_attn_x"].reshape(T * P, D),
        "cT0": g["L0_c"].T,
        "wmod0": g["L0_wmod"],
        "wqkv0": _np.concatenate([g["L0_attn_Wq"].T, g["L0_attn_Wk"].T, g["L0_attn_Wv"].T], axis=1),
        "bqkv0": _np.tile(_np.concatenate([g["L0_attn_bq"], g["L0_attn_bk"], g["L0_attn_bv"]])[None], (2, 1)),
        "wo0": g["L0_attn_Wo"].T,
        "bo0": _np.tile(g["L0_attn_bo"][None], (2, 1)),
        "wg": g["L0_ffn_Wg"],
        "w1": g["L0_ffn_w1"],
        "w3": g["L0_ffn_w3"],
        "w2": g["L0_ffn_w2"],
        "cT1": g["L1_c"].T,
        "wmod1": g["L1_wmod"],
        "wqkv1": _np.concatenate([g["L1_attn_Wq"].T, g["L1_attn_Wk"].T, g["L1_attn_Wv"].T], axis=1),
        "wo1": g["L1_attn_Wo"].T,
        "gamma": _np.tile(g["L1_attn_gamma"][None], (P, 1)),
        "beta": _np.tile(g["L1_attn_beta"][None], (P, 1)),
        "gw1": gates,
        "ew1": g["L1_ffn_expert_w"].transpose(0, 1, 3, 2).reshape(L1N * E1 * D, D),
        "consts": constant_table(),
    }
    nc = _bacc.Bacc("TRN2", target_bir_lowering=False, num_devices=1)
    arrays = {f"in_{k}": _np.ascontiguousarray(v) for k, v in a.items()}
    args = [nc.dram_tensor(k, v.shape, _mybir.dt.from_np(v.dtype), kind="ExternalInput").ap() for k, v in arrays.items()]
    out = nc.dram_tensor("out_x", (T * P, D), F32, kind="ExternalOutput").ap()
    adaln_kernel(nc, *args, out)
    r = _run(nc, [arrays], core_ids=[0])
    return r.results[0]["out_x"].reshape(B, S, D)
```

```python
from contextlib import ExitStack

import concourse.bass as bass
from concourse import mybir


F32 = mybir.dt.float32
F32R = mybir.dt.float32r
BF16 = mybir.dt.bfloat16
U32 = mybir.dt.uint32
I32 = mybir.dt.int32
ALU = mybir.AluOpType
ACT = mybir.ActivationFunctionType
AX_X = mybir.AxisListType.X

P = 128
D = 256
KC = D // P
B = 2
S = 1024
TB = S // P
T = B * TB
HN = 16
HD = D // HN
NQ = 4
E0 = 8
HID = 896
HC = HID // P
SLOT = 256
SLOTS = (T * P * 2 + E0 * (SLOT - 1)) // SLOT
E1 = 16
L1N = 4
PAIRS = E1 // 2
STK = 64
MH, ML = 48, 49
BIG = 3.0e38
LN_EPS = 1e-5
Z_EPS = 1e-5

C_ID, C_TRI, C_ONE, C_COS, C_SIN = 0, 128, 256, 384, 512
C_THR, C_SLOT, C_SC, C_BE, C_MQ, C_W = 640, 648, 672, 673, 801, 929


class Tally:

    def __init__(self, sem):
        self.sem, self.n, self.at = sem, 0, {}

    def plan(self, label, k=1):
        self.n += k
        self.at[label] = self.n

    def wait(self, eng, label):
        eng.wait_ge(self.sem, self.at[label])


def adaln_kernel(nc, x, cT0, wmod0, wqkv0, bqkv0, wo0, bo0, wg, w1, w3, w2,
                 cT1, wmod1, wqkv1, wo1, gamma, beta, gw1, ew1, consts, out):
    ctx = ExitStack()
    with ctx:
        def sem(name):
            return ctx.enter_context(nc.semaphore(name))

        def tally(name):
            return Tally(sem(name))

        def sb(name, shape, dt, scope=ctx):
            return scope.enter_context(nc.sbuf_tensor(name, shape, dt))

        PS = ctx.enter_context(nc.psum_tensor("PS", [P, 8, 512], F32))

        slot_in = nc.dram_tensor("slot_in", [SLOTS * SLOT, D], F32, kind="Internal").ap()
        slot_out = nc.dram_tensor("slot_out", [SLOTS * SLOT, D], F32, kind="Internal").ap()
        max_rows = nc.dram_tensor("max_rows", [B * NQ, 64, P], F32, kind="Internal").ap()

        X = sb("X", [P, T, D], F32)
        CST = sb("CST", [P, C_W], F32)
        IDB = sb("IDB", [P, P], BF16)
        MQB = sb("MQB", [P, P], BF16)
        BE = sb("BE", [P, P], F32R)
        CS = sb("CS", [P, 2, KC, B], F32)
        CB = sb("CB", [P, KC, B, P], F32)
        MOD = sb("MOD", [P, B, 3 * D], F32)
        STAT = sb("STAT", [P, T, 6], F32)
        MV = sb("MV", [P, T, 2], F32)
        SM = sb("SM", [P, 6, T], F32)
        GT2 = sb("GT2", [P, 2, D], F32)
        ident = CST[:, C_ID:C_ID + P]

        sa = ExitStack()
        Q = sb("Q", [P, HN // 2, S], F32R, sa)
        K = [sb("KA", [P, HN // 2, S], F32R, sa), sb("KB", [P, HN // 2, S], F32R, sa)]
        V = sb("V", [P, TB, HN, HD + 1], F32, sa)
        PR = sb("PR", [P, 2, 4, S], F32, sa)
        HTH = sb("HTH", [P, 2, KC, P], F32R, sa)
        HTL = sb("HTL", [P, 2, KC, P], F32R, sa)
        WH = sb("WH", [P, KC, 3 * D], F32R, sa)
        WL = sb("WL", [P, KC, 3 * D], F32R, sa)
        WOH = sb("WOH", [P, KC, D], F32R, sa)
        WOL = sb("WOL", [P, KC, D], F32R, sa)
        BZ = sb("BZ", [P, 3 * D], F32R, sa)
        BOZ = sb("BOZ", [P, D], F32R, sa)
        OT = sb("OT", [P, S], F32, sa)
        ON = sb("ON", [P, TB, D], F32, sa)
        GB = sb("GB", [P, 2, HD], F32, sa)
        MP = sb("MP", [P, 4, TB, 2], F32, sa)
        MX = sb("MX", [P, 2, 4, TB], F32, sa)
        MS = sb("MS", [P, 4, 2, TB], F32, sa)
        MT = sb("MT", [64, P], F32, sa)
        RC = sb("RC", [P, 2, 16], F32, sa)
        sa.close()
        flat = PR[:, :, :, :].rearrange("p a b c -> p (a b c)")
        QS = [flat[:, g * 2048:g * 2048 + 1024].rearrange("p (h c) -> p h c", h=HN) for g in range(2)]
        KS = [flat[:, g * 2048 + 1024:g * 2048 + 2048].rearrange("p (h c) -> p h c", h=HN) for g in range(2)]
        TA = flat[:, 4096:4608]
        TB_ = flat[:, 4608:5120]
        SQ = [TA, TB_]
        TQ = [flat[:, 5120 + 512 * g:5632 + 512 * g] for g in range(2)]
        HR = [flat[:, 6144 + 256 * g:6400 + 256 * g] for g in range(2)]
        FS = flat[:, 6656:6912].rearrange("p (a b) -> p a b", b=32)
        wraw = flat[:, 0:1536].rearrange("p (k n) -> p k n", k=KC)
        woraw = flat[:, 1536:2048].rearrange("p (k n) -> p k n", k=KC)
        wmraw = flat[:, 2048:3584].rearrange("p (k n) -> p k n", k=KC)
        braw = flat[:, 3584:4352]
        boraw = flat[:, 4352:4608]

        zero_rows = OT[:, 0:2 * D]

        sf = ExitStack()
        WM0 = sb("WM0", [P, KC, 3 * D], F32, sf)
        WG = sb("WG", [P, KC, E0], F32, sf)
        HF = sb("HF", [P, T, D], F32, sf)
        W01 = sb("W01", [P, 2, T], F32, sf)
        IX = sb("IX", [P, 2, T], U32, sf)
        HG = sb("HG", [P, 2, KC, P], F32, sf)
        LG = sb("LG", [P, T, 2 * E0], F32, sf)
        T8 = sb("T8", [P, T, 8], F32, sf)
        R2 = sb("R2", [P, T, 8], F32, sf)
        R1 = sb("R1", [P, T, 8], F32, sf)
        RP = sb("RP", [P, T, 2 * E0], F32, sf)
        RP1 = sb("RP1", [P, T, 2 * E0], F32, sf)
        MM = sb("MM", [P, T, E0], F32, sf)
        A0 = sb("A0", [P, T, E0], F32, sf)
        A1 = sb("A1", [P, T, E0], F32, sf)
        WT = sb("WT", [P, 2, T], F32, sf)
        WIN = sb("WIN", [P, T, E0], F32, sf)
        TOT = sb("TOT", [P, T, E0], F32, sf)
        PRE = sb("PRE", [P, T + 1, E0], F32, sf)
        CMP = sb("CMP", [P, E0, 8], F32, sf)
        NT = sb("NT", [P, E0], F32, sf)
        OF = sb("OF", [P, E0 + 1], F32, sf)
        POS = sb("POS", [P, T, E0], F32, sf)
        PA = sb("PA", [P, 2, T, E0], F32, sf)
        PF = sb("PF", [P, 2, T], F32, sf)
        SE = sb("SE", [P, 24, E0], F32, sf)
        EF = sb("EF", [P, 24], F32, sf)
        EI = sb("EI", [P, 24], I32, sf)
        XT = sb("XT", [P, 2, 2, D], F32, sf)
        XTH = sb("XTH", [P, 2, KC, SLOT], F32R, sf)
        XTL = sb("XTL", [P, 2, KC, SLOT], F32R, sf)
        R13 = sb("R13", [P, 2, KC, HID], F32, sf)
        RW2 = sb("RW2", [P, HC, D], F32, sf)
        H13 = sb("H13", [P, 2, 2, KC, HID], F32R, sf)
        L13 = sb("L13", [P, 2, 2, KC, HID], F32R, sf)
        H2 = sb("H2", [P, 2, HC, D], F32R, sf)
        L2 = sb("L2", [P, 2, HC, D], F32R, sf)
        SI = sb("SI", [P, 2, SLOT], F32, sf)
        GG = sb("GG", [P, 3, SLOT], F32, sf)
        HH = sb("HH", [P, HC, SLOT], F32R, sf)
        HL = sb("HL", [P, HC, SLOT], F32R, sf)
        YO = sb("YO", [P, 2, 2, D], F32, sf)
        sf.close()
        G0 = ON[:, 0:4, :].rearrange("p (a c) d -> p a c d", a=2)
        GT = ON[:, 4:6, :]

        def split_steps(n, par):
            if n < 2:
                return [(R13[:, n, k, :], H13[:, par, n, k, :], L13[:, par, n, k, :]) for k in range(KC)]
            return [(RW2[:, a:b, :], H2[:, par, a:b, :], L2[:, par, a:b, :]) for a, b in ((0, HC // 2), (HC // 2, HC))]

        sg = ExitStack()
        WM1 = sb("WM1", [P, KC, 3 * D], F32, sg)
        HR1 = sb("HR1", [P, 2, D], F32, sg)
        XH = sb("XH", [P, KC, T * P], F32R, sg)
        XL = sb("XL", [P, KC, T * P], F32R, sg)
        AC = sb("AC", [P, 2, T, D], F32, sg)
        GR = sb("GR", [P, L1N, KC, P], F32, sg)
        GWH = sb("GWH", [P, L1N, KC, P], F32R, sg)
        GWL = sb("GWL", [P, L1N, KC, P], F32R, sg)
        LT = sb("LT", [E1, T * P], F32, sg)
        LGT = sb("LGT", [P, T, E1], F32, sg)
        M8 = sb("M8", [P, T, 8], F32, sg)
        RPL = sb("RPL", [P, T, E1], F32, sg)
        EX = sb("EX", [P, T, E1], F32, sg)
        SU = sb("SU", [P, 2, T], F32, sg)
        MK = sb("MK", [P, T, E1], F32, sg)
        WD = sb("WD", [P, 2, T, E1], F32, sg)
        WP = sb("WP", [P, 2, T, 2], F32, sg)
        ER = sb("ER", [P, 2, KC, 2, D], F32, sg)
        EH = sb("EH", [P, 2, KC, 2, D], F32R, sg)
        EL = sb("EL", [P, 2, KC, 2, D], F32R, sg)
        OUT_T = sb("OUT_T", [P, 2, D], F32, sg)
        sg.close()

        USES = [("A", 0, 0), ("A", 0, 1), ("F", 0), ("A", 1, 0), ("A", 1, 1), ("F", 1)]
        UNITS = [(L, b) for L in range(2) for b in range(B)]

        loaded = sem("loaded")
        x_load = sem("x_load")
        cvt = sem("cvt")
        psum_zero = sem("psum_zero")
        chain = sem("chain")
        pool_chain = sem("pool_chain")
        stats_ready = tally("stats_ready")
        silu_c = sem("silu_c")
        cb_ready = sem("cb_ready")
        mod_w = tally("mod_w")
        mod_mm = tally("mod_mm")
        mod_ready = tally("mod_ready")
        w_load = tally("w_load")
        w_folded = sem("w_folded")
        w_hi = tally("w_hi")
        w_ready = tally("w_ready")
        sq_in = tally("sq_in")
        sq_out = tally("sq_out")
        fm_sq = tally("fm_sq")
        fm_in = tally("fm_in")
        fm_out = tally("fm_out")
        x_hat = tally("x_hat")
        scaled = tally("scaled")
        h_ready = tally("h_ready")
        tr_done = tally("tr_done")
        ht_hi = tally("ht_hi")
        ht_lo = tally("ht_lo")
        qkv_done = tally("qkv_done")
        q_ready = tally("q_ready")
        v_ready = tally("v_ready")
        stage_init = tally("stage_init")
        stage_hi = tally("stage_hi")
        stage_lo = tally("stage_lo")
        stk_tr = tally("stk_tr")
        stk_q = tally("stk_q")
        stk_ka = tally("stk_ka")
        stk_kb = tally("stk_kb")
        max_mm = tally("max_mm")
        max_red = tally("max_red")
        ms_ready = tally("ms_ready")
        ms_tr = tally("ms_tr")
        mt_ready = tally("mt_ready")
        m_out = tally("m_out")
        m_rows = tally("m_rows")
        st_done = tally("st_done")
        p_act = tally("p_act")
        p_dve = tally("p_dve")
        p_mask = tally("p_mask")
        pv_done = tally("pv_done")
        o_evac = tally("o_evac")
        o_tr = tally("o_tr")
        on_ready = tally("on_ready")
        on_tr = tally("on_tr")
        ont_hi = tally("ont_hi")
        gated = tally("gated")
        ont = tally("ont")
        pr_done = tally("pr_done")
        x_new = tally("x_new")
        wg_load = sem("wg_load")
        lg_mm = sem("lg_mm")
        gate_in = sem("gate_in")
        gate_exp = sem("gate_exp")
        route_in = sem("route_in")
        route_mm = sem("route_mm")
        zero_t = sem("zero_t")
        zeroed = sem("zeroed")
        idx_ready = sem("idx_ready")
        scattered = sem("scattered")
        xs_load = [sem(f"xs_load{n}") for n in range(2)]
        wr_load = [sem(f"wr_load{n}") for n in range(3)]
        xs_tr = sem("xs_tr")
        xs_hi = sem("xs_hi")
        xs_lo = sem("xs_lo")
        ws_hi = [sem(f"ws_hi{n}") for n in range(3)]
        ws_lo = [sem(f"ws_lo{n}") for n in range(3)]
        up_mm = sem("up_mm")
        up_silu = sem("up_silu")
        up_gate = sem("up_gate")
        up_hi = sem("up_hi")
        up_lo = sem("up_lo")
        dn_mm = sem("dn_mm")
        y_evac = sem("y_evac")
        y_out = [sem(f"y_out{n}") for n in range(2)]
        gathered = [sem(f"gathered{n}") for n in range(2)]
        g_first = sem("g_first")
        g_used = sem("g_used")
        gw_load = sem("gw_load")
        gw_hi = sem("gw_hi")
        gw_lo = sem("gw_lo")
        gt_mm = tally("gt_mm")
        gt_evac = tally("gt_evac")
        gt_tr = tally("gt_tr")
        gt_read = tally("gt_read")
        gt_max = tally("gt_max")
        gt_exp = tally("gt_exp")
        er_load = [sem("er_load0"), sem("er_load1")]
        er_hi = sem("er_hi")
        er_lo = sem("er_lo")
        ex_mm = sem("ex_mm")
        wp_ready = sem("wp_ready")
        ev_a = sem("ev_a")
        ev_b = sem("ev_b")
        ln_tr = tally("ln_tr")
        ln_hi = tally("ln_hi")
        ln_lo = tally("ln_lo")
        o_ready = sem("o_ready")
        stored = [sem(f"stored{n}") for n in range(2)]

        for n in range(4):
            mod_w.plan(n, 16)
            mod_mm.plan(n, B)
            mod_ready.plan((n, "rows"), 2 * B)
            for b in range(B):
                mod_ready.plan((n, b))
        for L in range(2):
            w_load.plan(L, 16 * 4)
            w_hi.plan(L, 4 if L == 0 else 3)
            w_ready.plan(L, 4 if L == 0 else 3)
        for u in USES:
            if u[2:] != (1,):
                for what in (sq_in, sq_out, stats_ready):
                    what.plan(u[:2])
            for t in range(T if u[0] == "F" else TB):
                h_ready.plan((u, t))
                if u[0] == "F":
                    x_hat.plan((u, t))
                    scaled.plan((u, t))
                tr_done.plan((u, t))
                ht_hi.plan((u, t))
                if u != ("F", 0):
                    ht_lo.plan((u, t))
        for L, b in UNITS:
            if (L, b) == (0, 0):
                for what in ("ones", "KA", "KB"):
                    stage_init.plan((L, what))
                stage_init.plan((L, b), 6)
            elif (L, b) == (1, 0):
                stage_init.plan((L, "ones"))
                stage_init.plan((L, b), 6)
            else:
                stage_init.plan((L, b), 6)
            for t in range(TB):
                qkv_done.plan((L, b, t))
                q_ready.plan((L, b, t))
                v_ready.plan((L, b, t))
                if L == 1:
                    fm_sq.plan((b, t))
                    fm_in.plan((b, t))
                    fm_out.plan((b, t))
                stage_hi.plan((L, b, t), 2)
                stage_lo.plan((L, b, t), 2)
                for what in ("q", "k"):
                    for h in range(2):
                        stk_tr.plan((L, b, t, what, h))
                for h in range(2):
                    stk_q.plan((L, b, t, h))
                    stk_ka.plan((L, b, t, h))
                    stk_kb.plan((L, b, t, h))

        def max_chunks(i):
            w = (i + 1) * P
            if w <= 512:
                return [(0, w)]
            return [(0, 384), (384, 256)] if w == 640 else [(0, 512), (512, w - 512)]

        COVER, PV_LAG = 13, (3, 3)

        def steps(L):
            order = [(i, j) for j in range(4) for i in (1, 5, 0, 4, 3, 7, 2, 6)]
            todo = []
            for g in range(1, NQ) if L == 0 else ():
                mine = [("max", g, i, j) for i, j in order]
                todo += [("msc", g - 1)] + mine[:2] + [("ms", g - 1)] + mine[2:]
            todo += [("msc", NQ - 1), ("ms", NQ - 1)] if L == 0 else []
            lead = 2 + COVER if L == 0 else 0
            seq, todo = todo[:lead], todo[lead:]
            for g in range(NQ):
                for n in range(TB * 4):
                    k, j = n // 4, n % 4
                    seq.append(("st", g, k, j))
                    if j == PV_LAG[L] and (g or k):
                        seq.append(("pv", g, k - 1) if k else ("pv", g - 1, TB - 1))
                    while todo:
                        seq.append(todo.pop(0))
                        if seq[-1][0] == "max":
                            break
                    if g and k == 4 and j == 2:
                        seq += [("otr", g - 1, 0), ("otr", g - 1, 1)]
            return seq + [("pv", NQ - 1, TB - 1), ("otr", NQ - 1, 0), ("otr", NQ - 1, 1)]

        STEPS = {L: steps(L) for L in range(2)}

        def on_vector(L, st):
            return L == 1 and st[3] == 3

        def transposes_in_flight(use):
            return 1 if use[:2] == ("A", 0) else 2

        def tile_v(L, t):
            return PS[:, 4 + (t % 2 if L else 0), 0:D]

        def tile_transposed(use, t):
            return PS[:, t % transposes_in_flight(use), 0:D]

        def early_maxes(L, s, part):
            i = s - 4
            return [("max", 0, i, j) for j in (2 * part, 2 * part + 1)] if L == 0 and 0 <= i < TB else []

        bank, bank_free, last_reader = {}, {}, {}

        def take(key, banks, reader, label):
            bank[key] = banks[0]
            waits = []
            for k in banks:
                if k in last_reader and last_reader[k] not in waits:
                    waits.append(last_reader[k])
                last_reader[k] = (reader, label)
            bank_free[key] = waits

        for L, b in UNITS:
            last_reader.clear()
            rows_out = pairs_out = 0
            for s in range(TB + 4):
                for part in range(2):
                    for st in early_maxes(L, s, part):
                        for c in range(len(max_chunks(st[2]))):
                            key = (L, b) + st + (c,)
                            max_mm.plan(key)
                            max_red.plan(key)
                            take(key, ((1, 5)[rows_out % 2],), max_red, key)
                            rows_out += 1
            scores_begun = L == 1
            for st in STEPS[L]:
                key = (L, b) + st
                scores_begun = scores_begun or st[0] == "st"
                narrow = (6, 7) if scores_begun else (6, 7, 0, 1, 2, 3)
                wide = ((0, 1), (2, 3), (6, 7)) if L == 1 or st[1] == NQ - 1 else ((0, 1), (2, 3))
                if st[0] == "max":
                    for c in range(len(max_chunks(st[2]))):
                        max_mm.plan(key + (c,))
                        max_red.plan(key + (c,))
                        take(key + (c,), (narrow[rows_out % len(narrow)],), max_red, key + (c,))
                        rows_out += 1
                elif st[0] == "msc":
                    ms_ready.plan((L, b, "ms", st[1]))
                elif st[0] == "ms":
                    for what in (ms_tr, mt_ready):
                        what.plan(key)
                    m_out.plan(key, 16)
                    m_rows.plan(key, 64)
                    take(key, (narrow[rows_out % len(narrow)],), mt_ready, key)
                    rows_out += 1
                elif st[0] == "st":
                    st_done.plan(key)
                    reader = p_dve if on_vector(L, st) else p_act
                    reader.plan(key)
                    p_mask.plan(key)
                    take(key, wide[pairs_out % len(wide)], reader, key)
                    pairs_out += 1
                elif st[0] == "pv":
                    pv_done.plan(key)
                    if st[2] == TB - 1:
                        o_evac.plan(key)
                elif st[0] == "otr":
                    o_tr.plan(key)
                    on_ready.plan(key)
                    take(key, (6 + st[2],), on_ready, key)
            for t in range(TB):
                on_tr.plan((L, b, t))
                ont_hi.plan((L, b, t))
                ont.plan((L, b, t))
                gated.plan((L, b, t))
                take((L, b, "ont", t), (6 + t % 2,), ont, (L, b, t))
                pr_done.plan((L, b, t))
                x_new.plan(("A", L, b, t))
            if (L, b) == (0, 1):
                for t in range(T):
                    x_new.plan(("F", 0, t))
        for l in range(L1N):
            for c in range(4):
                for what in (gt_mm, gt_evac, gt_tr, gt_read, gt_max, gt_exp):
                    what.plan((l, c))
            for t in range(T if l < L1N - 1 else 0):
                ln_tr.plan((l, t))
                ln_hi.plan((l, t))
                ln_lo.plan((l, t))

        def between(first):
            slots = [[] for _ in range(2 * T + 2)]
            after = 10 if first else T
            for t in range(T):
                if not first:
                    slots[t] += [("product", t), ("evac0", t)]
                    slots[t + 1].append(("evac1", t))
                else:
                    slots[t].insert(0, ("hat", t))
                    slots[t + 1].append(("normalise", t))
                slots[t + 2] += [("transpose", t), ("hi", t)]
                slots[t + 3].append(("lo", t))
                slots[after + t] += [("next_product", t), ("next_evac0", t)]
                slots[after + t + 1].append(("next_evac1", t))
            for c in range(4):
                slots[4 * c + 7] += [("gate", c), ("evac", c)]
                slots[4 * c + 8] += [("gate_rows", c), ("top", c), ("exp", c)]
                slots[4 * c + 9].append(("weights", c))
            return [x for slot in slots for x in slot]

        def run_between(l, parts):
            for what, x in between(l is None):
                if l == L1N - 1 and what not in ("product", "evac0", "evac1"):
                    what = "finish" if what == "lo" else None
                if what in parts:
                    parts[what](x)

        def scale_tile(eng, use, t, h, done):
            b = ((0 if use[0] == "F" else use[2] * TB) + t) // TB
            done(eng.tensor_tensor(h, h, MOD[:, b, D:2 * D], ALU.mult))

        def shift_tile(pool, use, t, h):
            b = ((0 if use[0] == "F" else use[2] * TB) + t) // TB
            pool.tensor_tensor(h, h, MOD[:, b, 0:D], ALU.add).then_inc(h_ready.sem, 1)

        class Links:

            def __init__(self, eng, sem_):
                self.eng, self.sem, self.n = eng, sem_, 0

            def __call__(self, ins):
                self.n += 1
                ins.then_inc(self.sem, 1)
                self.eng.wait_ge(self.sem, self.n)

        block = ctx.enter_context(nc.Block())

        @block.sync
        def _(sp):
            for par in range(2):
                sp.sem_inc(y_out[par], 16)
            sp.dma_start(CST[:, :], consts).then_inc(loaded, 16)
            sp.dma_start(CS[:, 0, :, :], cT0.rearrange("(k p) b -> p k b", p=P)).then_inc(loaded, 16)
            sp.dma_start(CS[:, 1, :, :], cT1.rearrange("(k p) b -> p k b", p=P)).then_inc(loaded, 16)

            def attention_loads(L):
                wm, w, wo = (wmod0, wqkv0, wo0) if L == 0 else (wmod1, wqkv1, wo1)
                sp.dma_start(wmraw, wm[:, 0:3 * D].rearrange("(k p) n -> p k n", p=P)).then_inc(mod_w.sem, 16)
                if L == 0:
                    sp.dma_start(X[:, :, :], x.rearrange("(t p) d -> p t d", p=P)).then_inc(x_load, 16)
                sp.dma_start(wraw, w.rearrange("(k p) n -> p k n", p=P)).then_inc(w_load.sem, 16)
                sp.dma_start(woraw, wo.rearrange("(k p) n -> p k n", p=P)).then_inc(w_load.sem, 16)
                if L == 0:
                    sp.dma_start(braw[0:2, :], bqkv0).then_inc(w_load.sem, 16)
                    sp.dma_start(boraw[0:2, :], bo0).then_inc(w_load.sem, 16)
                else:
                    sp.dma_start(GB[:, 0, :], gamma).then_inc(w_load.sem, 16)
                    sp.dma_start(GB[:, 1, :], beta).then_inc(w_load.sem, 16)

            attention_loads(0)
            sp.wait_ge(zero_t, 1)
            zrows = slot_in.rearrange("(c p r) d -> c p (r d)", p=P, r=2)
            for c in range(SLOTS):
                sp.dma_start(zrows[c], zero_rows).then_inc(zeroed, 16)
            for b in range(B):
                for st in STEPS[0]:
                    if st[0] != "ms":
                        continue
                    g, key = st[1], (0, b) + st
                    scratch = max_rows[b * NQ + g, :, :]
                    mt_ready.wait(sp, key)
                    sp.dma_start(scratch, MT[:, :]).then_inc(m_out.sem, 16)
                    m_out.wait(sp, key)
                    for j in range(4):
                        row = STK * (j % 2) + MH
                        sp.dma_start(Q[row:row + 2, 2 * g + j // 2, :].bitcast(F32),
                                     scratch[16 * j:16 * j + 16, :].rearrange("(h i) q -> h (i q)", h=2)
                                     ).then_inc(m_rows.sem, 16)

            st_done.wait(sp, (0, 1, "st", NQ - 1, TB - 1, 3))
            sp.dma_start(WM0[:, :, :], wmod0[:, 3 * D:].rearrange("(k p) n -> p k n", p=P)).then_inc(mod_w.sem, 16)
            sp.dma_start(WG[:, :, :], wg.rearrange("(k p) e -> p k e", p=P)).then_inc(wg_load, 16)

            def slot_rows(s, par):
                sp.dma_start(XT[:, par, :, :], slot_in[bass.ds(s * SLOT, SLOT), :]
                             .rearrange("(a p) d -> p a d", p=P)).then_inc(xs_load[par], 16)

            def slot_weights(s, wait):
                e = sp.value_load(EI[0:1, bass.ds(s, 1)], min_val=0, max_val=E0 - 1)
                for n, w in enumerate((w1, w3, w2)):
                    if wait:
                        sp.wait_ge(ws_hi[n], s * 2)
                        sp.wait_ge(ws_lo[n], s * 2)
                    dst = R13[:, n, :, :] if n < 2 else RW2[:, :, :]
                    sp.dma_start(dst, w[bass.ds(e, 1), :, :].rearrange("a (k p) n -> p (a k) n", p=P)
                                 ).then_inc(wr_load[n], 16)

            def slot_store(s, par):
                sp.wait_ge(y_evac, s + 2)
                sp.dma_start(slot_out[bass.ds(s * SLOT, SLOT), :].rearrange("(a p) d -> p a d", p=P),
                             YO[:, par, :, :]).then_inc(y_out[par], 16)

            sp.wait_ge(idx_ready, 3)
            slot_weights(0, False)
            sp.wait_ge(scattered, 16 * 2 * T)
            slot_rows(0, 0)
            slot_rows(1, 1)
            slot_weights(1, True)
            with sp.Fori(0, (SLOTS - 3) // 2, 1) as i:
                for par in range(2):
                    s = i * 2 + par
                    sp.wait_ge(xs_tr, s + 1)
                    slot_rows(s + 2, par)
                    slot_weights(s + 2, True)
                    slot_store(s, par)
            sp.wait_ge(xs_tr, SLOTS - 2)
            slot_rows(SLOTS - 1, (SLOTS - 1) % 2)
            slot_weights(SLOTS - 1, True)
            for s in range(SLOTS - 3, SLOTS):
                slot_store(s, s % 2)

            sp.wait_ge(dn_mm, SLOTS + 2)
            for par in range(2):
                sp.wait_ge(y_out[par], 16 + 16 * ((SLOTS + 1 - par) // 2))
            attention_loads(1)

            st_done.wait(sp, (1, 1, "st", NQ - 1, TB - 1, 3))
            sp.dma_start(WM1[:, :, :], wmod1[:, 3 * D:].rearrange("(k p) n -> p k n", p=P)).then_inc(mod_w.sem, 16)
            for l in range(L1N):
                sp.dma_start(GR[:, l, :, :], gw1[l].rearrange("(k p) e -> p k e", p=P)).then_inc(gw_load, 16)
            pv_done.wait(sp, (1, 1, "pv", NQ - 1, TB - 1))
            ew_pairs = ew1.rearrange("(n e k p) m -> n k p e m", e=2, k=KC, p=P)
            for par in range(2):
                for k in range(KC):
                    sp.dma_start(ER[:, par, k, :, :], ew_pairs[par, k]).then_inc(er_load[par], 16)
            with sp.Fori(0, L1N * PAIRS // 2 - 1, 1) as i:
                for par in range(2):
                    sp.wait_ge(er_lo, i * 2 + (par + 1))
                    for k in range(KC):
                        sp.dma_start(ER[:, par, k, :, :],
                                     ew_pairs[bass.ds(i * 2 + (2 + par), 1), k, :, :, :]
                                     .rearrange("a p e m -> p (a e) m")).then_inc(er_load[par], 16)
            for t in range(T):
                sp.wait_ge(o_ready, t + 1)
                sp.dma_start(out[t * P:(t + 1) * P, :], OUT_T[:, t % 2, :]).then_inc(stored[t % 2], 16)
            for par in range(2):
                sp.wait_ge(stored[par], 16 * T // 2)

        @block.gpsimd
        def _(pool):
            link = Links(pool, pool_chain)

            def normalised(L, b, t):
                use, x_tile, h = ("A", L, b), b * TB + t, HR[t % 2]
                if t >= 2:
                    tr_done.wait(pool, (use, t - 2))
                link(pool.tensor_scalar(h, X[:, x_tile, :], SM[:, 2, x_tile:x_tile + 1], SM[:, 4, x_tile:x_tile + 1],
                                        ALU.mult, ALU.add))
                scale_tile(pool, use, t, h, link)
                shift_tile(pool, use, t, h)

            def ffn_shifts(n, tile_of, tiles=range(T)):
                use = ("F", n)
                mod_ready.wait(pool, (2 * n + 1, "rows"))
                for t in tiles:
                    scaled.wait(pool, (use, t))
                    shift_tile(pool, use, t, tile_of(t))

            def stage(L, b):
                if b == 0:
                    if L == 1:
                        pool.wait_ge(dn_mm, SLOTS + 2)
                    pool.memset(V[:, :, :, HD:HD + 1], 1.0).then_inc(stage_init.sem, 1)
                    if L == 0:
                        stage_init.wait(pool, (L, "ones"))
                        pool.memset(K[0][STK:P, :, :].bitcast(F32), 0.0).then_inc(stage_init.sem, 1)
                        stage_init.wait(pool, (L, "KA"))
                        pool.memset(K[1][0:STK, :, :].bitcast(F32), 0.0).then_inc(stage_init.sem, 1)
                        stage_init.wait(pool, (L, "KB"))
                else:
                    pv_done.wait(pool, (L, 0, "pv", NQ - 1, TB - 1))
                stats_ready.wait(pool, ("A", L))
                mod_ready.wait(pool, (2 * L, "rows"))
                normalised(L, b, 0)
                if b == 0:
                    w_ready.wait(pool, L)
                    mod_mm.wait(pool, 2 * L)
                for g in range(2):
                    pool.memset(QS[g][:, :, MH:STK], 0.0).then_inc(stage_init.sem, 1)
                    pool.memset(KS[g][:, :, MH:MH + 2], 1.0).then_inc(stage_init.sem, 1)
                    pool.memset(KS[g][:, :, MH + 2:STK], 0.0).then_inc(stage_init.sem, 1)
            def project(L, b):
                stage(L, b)
                for s in range(TB + 2):
                    if s + 1 < TB:
                        normalised(L, b, s + 1)
                    if s >= 2:
                        t = s - 2
                        stage_hi.wait(pool, (L, b, t))
                        src = TQ[t % 2].rearrange("p (a h c) -> p a h c", a=2, h=HN)
                        pool.tensor_tensor(QS[t % 2][:, :, 2 * HD:3 * HD].bitcast(F32R), src[:, 0, :, :], QS[t % 2][:, :, 0:HD],
                                           ALU.subtract).then_inc(stage_lo.sem, 1)
                        pool.tensor_tensor(KS[t % 2][:, :, HD:2 * HD].bitcast(F32R), src[:, 1, :, :], KS[t % 2][:, :, 0:HD],
                                           ALU.subtract).then_inc(stage_lo.sem, 1)

            def mask(L, b):
                for st in STEPS[L]:
                    if st[0] != "st":
                        continue
                    _, g, k, j = st
                    key = (L, b) + st
                    (p_dve if on_vector(L, st) else p_act).wait(pool, key)
                    diag = PR[:, k % 2, j, k * P:(k + 1) * P]
                    pool.affine_select(out=diag, in_=diag, compare_op=ALU.is_ge, fill=0.0, base=0,
                                       pattern=[[1, P]], channel_multiplier=-1).then_inc(p_mask.sem, 1)
                for t in range(TB):
                    gated.wait(pool, (L, b, t))
                    tile = X[:, b * TB + t, :]
                    pool.tensor_tensor(tile, tile, GT2[:, t % 2, :], ALU.add).then_inc(x_new.sem, 1)

            for b in range(B):
                project(0, b)
                mask(0, b)
            ffn_shifts(0, lambda t: HF[:, t, :])
            pool.wait_ge(idx_ready, 3)
            pool.wait_ge(zeroed, 16 * SLOTS)
            for t in range(T):
                for c in range(2):
                    pool.indirect_dma_start(slot_in[:, :], bass.IndirectOffsetOnAxis(ap=IX[:, c, t:t + 1], axis=0),
                                            HF[:, t, :], None).then_inc(scattered, 16)

            def low_slot_weights(s, par):
                pool.wait_ge(dn_mm, s + 1)
                for n in (1, 2):
                    for h, (raw, hi, lo) in enumerate(split_steps(n, par)):
                        pool.wait_ge(ws_hi[n], s * 2 + (h + 1))
                        pool.tensor_tensor(lo, raw, hi.bitcast(F32), ALU.subtract).then_inc(ws_lo[n], 1)

            with pool.Fori(0, (SLOTS - 1) // 2, 1) as i:
                for par in range(2):
                    low_slot_weights(i * 2 + par, par)
            low_slot_weights(SLOTS - 1, 0)
            for par in range(2):
                pool.wait_ge(y_out[par], 16 + 16 * ((SLOTS + 1 - par) // 2))
            for t in range(T):
                if t >= 2:
                    pool.wait_ge(g_used, t - 1)
                for c in range(2):
                    pool.indirect_dma_start(G0[:, t % 2, c, :], None, slot_out[:, :],
                                            bass.IndirectOffsetOnAxis(ap=IX[:, c, t:t + 1], axis=0)
                                            ).then_inc(gathered[t % 2], 16)
            for b in range(B):
                project(1, b)
                mask(1, b)
            x_new.wait(pool, ("A", 1, 1, TB - 1))
            pool.wait_ge(gw_hi, 1)
            pool.tensor_tensor(GWL[:, :, :, :], GR[:, :, :, :], GWH[:, :, :, :].bitcast(F32), ALU.subtract).then_inc(gw_lo, 1)

            def low_pair(n, par):
                pool.wait_ge(er_hi, n + 1)
                pool.wait_ge(ex_mm, n * T + T)
                pool.tensor_tensor(EL[:, par, :, :, :], ER[:, par, :, :, :],
                                   EH[:, par, :, :, :].bitcast(F32), ALU.subtract).then_inc(er_lo, 1)

            ffn_shifts(1, lambda t: HR1[:, t % 2, :], range(0, 6))
            low_pair(0, 0)
            ffn_shifts(1, lambda t: HR1[:, t % 2, :], range(6, T))
            with pool.Fori(0, L1N * PAIRS // 2 - 1, 1) as i:
                for par in (1, 0):
                    low_pair(i * 2 + (2 - par), par)
            low_pair(L1N * PAIRS - 1, 1)

        @block.scalar
        def _(act):
            act.wait_ge(loaded, 48)
            act.activation(CS[:, :, :, :], CS[:, :, :, :], ACT.Silu).then_inc(silu_c, 1)

            def high_weights(L):
                w_load.wait(act, L)
                if L == 1:
                    act.wait_ge(w_folded, 3)
                act.activation(WH[:, :, :], wraw, ACT.Copy).then_inc(w_hi.sem, 1)
                act.activation(WOH[:, :, :], woraw, ACT.Copy).then_inc(w_hi.sem, 1)
                act.activation(BZ[0:2, :], braw[0:2, :], ACT.Copy).then_inc(w_hi.sem, 1)
                if L == 0:
                    act.activation(BOZ[0:2, :], boraw[0:2, :], ACT.Copy).then_inc(w_hi.sem, 1)

            def root(use):
                sq_in.wait(act, use)
                act.activation(SM[:, 1, :], SM[:, 0, :], ACT.Sqrt).then_inc(sq_out.sem, 1)

            def hat(use, t, h):
                if t >= 2 and use == ("F", 1):
                    tr_done.wait(act, (use, t - 2))
                act.activation(h, X[:, t, :], ACT.Identity, bias=SM[:, 4, t:t + 1],
                               scale=SM[:, 2, t:t + 1]).then_inc(x_hat.sem, 1)

            def transposed_hi(use, t):
                tr_done.wait(act, (use, t))
                if use == ("F", 0):
                    if t >= 2:
                        act.wait_ge(lg_mm, t - 1)
                    dst = HG[:, t % 2, :, :]
                elif use == ("F", 1):
                    dst = XH[:, :, t * P:(t + 1) * P]
                else:
                    if t >= 2:
                        qkv_done.wait(act, use[1:] + (t - 2,))
                    dst = HTH[:, t % 2, :, :]
                act.activation(dst, tile_transposed(use, t).rearrange("p (k c) -> p k c", k=KC),
                               ACT.Copy).then_inc(ht_hi.sem, 1)

            def project(L, b):
                if b == 0:
                    root(("A", L))
                stage_init.wait(act, (L, b))
                for s in range(TB + 3):
                    if s < TB:
                        transposed_hi(("A", L, b), s)
                    if L == 1 and 0 <= s - 2 < TB:
                        t = s - 2
                        fm_in.wait(act, (b, t))
                        act.activation(FS[:, 1, :], FS[:, 0, :], ACT.Sqrt).then_inc(fm_out.sem, 1)
                    if 0 <= s - 1 < TB:
                        t = s - 1
                        qkv_done.wait(act, (L, b, t))
                        act.activation(V[:, t, :, 0:HD], tile_v(L, t).rearrange("p (h c) -> p h c", h=HN),
                                       ACT.Copy).then_inc(v_ready.sem, 1)
                        if L == 1:
                            if t >= 2:
                                fm_in.wait(act, (b, t - 2))
                            act.activation(SQ[t % 2], PS[:, 2 + t % 2, :], ACT.Square).then_inc(fm_sq.sem, 1)
                    if 0 <= s - 3 < TB:
                        t = s - 3
                        for h in range(2):
                            stk_tr.wait(act, (L, b, t, "q", h))
                            act.activation(Q[:, 4 * h:4 * h + 4, t * P:(t + 1) * P],
                                           PS[:, 6 + h, :].rearrange("p (a c) -> p a c", a=4),
                                           ACT.Copy).then_inc(stk_q.sem, 1)
                        for h in range(2):
                            stk_tr.wait(act, (L, b, t, "k", h))
                            act.activation(K[0][0:STK, 4 * h:4 * h + 4, t * P:(t + 1) * P],
                                           PS[0:STK, 6 + h, :].rearrange("p (a c) -> p a c", a=4),
                                           ACT.Copy).then_inc(stk_ka.sem, 1)
                    if 0 <= s - 2 < TB:
                        t = s - 2
                        q_ready.wait(act, (L, b, t))
                        if t >= 2:
                            stk_tr.wait(act, (L, b, t - 2, "k", 1))
                        src = TQ[t % 2].rearrange("p (a h c) -> p a h c", a=2, h=HN)
                        for a, dst in ((0, QS[t % 2][:, :, 0:2 * HD].rearrange("p h (r c) -> p h r c", r=2)),
                                       (1, KS[t % 2][:, :, 0:4 * HD].rearrange("p h (r c) -> p h r c", r=4)[:, :, 0:3:2, :])):
                            act.activation(dst.bitcast(F32R), src[:, a, :, None, :].to_broadcast([P, HN, 2, HD]),
                                           ACT.Copy).then_inc(stage_hi.sem, 1)

            def attend(L, b):
                for st in STEPS[L]:
                    key = (L, b) + st
                    if st[0] == "st" and not on_vector(L, st):
                        _, g, k, j = st
                        st_done.wait(act, key)
                        if g or k >= 2:
                            pv_done.wait(act, (L, b, "pv") + ((g, k - 2) if k >= 2 else (g - 1, k + 6)))
                        else:
                            stk_kb.wait(act, (L, b, TB - 1, 1))
                        src = PS[:, bank[key]:bank[key] + 2, :].rearrange("p a c -> p (a c)")[:, k * P:S]
                        act.activation(PR[:, k % 2, j, k * P:S], src, ACT.Exp if L == 0 else ACT.Square,
                                       scale=1.0 if L else 0.25).then_inc(p_act.sem, 1)
                    if st[0] == "pv" and st[2] == TB - 1:
                        pv_done.wait(act, key)
                        if st[1] > 0:
                            o_tr.wait(act, (L, b, "otr", st[1] - 1, 1))
                        if key == (0, 0, "pv", 0, TB - 1):
                            act.wait_ge(zeroed, 16 * SLOTS)
                        act.activation(OT[:, :], PS[:, 4:6, :].rearrange("p a c -> p (a c)"),
                                       ACT.Copy).then_inc(o_evac.sem, 1)
                for t in range(TB):
                    on_tr.wait(act, (L, b, t))
                    if t >= 2:
                        pr_done.wait(act, (L, b, t - 2))
                    act.activation(HTH[:, t % 2, :, :],
                                   PS[:, bank[(L, b, "ont", t)], 0:D].rearrange("p (k c) -> p k c", k=KC),
                                   ACT.Copy).then_inc(ont_hi.sem, 1)

            act.wait_ge(cvt, 5)
            high_weights(0)
            for L, b in UNITS[:2]:
                project(L, b)
                attend(L, b)

            root(("F", 0))
            stats_ready.wait(act, ("F", 0))
            for t in range(T + 4):
                if t < T:
                    hat(("F", 0), t, HF[:, t, :])
                if t >= 4:
                    transposed_hi(("F", 0), t - 4)
            act.wait_ge(gate_in, 1)
            act.activation(WT[:, 0, :], WT[:, 1, :], ACT.Exp).then_inc(gate_exp, 1)

            def high_slot_weights(s, par, n, h):
                act.wait_ge(wr_load[n], s * 16 + 16)
                act.wait_ge(dn_mm, s + 1)
                raw, hi, _ = split_steps(n, par)[h]
                act.activation(hi, raw, ACT.Copy).then_inc(ws_hi[n], 1)

            def high_slot_rows(s, par):
                act.wait_ge(xs_tr, s + 1)
                act.activation(XTH[:, par, :, :], PS[:, 6, :].rearrange("p (k c) -> p k c", k=KC), ACT.Copy).then_inc(xs_hi, 1)

            def hidden_silu(s, c):
                act.wait_ge(up_mm, s * HC + (c + 1))
                act.activation(SI[:, c % 2, :], PS[:, c % 4, 0:SLOT], ACT.Silu).then_inc(up_silu, 1)

            def hidden_high(s, c):
                act.wait_ge(up_gate, s * HC + (c + 1))
                act.activation(HH[:, c, :], GG[:, c % 3, :], ACT.Copy).then_inc(up_hi, 1)

            for n in range(3):
                for h in range(2):
                    high_slot_weights(0, 0, n, h)
            high_slot_rows(0, 0)
            with act.Fori(0, (SLOTS - 1) // 2, 1) as i:
                for par in range(2):
                    s = i * 2 + par
                    for c in range(HC):
                        hidden_silu(s, c)
                        if c:
                            hidden_high(s, c - 1)
                        if c < 6:
                            high_slot_weights(s + 1, (par + 1) % 2, c // 2, c % 2)
                        if c == 4:
                            high_slot_rows(s + 1, (par + 1) % 2)
                    hidden_high(s, HC - 1)
            for c in range(HC):
                hidden_silu(SLOTS - 1, c)
                if c:
                    hidden_high(SLOTS - 1, c - 1)
            hidden_high(SLOTS - 1, HC - 1)

            act.wait_ge(zero_t, 2)
            for t in range(T):
                act.wait_ge(gathered[t % 2], 32 * (t // 2 + 1))
                if t >= 2:
                    act.wait_ge(g_used, t - 1)
                act.activation(GT[:, t % 2, :], G0[:, t % 2, 0, :], ACT.Copy, scale=W01[:, 0, t:t + 1]).then_inc(g_first, 1)
                if t == 7:
                    high_weights(1)
                rows = (slice(STK, P), slice(0, STK))[t % 2]
                act.activation(K[t % 2][rows, t // 2, :].rearrange("p (a c) -> p a c", a=2),
                               zero_rows[rows, None, :].to_broadcast([STK, 2, 2 * D]), ACT.Copy)
            for L, b in UNITS[2:]:
                project(L, b)
                attend(L, b)
            act.wait_ge(gw_load, 16 * L1N)
            act.activation(GWH[:, :, :, :], GR[:, :, :, :], ACT.Copy).then_inc(gw_hi, 1)

            def high_pair(n, par, count):
                act.wait_ge(er_load[par], count)
                act.wait_ge(ex_mm, n * T + T)
                act.activation(EH[:, par, :, :, :], ER[:, par, :, :, :], ACT.Copy).then_inc(er_hi, 1)

            def gate_evac(l, c):
                gt_mm.wait(act, (l, c))
                if l:
                    gt_tr.wait(act, (l - 1, c))
                act.activation(LT[:, c * 512:(c + 1) * 512], PS[0:E1, 6, :], ACT.Copy).then_inc(gt_evac.sem, 1)

            def gate_exp_(l, c):
                gt_max.wait(act, (l, c))
                tiles = EX[:, 4 * c:4 * c + 4, :]
                act.activation(tiles, tiles, ACT.Exp).then_inc(gt_exp.sem, 1)

            def layer_input_hi(l, t):
                ln_tr.wait(act, (l, t))
                act.activation(XH[:, :, t * P:(t + 1) * P], PS[:, t % 2, 0:D].rearrange("p (k c) -> p k c", k=KC),
                               ACT.Copy).then_inc(ln_hi.sem, 1)

            root(("F", 1))
            high_pair(0, 0, 32)
            stats_ready.wait(act, ("F", 1))
            run_between(None, {"hat": lambda t: hat(("F", 1), t, HR1[:, t % 2, :]),
                               "hi": lambda t: transposed_hi(("F", 1), t),
                               "evac": lambda c: gate_evac(0, c), "exp": lambda c: gate_exp_(0, c)})
            for l in range(L1N):
                with act.Fori(0, PAIRS // 2 - 1, 1) as i:
                    for par in range(2):
                        high_pair(i * 2 + (l * PAIRS + 1 + par), 1 - par, i * 32 + 32 * (l * PAIRS // 2 + 1 + par))
                high_pair(l * PAIRS + PAIRS - 1, 1, 32 * (l + 1) * PAIRS // 2)
                if l < L1N - 1:
                    high_pair((l + 1) * PAIRS, 0, 32 * ((l + 1) * PAIRS // 2 + 1))
                    run_between(l, {"hi": lambda t: layer_input_hi(l, t), "evac": lambda c: gate_evac(l + 1, c),
                                    "exp": lambda c: gate_exp_(l + 1, c)})

        @block.vector
        def _(dve):
            link = Links(dve, chain)

            dve.sem_inc(ev_b, T)
            dve.sem_inc(y_evac, 1)
            dve.memset(zero_rows, 0.0).then_inc(zero_t, 1)
            dve.memset(PS[:, 4:6, :], 0.0).then_inc(psum_zero, 1)
            dve.memset(BZ[:, :].bitcast(F32), 0.0).then_inc(cvt, 1)
            dve.memset(BOZ[:, :].bitcast(F32), 0.0).then_inc(cvt, 1)
            dve.memset(MP[:, :, :, :], -BIG).then_inc(cvt, 1)
            dve.wait_ge(loaded, 48)
            dve.tensor_copy(IDB[:, :], ident).then_inc(cvt, 1)
            dve.tensor_copy(MQB[:, :], CST[:, C_MQ:C_MQ + P]).then_inc(cvt, 1)
            dve.tensor_copy(BE[:, :], CST[:, C_BE:C_BE + P]).then_inc(cvt, 1)
            dve.wait_ge(silu_c, 1)

            def spread(L):
                dve.tensor_copy(CB[:, :, :, :].rearrange("p k b c -> p (k b) c"),
                                CS[:, L, :, :].rearrange("p k b -> p (k b)")[:, :, None].to_broadcast([P, KC * B, P])
                                ).then_inc(cb_ready, 1)

            def modulation_of(b):
                return PS[:, 2 + 2 * b:4 + 2 * b, :].rearrange("p a c -> p (a c)")

            def modulation_rows(n):
                mod_mm.wait(dve, n)
                for b in range(B):
                    src = modulation_of(b)
                    dve.tensor_copy(MOD[:, b, 0:D], src[:, 0:D]).then_inc(mod_ready.sem, 1)
                    dve.tensor_scalar(MOD[:, b, D:2 * D], src[:, D:2 * D], 1.0, None, ALU.add).then_inc(mod_ready.sem, 1)
                mod_ready.wait(dve, (n, "rows"))

            def modulation_gate(n, batches=range(B)):
                for b in batches:
                    gate = modulation_of(b)[:, 2 * D:3 * D]
                    dve.tensor_scalar(GT2[:, 1, :], gate, 0.0, 2.0, ALU.is_ge, ALU.mult)
                    link(dve.tensor_scalar(GT2[:, 0, :], gate, -1.0, None, ALU.mult))
                    link(dve.tensor_tensor(GT2[:, 0, :], gate, GT2[:, 0, :], ALU.max))
                    link(dve.tensor_scalar(GT2[:, 0, :], GT2[:, 0, :], 0.25, None, ALU.max))
                    dve.scalar_tensor_tensor(out=MOD[:, b, 2 * D:3 * D], in0=GT2[:, 1, :], scalar=-1.0,
                                             in1=GT2[:, 0, :], op0=ALU.add, op1=ALU.mult).then_inc(mod_ready.sem, 1)
                    mod_ready.wait(dve, (n, b))

            def fold_feature_map():
                w_load.wait(dve, 1)
                heads = {k: wraw[:, k, 0:2 * D].rearrange("p (h c) -> p h c", c=HD) for k in range(KC)}
                for k in range(KC):
                    link(dve.tensor_tensor(heads[k], heads[k], GB[:, 0, None, :].to_broadcast([P, 2 * HN, HD]), ALU.mult))
                    link(dve.tensor_reduce(FS[:, k, :], heads[k], AX_X, ALU.add))
                    dve.scalar_tensor_tensor(out=heads[k], in0=FS[:, k, :, None].to_broadcast([P, 2 * HN, HD]), scalar=-1.0 / HD,
                                             in1=heads[k], op0=ALU.mult, op1=ALU.add).then_inc(w_folded, 1)
                dve.memset(BZ[:, :].bitcast(F32), 0.0)
                dve.memset(braw[0:2, 2 * D:3 * D], 0.0)
                link(dve.tensor_reduce(FS[:, KC, 0:1], GB[:, 1, :], AX_X, ALU.add))
                link(dve.tensor_scalar(FS[:, KC, 1:2], FS[:, KC, 0:1], -1.0 / HD, None, ALU.mult))
                dve.tensor_scalar(braw[0:2, 0:2 * D].rearrange("p (h c) -> p h c", c=HD),
                                  GB[0:2, 1, None, :].to_broadcast([2, 2 * HN, HD]), FS[0:2, KC, 1:2], None,
                                  ALU.add).then_inc(w_folded, 1)

            def low_weights(L):
                w_hi.wait(dve, L)
                dve.tensor_tensor(WL[:, :, :], wraw, WH[:, :, :].bitcast(F32), ALU.subtract).then_inc(w_ready.sem, 1)
                dve.tensor_tensor(WOL[:, :, :], woraw, WOH[:, :, :].bitcast(F32), ALU.subtract).then_inc(w_ready.sem, 1)
                for dst, raw in ((BZ, braw), (BOZ, boraw))[:2 - L]:
                    dve.scalar_tensor_tensor(out=dst[0:2, :], in0=dst[0:2, :].bitcast(F32), scalar=CST[0:2, C_SC:C_SC + 1],
                                             in1=raw[0:2, :], op0=ALU.mult, op1=ALU.add).then_inc(w_ready.sem, 1)

            def refine(y, v, tmp):
                link(dve.tensor_tensor(tmp, y, y, ALU.mult))
                link(dve.tensor_tensor(tmp, tmp, v, ALU.mult))
                link(dve.tensor_scalar(tmp, tmp, -0.5, 1.5, ALU.mult, ALU.add))
                link(dve.tensor_tensor(y, y, tmp, ALU.mult))

            def tile_statistics(t):
                link(dve.bn_stats(STAT[:, t, :], X[:, t, :]))
                link(dve.bn_aggr(MV[:, t, :], STAT[:, t, :]))

            def statistics(use):
                dve.tensor_scalar(SM[:, 0, :], MV[:, :, 1], LN_EPS, None, ALU.add).then_inc(sq_in.sem, 1)
                sq_out.wait(dve, use)
                link(dve.reciprocal(SM[:, 2, :], SM[:, 1, :]))
                refine(SM[:, 2, :], SM[:, 0, :], SM[:, 3, :])
                dve.scalar_tensor_tensor(out=SM[:, 4, :], in0=MV[:, :, 0], scalar=-1.0, in1=SM[:, 2, :],
                                         op0=ALU.mult, op1=ALU.mult).then_inc(stats_ready.sem, 1)
                stats_ready.wait(dve, use)

            def ffn_scale(n, t, h):
                x_hat.wait(dve, (("F", n), t))
                scale_tile(dve, ("F", n), t, h, lambda ins: ins.then_inc(scaled.sem, 1))

            def transposed_lo(use, t):
                ht_hi.wait(dve, (use, t))
                hi, lo = ((XH[:, :, t * P:(t + 1) * P], XL[:, :, t * P:(t + 1) * P]) if use == ("F", 1)
                          else (HTH[:, t % 2, :, :], HTL[:, t % 2, :, :]))
                dve.tensor_tensor(lo, tile_transposed(use, t).rearrange("p (k c) -> p k c", k=KC), hi.bitcast(F32),
                                  ALU.subtract).then_inc(ht_lo.sem, 1)

            def rotate(b, t):
                qkv_done.wait(dve, (0, b, t))
                if t:
                    q_ready.wait(dve, (0, b, t - 1))
                src = PS[:, 2 + t % 2, :].rearrange("p (h c) -> p h c", c=HD)
                cos = CST[:, C_COS + t * HD:C_COS + (t + 1) * HD]
                sin = CST[:, C_SIN + t * HD:C_SIN + (t + 1) * HD]
                dve.tensor_tensor(TA.rearrange("p (h c) -> p h c", c=HD), src,
                                  cos[:, None, :].to_broadcast([P, 2 * HN, HD]), ALU.mult)
                tb = TB_.rearrange("p (h c) -> p h c", c=HD)
                for o in range(2):
                    last = dve.tensor_tensor(tb[:, :, o:HD:2], src[:, :, 1 - o:HD:2],
                                             sin[:, None, o:HD:2].to_broadcast([P, 2 * HN, HD // 2]), ALU.mult)
                link(last)
                dve.tensor_tensor(TQ[t % 2], TA, TB_, ALU.add).then_inc(q_ready.sem, 1)

            def feature_map(b, t):
                fm_sq.wait(dve, (b, t))
                link(dve.tensor_reduce(FS[:, 3, :], SQ[t % 2].rearrange("p (h c) -> p h c", c=HD), AX_X, ALU.add))
                dve.tensor_scalar(FS[:, 0, :], FS[:, 3, :], 1.0 / HD, LN_EPS, ALU.mult, ALU.add).then_inc(fm_in.sem, 1)
                fm_out.wait(dve, (b, t))
                link(dve.reciprocal(FS[:, 4, :], FS[:, 1, :]))
                refine(FS[:, 4, :], FS[:, 0, :], FS[:, 5, :])
                link(dve.tensor_scalar(FS[:, 4, 0:HN], FS[:, 4, 0:HN], 0.25, None, ALU.mult))
                dve.tensor_tensor(TQ[t % 2].rearrange("p (h c) -> p h c", c=HD),
                                  PS[:, 2 + t % 2, :].rearrange("p (h c) -> p h c", c=HD),
                                  FS[:, 4, :, None].to_broadcast([P, 2 * HN, HD]), ALU.mult).then_inc(q_ready.sem, 1)

            def maxima(L, b, st):
                _, g, i, j = st
                for c, (c0, w) in enumerate(max_chunks(i)):
                    key = (L, b) + st + (c,)
                    max_mm.wait(dve, key)
                    dve.tensor_reduce(MP[:, j, i, c:c + 1], PS[:, bank[key], 0:w], AX_X, ALU.max).then_inc(max_red.sem, 1)
                return key

            def project(L, b):
                use = ("A", L, b)
                stage_init.wait(dve, (L, b))
                for s in range(TB + 4):
                    if s < TB:
                        if s >= 2:
                            qkv_done.wait(dve, (L, b, s - 2))
                        transposed_lo(use, s)
                    for st in early_maxes(L, s, 0):
                        maxima(L, b, st)
                    if 0 <= s - 2 < TB:
                        (feature_map if L else rotate)(b, s - 2)
                    for st in early_maxes(L, s, 1):
                        maxima(L, b, st)
                    if 0 <= s - 3 < TB:
                        t = s - 3
                        for h in range(2):
                            stk_tr.wait(dve, (L, b, t, "k", h))
                            dve.tensor_copy(K[1][STK:P, 4 * h:4 * h + 4, t * P:(t + 1) * P],
                                            PS[STK:P, 6 + h, :].rearrange("p (a c) -> p a c", a=4)).then_inc(stk_kb.sem, 1)

            def attend(L, b):
                last_max = (L, b, "max", 0, TB - 1, 3, 1)
                for st in STEPS[L]:
                    key = (L, b) + st
                    if st[0] == "max":
                        last_max = maxima(L, b, st)
                    elif st[0] == "msc":
                        g = st[1]
                        max_red.wait(dve, last_max)
                        link(dve.tensor_reduce(MX[:, 0, :, :], MP[:, :, :, :], AX_X, ALU.max))
                        link(dve.tensor_scalar(MX[:, 1, :, :], MX[:, 0, :, :], -1.0, None, ALU.mult))
                        link(dve.tensor_copy(MS[:, :, 0, :].bitcast(F32R), MX[:, 1, :, :]))
                        dve.tensor_tensor(MS[:, :, 1, :].bitcast(F32R), MX[:, 1, :, :], MS[:, :, 0, :],
                                          ALU.subtract).then_inc(ms_ready.sem, 1)
                    elif st[0] == "ms":
                        ms_tr.wait(dve, key)
                        if b or st[1]:
                            m_out.wait(dve, (L, b, "ms", st[1] - 1) if st[1] else (L, 0, "ms", NQ - 1))
                        dve.tensor_copy(MT[:, :], PS[0:64, bank[key], 0:P]).then_inc(mt_ready.sem, 1)
                    if b == 1 and st[0] == "st" and st[1] == NQ - 1 and st[3] == 0:
                        tile_statistics(st[2])
                    if st[0] == "st" and on_vector(L, st):
                        _, g, k, j = st
                        st_done.wait(dve, key)
                        if g or k >= 2:
                            pv_done.wait(dve, (L, b, "pv") + ((g, k - 2) if k >= 2 else (g - 1, k + 6)))
                        else:
                            stk_ka.wait(dve, (L, b, TB - 1, 1))
                        src = PS[:, bank[key]:bank[key] + 2, :].rearrange("p a c -> p (a c)")[:, k * P:S]
                        dst = PR[:, k % 2, j, k * P:S]
                        link(dve.tensor_copy(dst, src))
                        dve.tensor_tensor(dst, src, dst, ALU.mult).then_inc(p_dve.sem, 1)
                    if st[0] == "otr":
                        _, g, half = st
                        o_tr.wait(dve, key)
                        if g or half:
                            on_ready.wait(dve, (L, b, "otr") + ((g, 0) if half else (g - 1, 1)))
                        src = PS[:, bank[key], :].rearrange("p (t j c) -> p t j c", t=4, j=4)
                        sums = src[:, :, :, HD:HD + 1].rearrange("p t j a -> p t (j a)")
                        rc = RC[:, 0, :].rearrange("p (t j) -> p t j", t=4)
                        if L == 1:
                            link(dve.tensor_scalar(RC[:, 1, :].rearrange("p (t j) -> p t j", t=4), sums, Z_EPS, None, ALU.add))
                            sums = RC[:, 1, :].rearrange("p (t j) -> p t j", t=4)
                        link(dve.reciprocal(rc, sums))
                        dve.tensor_tensor(ON[:, 4 * half:4 * half + 4, 64 * g:64 * g + 64].rearrange("p t (j c) -> p t j c", j=4),
                                          src[:, :, :, 0:HD], rc[:, :, :, None].to_broadcast([P, 4, 4, HD]),
                                          ALU.mult).then_inc(on_ready.sem, 1)
                for t in range(TB + 3):
                    if t < TB:
                        ont_hi.wait(dve, (L, b, t))
                        dve.tensor_tensor(HTL[:, t % 2, :, :],
                                          PS[:, bank[(L, b, "ont", t)], 0:D].rearrange("p (k c) -> p k c", k=KC),
                                          HTH[:, t % 2, :, :].bitcast(F32), ALU.subtract).then_inc(ont.sem, 1)
                    if 1 <= t <= TB:
                        pr_done.wait(dve, (L, b, t - 1))
                        if t >= 3:
                            x_new.wait(dve, ("A", L, b, t - 3))
                        dve.tensor_tensor(GT2[:, (t - 1) % 2, :], PS[:, (t - 1) % 2, 0:D], MOD[:, b, 2 * D:3 * D],
                                          ALU.mult).then_inc(gated.sem, 1)
                    if b == 1 and t >= 3:
                        x_new.wait(dve, ("A", L, b, t - 3))
                        tile_statistics(TB + t - 3)

            spread(0)
            dve.wait_ge(x_load, 16)
            for t in range(T):
                last = dve.bn_stats(STAT[:, t, :], X[:, t, :])
            link(last)
            for t in range(T):
                last = dve.bn_aggr(MV[:, t, :], STAT[:, t, :])
            link(last)
            modulation_rows(0)
            statistics(("A", 0))
            low_weights(0)
            modulation_gate(0)
            for L, b in UNITS[:2]:
                project(L, b)
                attend(L, b)

            statistics(("F", 0))
            modulation_rows(1)
            for t in range(T):
                ffn_scale(0, t, HF[:, t, :])
            spread(1)
            dve.memset(LG[:, :, :], BIG)
            dve.memset(R1[:, :, :], BIG)
            dve.memset(R2[:, :, :], BIG)
            dve.memset(PRE[:, :, :], 0.0)
            link(dve.memset(OF[:, :], 0.0))
            modulation_gate(1)
            dve.wait_ge(lg_mm, T)
            link(dve.tensor_copy(LG[:, :, 0:E0], PS[:, 6, 0:T * E0].rearrange("p (t e) -> p t e", t=T)))
            for t in range(T):
                last = dve.max(T8[:, t, :], LG[:, t, 0:E0])
            link(last)
            dve.tensor_copy(R2[:, :, 0:2], T8[:, :, 0:2])
            dve.tensor_copy(R1[:, :, 0:1], T8[:, :, 0:1])
            link(dve.tensor_tensor(WT[:, 1, :], T8[:, :, 1], T8[:, :, 0], ALU.subtract))
            dve.tensor_copy(WT[:, 1, :], WT[:, 1, :]).then_inc(gate_in, 1)
            for t in range(T):
                dve.match_replace(RP[:, t, :], R2[:, t, :], LG[:, t, :], -BIG)
                last = dve.match_replace(RP1[:, t, :], R1[:, t, :], LG[:, t, :], -BIG)
            link(last)
            dve.tensor_tensor(MM[:, :, :], RP[:, :, 0:E0], LG[:, :, 0:E0], ALU.not_equal).then_inc(route_in, 1)
            link(dve.tensor_tensor(A0[:, :, :], RP1[:, :, 0:E0], LG[:, :, 0:E0], ALU.not_equal))
            dve.wait_ge(route_in, 1)
            link(dve.tensor_tensor(A1[:, :, :], MM[:, :, :], A0[:, :, :], ALU.subtract))
            dve.wait_ge(gate_exp, 1)
            link(dve.tensor_scalar(WT[:, 1, :], WT[:, 0, :], 1.0, None, ALU.add))
            link(dve.reciprocal(W01[:, 0, :], WT[:, 1, :]))
            link(dve.tensor_tensor(W01[:, 1, :], W01[:, 0, :], WT[:, 0, :], ALU.mult))
            dve.wait_ge(route_mm, 1)
            dve.tensor_copy(WIN[:, :, :], PS[:, 7, 0:T * E0].rearrange("p (t e) -> p t e", t=T))
            link(dve.tensor_copy(TOT[:, :, :], PS[:, 7, P:P + T * E0].rearrange("p (t e) -> p t e", t=T)))
            for t in range(T):
                link(dve.tensor_tensor(PRE[:, t + 1, :], PRE[:, t, :], TOT[:, t, :], ALU.add))
            link(dve.tensor_tensor(CMP[:, :, :], PRE[:, T, :, None].to_broadcast([P, E0, 8]),
                                   CST[:, None, C_THR:C_THR + 8].to_broadcast([P, E0, 8]), ALU.is_gt))
            link(dve.tensor_reduce(NT[:, :], CMP[:, :, :], AX_X, ALU.add))
            for e in range(E0):
                link(dve.tensor_tensor(OF[:, e + 1:e + 2], OF[:, e:e + 1], NT[:, e:e + 1], ALU.add))
            link(dve.tensor_tensor(POS[:, :, :], WIN[:, :, :], PRE[:, 0:T, :], ALU.add))
            link(dve.scalar_tensor_tensor(out=POS[:, :, :], in0=OF[:, None, 0:E0].to_broadcast([P, T, E0]), scalar=float(SLOT),
                                          in1=POS[:, :, :], op0=ALU.mult, op1=ALU.add))
            dve.tensor_tensor(PA[:, 0, :, :], POS[:, :, :], A0[:, :, :], ALU.mult)
            link(dve.tensor_tensor(PA[:, 1, :, :], POS[:, :, :], A1[:, :, :], ALU.mult))
            link(dve.tensor_reduce(PF[:, :, :], PA[:, :, :, :], AX_X, ALU.add))
            dve.tensor_copy(IX[:, :, :], PF[:, :, :]).then_inc(idx_ready, 1)
            link(dve.tensor_tensor(SE[:, :, :], CST[:, C_SLOT:C_SLOT + 24, None].to_broadcast([P, 24, E0]),
                                   OF[:, None, 1:E0 + 1].to_broadcast([P, 24, E0]), ALU.is_ge))
            link(dve.tensor_reduce(EF[:, :], SE[:, :, :], AX_X, ALU.add))
            dve.tensor_scalar(EF[:, :], EF[:, :], float(E0 - 1), None, ALU.min).then_inc(idx_ready, 1)
            dve.wait_ge(idx_ready, 2)
            dve.tensor_copy(EI[:, :], EF[:, :]).then_inc(idx_ready, 1)

            def low_slot_weights(s, par, h):
                dve.wait_ge(ws_hi[0], s * 2 + (h + 1))
                raw, hi, lo = split_steps(0, par)[h]
                dve.tensor_tensor(lo, raw, hi.bitcast(F32), ALU.subtract).then_inc(ws_lo[0], 1)

            def low_slot_rows(s, par):
                dve.wait_ge(xs_hi, s + 1)
                dve.tensor_tensor(XTL[:, par, :, :], PS[:, 6, :].rearrange("p (k c) -> p k c", k=KC),
                                  XTH[:, par, :, :].bitcast(F32), ALU.subtract).then_inc(xs_lo, 1)

            def hidden_gate(s, c):
                dve.wait_ge(up_silu, s * HC + (c + 1))
                if c >= 3:
                    dve.wait_ge(up_lo, s * HC + (c - 2))
                dve.tensor_tensor(GG[:, c % 3, :], PS[:, c % 4, SLOT:2 * SLOT], SI[:, c % 2, :], ALU.mult).then_inc(up_gate, 1)

            def hidden_low(s, c):
                dve.wait_ge(up_hi, s * HC + (c + 1))
                dve.tensor_tensor(HL[:, c, :], GG[:, c % 3, :], HH[:, c, :].bitcast(F32), ALU.subtract).then_inc(up_lo, 1)

            def slot_output(s, par, pair):
                dve.wait_ge(dn_mm, s + 3)
                dve.wait_ge(y_out[par], pair * 16 + 16)
                dve.tensor_copy(YO[:, par, :, :], PS[:, 4:6, 0:D]).then_inc(y_evac, 1)

            low_slot_weights(0, 0, 0)
            low_slot_weights(0, 0, 1)
            low_slot_rows(0, 0)
            with dve.Fori(0, (SLOTS - 1) // 2, 1) as i:
                for par in range(2):
                    s = i * 2 + par
                    for c in range(HC):
                        hidden_gate(s, c)
                        if c >= 2:
                            hidden_low(s, c - 2)
                        if c in (2, 3):
                            low_slot_weights(s + 1, (par + 1) % 2, c - 2)
                        if c == 5:
                            low_slot_rows(s + 1, (par + 1) % 2)
                    hidden_low(s, HC - 2)
                    hidden_low(s, HC - 1)
                    slot_output(s, par, i)
            for c in range(HC):
                hidden_gate(SLOTS - 1, c)
                if c >= 2:
                    hidden_low(SLOTS - 1, c - 2)
            hidden_low(SLOTS - 1, HC - 2)
            hidden_low(SLOTS - 1, HC - 1)
            slot_output(SLOTS - 1, 0, SLOTS // 2)
            dve.memset(zero_rows, 0.0).then_inc(zero_t, 1)
            for t in range(T):
                dve.wait_ge(gathered[t % 2], 32 * (t // 2 + 1))
                dve.wait_ge(g_first, t + 1)
                if t >= 2:
                    x_new.wait(dve, ("F", 0, t - 2))
                dve.scalar_tensor_tensor(out=GT2[:, 1, :], in0=G0[:, t % 2, 1, :], scalar=W01[:, 1, t:t + 1], in1=GT[:, t % 2, :],
                                         op0=ALU.mult, op1=ALU.add).then_inc(g_used, 1)
                dve.wait_ge(g_used, t + 1)
                link(dve.tensor_tensor(GT2[:, 0, :], GT2[:, 1, :], MOD[:, t // TB, 2 * D:3 * D], ALU.mult))
                dve.tensor_tensor(X[:, t, :], X[:, t, :], GT2[:, 0, :], ALU.add).then_inc(x_new.sem, 1)
                x_new.wait(dve, ("F", 0, t))
                tile_statistics(t)
                if t == 2:
                    modulation_rows(2)
                if t == 4:
                    fold_feature_map()
                if t == 9:
                    low_weights(1)

            statistics(("A", 1))
            modulation_gate(2)
            for L, b in UNITS[2:]:
                project(L, b)
                attend(L, b)
            statistics(("F", 1))
            modulation_rows(3)
            def gate_top(l, c):
                gt_tr.wait(dve, (l, c))
                tiles = slice(4 * c, 4 * c + 4)
                dve.tensor_copy(LGT[:, tiles, :], PS[:, 7, 0:4 * E1].rearrange("p (t e) -> p t e", t=4)).then_inc(gt_read.sem, 1)
                gt_read.wait(dve, (l, c))
                for t in range(4 * c, 4 * c + 4):
                    last = dve.max(M8[:, t, :], LGT[:, t, :])
                link(last)
                dve.tensor_tensor(EX[:, tiles, :], LGT[:, tiles, :], M8[:, tiles, 0:1].to_broadcast([P, 4, E1]),
                                  ALU.subtract).then_inc(gt_max.sem, 1)
                for t in range(4 * c, 4 * c + 4):
                    last = dve.match_replace(RPL[:, t, :], M8[:, t, :], LGT[:, t, :], -BIG)
                link(last)
                dve.tensor_tensor(MK[:, tiles, :], RPL[:, tiles, :], LGT[:, tiles, :], ALU.not_equal)

            def gate_weights(l, c):
                gt_exp.wait(dve, (l, c))
                tiles = slice(4 * c, 4 * c + 4)
                link(dve.tensor_reduce(SU[:, 0, tiles], EX[:, tiles, :], AX_X, ALU.add))
                link(dve.reciprocal(SU[:, 1, tiles], SU[:, 0, tiles]))
                weights = WD[:, l % 2, tiles, :]
                link(dve.tensor_tensor(weights, EX[:, tiles, :], MK[:, tiles, :], ALU.mult))
                link(dve.tensor_tensor(weights, weights, SU[:, 1, tiles, None].to_broadcast([P, 4, E1]), ALU.mult))

            def accumulate(l, n, weights, e, t, first=False):
                if e == 0:
                    dve.wait_ge(ex_mm, n * T + (2 * T + t + 1))
                    dve.wait_ge(ev_b, n * T + (t + 1))
                else:
                    dve.wait_ge(ev_a, n * T + (t + 1))
                acc = AC[:, l % 2, t, :]
                if first:
                    dve.tensor_scalar(acc, PS[:, 2 + t % 4, 0:D], weights[:, t, 0:1], None, ALU.mult).then_inc(ev_a, 1)
                    return
                dve.scalar_tensor_tensor(out=acc, in0=PS[:, 2 + t % 4, e * D:(e + 1) * D],
                                         scalar=weights[:, t, e:e + 1], in1=acc, op0=ALU.mult,
                                         op1=ALU.add).then_inc((ev_a, ev_b)[e], 1)

            def pair_weights(l, pair, par, first):
                dve.tensor_copy(WP[:, par, :, :], WD[:, l % 2, :, bass.ds(first, 2)]).then_inc(wp_ready, 1)
                dve.wait_ge(wp_ready, pair)

            def layer_input_lo(l, t):
                ln_hi.wait(dve, (l, t))
                dve.tensor_tensor(XL[:, :, t * P:(t + 1) * P], PS[:, t % 2, 0:D].rearrange("p (k c) -> p k c", k=KC),
                                  XH[:, :, t * P:(t + 1) * P].bitcast(F32), ALU.subtract).then_inc(ln_lo.sem, 1)

            def next_parts(l):
                weights = WD[:, l % 2, :, 0:2]

                def first_evac(t):
                    accumulate(l, l * PAIRS, weights, 0, t, first=True)

                return {"top": lambda c: gate_top(l, c), "weights": lambda c: gate_weights(l, c),
                        "next_evac0": first_evac, "next_evac1": lambda t: accumulate(l, l * PAIRS, weights, 1, t)}

            def result(t):
                dve.wait_ge(ev_b, (L1N * PAIRS - 1) * T + T + t + 1)
                if t >= 2:
                    dve.wait_ge(stored[t % 2], 16 * (t // 2))
                link(dve.tensor_tensor(GT2[:, t % 2, :], AC[:, (L1N - 1) % 2, t, :], MOD[:, t // TB, 2 * D:3 * D], ALU.mult))
                dve.tensor_tensor(OUT_T[:, t % 2, :], X[:, t, :], GT2[:, t % 2, :], ALU.add).then_inc(o_ready, 1)

            def normalise(t):
                ffn_scale(1, t, HR1[:, t % 2, :])
                if t in (3, 6):
                    modulation_gate(3, [t // 6])

            run_between(None, {"normalise": normalise,
                               "lo": lambda t: transposed_lo(("F", 1), t), **next_parts(0)})
            for l in range(L1N):
                with dve.Fori(0, PAIRS // 2 - 1, 1) as i:
                    for par in (1, 0):
                        n = i * 2 + (l * PAIRS + 2 - par)
                        pair_weights(l, i * 2 + (l * (PAIRS - 1) + 2 - par), par, i * 4 + 2 * (2 - par))
                        for s in range(T + 1):
                            if s < T:
                                accumulate(l, n, WP[:, par, :, :], 0, s)
                            if s:
                                accumulate(l, n, WP[:, par, :, :], 1, s - 1)
                last_pair = (l + 1) * PAIRS - 1
                pair_weights(l, (l + 1) * (PAIRS - 1), 1, E1 - 2)
                run_between(l, {"evac0": lambda t: accumulate(l, last_pair, WP[:, 1, :, :], 0, t),
                                "evac1": lambda t: accumulate(l, last_pair, WP[:, 1, :, :], 1, t),
                                "lo": lambda t: layer_input_lo(l, t), "finish": result, **next_parts(l + 1)})

        @block.tensor
        def _(pe):
            pe.sem_inc(dn_mm, 2)
            pe.sem_inc(ex_mm, 2 * T)

            def exact(out_, pairs, first=True, last=True):
                for n, (a, w) in enumerate(pairs):
                    ins = pe.matmul(out_, a, w, start=first and n == 0, stop=last and n == len(pairs) - 1,
                                    skip_group_check=True)
                return ins

            def modulation(n, batches=range(B)):
                mod_w.wait(pe, n)
                pe.wait_ge(cb_ready, n // 2 + 1)
                w = {0: wmraw, 1: WM0[:, :, :], 2: wmraw, 3: WM1[:, :, :]}[n]
                for b in batches:
                    for c, (c0, width) in enumerate(((0, 512), (512, 256))):
                        for k in range(KC):
                            ins = pe.matmul(PS[:, 2 + 2 * b + c, 0:width], CB[:, k, b, :], w[:, k, c0:c0 + width],
                                            start=k == 0, stop=k == KC - 1)
                    ins.then_inc(mod_mm.sem, 1)

            def normalised_transposes(use, t, h):
                h_ready.wait(pe, (use, t))
                before = t - transposes_in_flight(use)
                if before >= 0:
                    (ht_hi if use == ("F", 0) else ht_lo).wait(pe, (use, before))
                for k in range(KC):
                    ins = pe.transpose(tile_transposed(use, t)[:, k * P:(k + 1) * P], h[:, k * P:(k + 1) * P], ident)
                ins.then_inc(tr_done.sem, 1)

            def free(key):
                for reader, label in bank_free[key]:
                    reader.wait(pe, label)

            def max_products(L, b, st):
                _, g, i, j = st
                pair, keys = 2 * g + j // 2, K[j % 2]
                for c, (c0, w) in enumerate(max_chunks(i)):
                    free((L, b) + st + (c,))
                    to = bank[(L, b) + st + (c,)]
                    last = c0 + w == (i + 1) * P
                    ins = pe.matmul(PS[:, to, 0:w], Q[:, pair, i * P:(i + 1) * P], keys[:, pair, c0:c0 + w],
                                    start=True, stop=not last, skip_group_check=True)
                    if last:
                        ins = pe.matmul(PS[:, to, w - P:w], IDB[:, :], MQB[:, :], start=False, stop=True,
                                        skip_group_check=True)
                    ins.then_inc(max_mm.sem, 1)

            def project(L, b):
                use = ("A", L, b)
                w_ready.wait(pe, L)
                if b:
                    x_new.wait(pe, ("A", L, 0, TB - 1))
                for s in range(TB + 4):
                    if s < TB:
                        normalised_transposes(use, s, HR[s % 2])
                    if early_maxes(L, s, 0):
                        for stored_ in (stk_ka, stk_kb):
                            stored_.wait(pe, (L, b, s - 4, 1))
                    for st in early_maxes(L, s, 0):
                        max_products(L, b, st)
                    if 0 <= s - 1 < TB:
                        t = s - 1
                        ht_lo.wait(pe, (use, t))
                        if t >= 2:
                            q_ready.wait(pe, (L, b, t - 2))
                        qk, v = PS[:, 2 + t % 2, :], tile_v(L, t)
                        for dst, c0, c1 in ((qk, 0, 2 * D), (v, 2 * D, 3 * D)):
                            if c0 and t > L:
                                v_ready.wait(pe, (L, b, t - 1 - L))
                            biased = L == 0 or c0 == 0
                            if biased:
                                exact(dst, [(BE[:, :], BZ[:, c0:c1])], last=False)
                            ins = exact(dst, [(a[:, t % 2, k, :], w[:, k, c0:c1]) for k in range(KC)
                                              for a, w in ((HTH, WH), (HTH, WL), (HTL, WH))], first=not biased)
                        ins.then_inc(qkv_done.sem, 1)
                    for st in early_maxes(L, s, 1):
                        max_products(L, b, st)
                    if 0 <= s - 3 < TB:
                        t = s - 3
                        stage_lo.wait(pe, (L, b, t))
                        for n, (what, src) in enumerate((("q", QS), ("k", KS))):
                            for h in range(2):
                                if what == "k":
                                    stk_q.wait(pe, (L, b, t, h))
                                elif t:
                                    stk_ka.wait(pe, (L, b, t - 1, h))
                                    stk_kb.wait(pe, (L, b, t - 1, h))
                                for a in range(4):
                                    pair = 4 * h + a
                                    ins = pe.transpose(PS[:, 6 + h, a * P:(a + 1) * P],
                                                       src[t % 2][:, 2 * pair:2 * pair + 2, :].rearrange("p h c -> p (h c)"),
                                                       ident)
                                ins.then_inc(stk_tr.sem, 1)
                stk_ka.wait(pe, (L, b, TB - 1, 1))
                stk_kb.wait(pe, (L, b, TB - 1, 1))
                stk_q.wait(pe, (L, b, TB - 1, 1))

            def attend(L, b):
                for st in STEPS[L]:
                    key = (L, b) + st
                    if st[0] == "max":
                        max_products(L, b, st)
                    elif st[0] == "ms":
                        ms_ready.wait(pe, key)
                        free(key)
                        pe.transpose(PS[0:64, bank[key], 0:P], MS[:, :, :, :].rearrange("p j h i -> p (j h i)"),
                                     ident).then_inc(ms_tr.sem, 1)
                    elif st[0] == "st":
                        _, g, k, j = st
                        if k == 0 and j == 0 and L == 0:
                            m_rows.wait(pe, (L, b, "ms", g))
                        free(key)
                        pair, keys = 2 * g + j // 2, K[j % 2]
                        for c in range(2):
                            lo, hi = max(k * P, 512 * c), 512 * (c + 1)
                            if lo >= hi:
                                continue
                            to = bank[key] + c
                            ins = pe.matmul(PS[:, to, lo - 512 * c:512], keys[:, pair, k * P:(k + 1) * P], Q[:, pair, lo:hi],
                                            start=True, stop=True)
                        ins.then_inc(st_done.sem, 1)
                    elif st[0] == "pv":
                        _, g, k = st
                        p_mask.wait(pe, (L, b, "st", g, k, 3))
                        if k == 0 and g:
                            o_evac.wait(pe, (L, b, "pv", g - 1, TB - 1))
                        for c in range(2):
                            lo, hi = max(k * P, 512 * c), 512 * (c + 1)
                            if lo >= hi:
                                continue
                            for j in range(4):
                                ins = pe.matmul(PS[32 * j:32 * j + HD + 1, 4 + c, lo - 512 * c:512], V[:, k, 4 * g + j, :],
                                                PR[:, k % 2, j, lo:hi], start=k == 0, stop=k == 4 * c + 3,
                                                skip_group_check=True)
                        ins.then_inc(pv_done.sem, 1)
                    elif st[0] == "otr":
                        _, g, half = st
                        free(key)
                        o_evac.wait(pe, (L, b, "pv", g, TB - 1))
                        for a in range(4):
                            t = 4 * half + a
                            ins = pe.transpose(PS[:, bank[key], a * P:(a + 1) * P], OT[:, t * P:(t + 1) * P], ident)
                        ins.then_inc(o_tr.sem, 1)
                on_ready.wait(pe, (L, b, "otr", NQ - 1, 1))
                for t in range(TB + 1):
                    if t < TB:
                        free((L, b, "ont", t))
                        for k in range(KC):
                            ins = pe.transpose(PS[:, bank[(L, b, "ont", t)], k * P:(k + 1) * P], ON[:, t, k * P:(k + 1) * P], ident)
                        ins.then_inc(on_tr.sem, 1)
                    if t:
                        ont.wait(pe, (L, b, t - 1))
                        if t >= 3:
                            gated.wait(pe, (L, b, t - 3))
                        dst = PS[:, (t - 1) % 2, 0:D]
                        if L == 0:
                            exact(dst, [(BE[:, :], BOZ[:, :])], last=False)
                        exact(dst, [(a[:, (t - 1) % 2, k, :], w[:, k, :]) for k in range(KC)
                                    for a, w in ((HTH, WOH), (HTH, WOL), (HTL, WOH))], first=L == 1).then_inc(pr_done.sem, 1)
                    if b == 1 and t in (3, 5):
                        modulation(2 * L + 1, [(t - 3) // 2])

            pe.wait_ge(cvt, 6)
            pe.wait_ge(psum_zero, 1)
            modulation(0)
            for L, b in UNITS[:2]:
                mod_ready.wait(pe, (0, 1))
                project(L, b)
                attend(L, b)

            pe.wait_ge(wg_load, 16)
            for s in range(T + 1):
                if s < T:
                    normalised_transposes(("F", 0), s, HF[:, s, :])
                if s:
                    t = s - 1
                    ht_hi.wait(pe, (("F", 0), t))
                    for k in range(KC):
                        ins = pe.matmul(PS[:, 6, t * E0:(t + 1) * E0], HG[:, t % 2, k, :], WG[:, k, :],
                                        start=k == 0, stop=k == KC - 1)
                    ins.then_inc(lg_mm, 1)
            pe.wait_ge(route_in, 1)
            chosen = MM[:, :, :].rearrange("p t e -> p (t e)")
            pe.matmul(PS[:, 7, 0:P], CST[:, C_TRI:C_TRI + P], chosen, start=True, stop=True)
            pe.matmul(PS[:, 7, P:2 * P], CST[:, C_ONE:C_ONE + P], chosen, start=True, stop=True).then_inc(route_mm, 1)

            def slot_transposes(par, pair):
                pe.wait_ge(xs_load[par], pair * 16 + 16)
                for k in range(KC):
                    for a in range(2):
                        ins = pe.transpose(PS[:, 6, k * SLOT + a * P:k * SLOT + (a + 1) * P], XT[:, par, a, k * P:(k + 1) * P], ident)
                ins.then_inc(xs_tr, 1)

            def slot_up(s, par, c):
                if c == 0:
                    pe.wait_ge(xs_lo, s + 1)
                if c >= 4:
                    pe.wait_ge(up_gate, s * HC + (c - 3))
                for n in range(2):
                    if c == 0:
                        pe.wait_ge(ws_lo[n], s * 2 + 2)
                    cols = slice(c * P, (c + 1) * P)
                    ins = exact(PS[:, c % 4, n * SLOT:(n + 1) * SLOT],
                                [(w[:, par, n, k, cols], r[:, par, k, :]) for k in range(KC)
                                 for w, r in ((H13, XTH), (H13, XTL), (L13, XTH))])
                ins.then_inc(up_mm, 1)

            def slot_down(s, par):
                pe.wait_ge(y_evac, s + 1)
                pe.wait_ge(ws_lo[2], s * 2 + 2)
                for c in range(HC):
                    pe.wait_ge(up_lo, s * HC + (c + 1))
                    for a in range(2):
                        cols = slice(a * P, (a + 1) * P)
                        ins = exact(PS[:, 4 + a, 0:D], [(HH[:, c, cols], H2[:, par, c, :]), (HH[:, c, cols], L2[:, par, c, :]),
                                                        (HL[:, c, cols], H2[:, par, c, :])], first=c == 0, last=c == HC - 1)
                ins.then_inc(dn_mm, 1)

            mod_ready.wait(pe, (1, 1))
            slot_transposes(0, 0)
            with pe.Fori(0, (SLOTS - 1) // 2, 1) as i:
                for par in range(2):
                    s = i * 2 + par
                    for c in range(HC):
                        slot_up(s, par, c)
                        if c == 3:
                            slot_transposes((par + 1) % 2, i + par)
                    slot_down(s, par)
            for c in range(HC):
                slot_up(SLOTS - 1, 0, c)
            slot_down(SLOTS - 1, 0)

            pe.wait_ge(y_evac, SLOTS + 1)
            modulation(2)
            for L, b in UNITS[2:]:
                mod_ready.wait(pe, (2, 1))
                project(L, b)
                attend(L, b)

            pe.wait_ge(gw_lo, 1)

            def gate_logits(l, c):
                last = 4 * c + 3
                if l:
                    ln_lo.wait(pe, (l - 1, last))
                else:
                    ht_lo.wait(pe, (("F", 1), last))
                if c or l:
                    gt_evac.wait(pe, (l, c - 1) if c else (l - 1, 3))
                cols = slice(c * 512, (c + 1) * 512)
                exact(PS[:, 6, :], [(g[:, l, k, :], r[:, k, cols]) for k in range(KC)
                                    for g, r in ((GWH, XH), (GWH, XL), (GWL, XH))]).then_inc(gt_mm.sem, 1)

            def gate_rows(l, c):
                gt_evac.wait(pe, (l, c))
                if c or l:
                    gt_read.wait(pe, (l, c - 1) if c else (l - 1, 3))
                for a in range(4):
                    t = 4 * c + a
                    ins = pe.transpose(PS[:, 7, a * E1:(a + 1) * E1], LT[:, t * P:(t + 1) * P], CST[0:E1, C_ID:C_ID + E1])
                ins.then_inc(gt_tr.sem, 1)

            def product(n, par, t):
                pe.wait_ge(ev_b, n * T + (t + T - 3))
                cols = slice(t * P, (t + 1) * P)
                exact(PS[:, 2 + t % 4, :], [(r[:, k, cols], w[:, par, k, :, :].rearrange("p e m -> p (e m)"))
                                            for k in range(KC) for r, w in ((XH, EH), (XH, EL), (XL, EH))]
                      ).then_inc(ex_mm, 1)

            def output_transposes(l, t):
                pe.wait_ge(ev_b, ((l + 1) * PAIRS - 1) * T + T + t + 1)
                if t >= 2:
                    ln_lo.wait(pe, (l, t - 2))
                for k in range(KC):
                    ins = pe.transpose(PS[:, t % 2, k * P:(k + 1) * P], AC[:, l % 2, t, k * P:(k + 1) * P], ident)
                ins.then_inc(ln_tr.sem, 1)


            def next_parts(l):
                def first_product(t):
                    if t == 0:
                        pe.wait_ge(er_lo, l * PAIRS + 1)
                        if l == 0:
                            mod_ready.wait(pe, (3, 1))
                    product(l * PAIRS, 0, t)

                return {"gate": lambda c: gate_logits(l, c), "gate_rows": lambda c: gate_rows(l, c),
                        "next_product": first_product}

            run_between(None, {"transpose": lambda t: normalised_transposes(("F", 1), t, HR1[:, t % 2, :]), **next_parts(0)})
            for l in range(L1N):
                with pe.Fori(0, PAIRS // 2 - 1, 1) as i:
                    for par in (1, 0):
                        n = i * 2 + (l * PAIRS + 2 - par)
                        pe.wait_ge(er_lo, n + 1)
                        for t in range(T):
                            product(n, par, t)
                last_pair = (l + 1) * PAIRS - 1
                pe.wait_ge(er_lo, last_pair + 1)
                run_between(l, {"product": lambda t: product(last_pair, 1, t),
                                "transpose": lambda t: output_transposes(l, t), **next_parts(l + 1)})


def constant_table():
    import numpy as np

    c = np.zeros((P, C_W), np.float32)
    r, k = np.arange(P)[:, None], np.arange(P)[None, :]
    c[:, C_ID:C_ID + P] = r == k
    c[:, C_TRI:C_TRI + P] = r < k
    c[:, C_ONE:C_ONE + P] = 1.0
    inv = np.float32(1.0) / np.float32(10000.0) ** (np.arange(HD // 2, dtype=np.float32) / np.float32(HD // 2))
    angle = np.arange(S, dtype=np.float32)[:, None] * inv[None, :].astype(np.float32)
    cos = np.repeat(np.cos(angle), 2, axis=-1).astype(np.float32)
    sin = np.repeat(np.sin(angle), 2, axis=-1).astype(np.float32)
    sin[:, 0::2] *= -1
    c[:, C_COS:C_COS + TB * HD] = cos.reshape(TB, P, HD).transpose(1, 0, 2).reshape(P, -1)
    c[:, C_SIN:C_SIN + TB * HD] = sin.reshape(TB, P, HD).transpose(1, 0, 2).reshape(P, -1)
    c[:, C_THR:C_THR + 8] = SLOT * np.arange(8)
    c[:, C_SLOT:C_SLOT + 24] = np.arange(24)
    c[1, C_SC] = -1.0
    c[0:2, C_BE:C_BE + P] = 1.0
    c[:, C_MQ:C_MQ + P] = np.where(k > r, -1e30, 0.0)
    return c


def kernel(**inputs):
    import numpy as _np
    import concourse.bacc as _bacc
    from concourse import mybir as _mybir
    from concourse.bass_utils import run_bass_kernel_spmd as _run

    g = {k: _np.asarray(v) for k, v in inputs.items()}
    gates = _np.zeros((L1N, D, P), _np.float32)
    gates[:, :, 0:E1] = g["L1_ffn_gate_w"].transpose(0, 2, 1)
    a = {
        "x": g["L0_attn_x"].reshape(T * P, D),
        "cT0": g["L0_c"].T,
        "wmod0": g["L0_wmod"],
        "wqkv0": _np.concatenate([g["L0_attn_Wq"].T, g["L0_attn_Wk"].T, g["L0_attn_Wv"].T], axis=1),
        "bqkv0": _np.tile(_np.concatenate([g["L0_attn_bq"], g["L0_attn_bk"], g["L0_attn_bv"]])[None], (2, 1)),
        "wo0": g["L0_attn_Wo"].T,
        "bo0": _np.tile(g["L0_attn_bo"][None], (2, 1)),
        "wg": g["L0_ffn_Wg"],
        "w1": g["L0_ffn_w1"],
        "w3": g["L0_ffn_w3"],
        "w2": g["L0_ffn_w2"],
        "cT1": g["L1_c"].T,
        "wmod1": g["L1_wmod"],
        "wqkv1": _np.concatenate([g["L1_attn_Wq"].T, g["L1_attn_Wk"].T, g["L1_attn_Wv"].T], axis=1),
        "wo1": g["L1_attn_Wo"].T,
        "gamma": _np.tile(g["L1_attn_gamma"][None], (P, 1)),
        "beta": _np.tile(g["L1_attn_beta"][None], (P, 1)),
        "gw1": gates,
        "ew1": g["L1_ffn_expert_w"].transpose(0, 1, 3, 2).reshape(L1N * E1 * D, D),
        "consts": constant_table(),
    }
    nc = _bacc.Bacc("TRN2", target_bir_lowering=False, num_devices=1)
    arrays = {f"in_{k}": _np.ascontiguousarray(v) for k, v in a.items()}
    args = [nc.dram_tensor(k, v.shape, _mybir.dt.from_np(v.dtype), kind="ExternalInput").ap() for k, v in arrays.items()]
    out = nc.dram_tensor("out_x", (T * P, D), F32, kind="ExternalOutput").ap()
    adaln_kernel(nc, *args, out)
    r = _run(nc, [arrays], core_ids=[0])
    return r.results[0]["out_x"].reshape(B, S, D)
```
